# Optimizing a Trainium2 kernel written in Bass

```python
import numpy as np
import jax
import jax.numpy as jnp

def _softmax(x, axis=-1):
    return jax.nn.softmax(x, axis=axis)

def _gelu(x):
    return jax.nn.gelu(x, approximate=True)

def _silu(x):
    return jax.nn.silu(x)

def _sigmoid(x):
    return jax.nn.sigmoid(x)

def _layernorm(x, axis=-1, eps=1e-05):
    m = jnp.mean(x, axis=axis, keepdims=True)
    v = jnp.var(x, axis=axis, keepdims=True)
    return (x - m) / jnp.sqrt(v + eps)

def _scatter_add(tgt, idx, src, axis=0):
    return tgt.at[idx].add(src)

def _segment_sum(src, seg, n):
    return jax.ops.segment_sum(src, seg, n)
kernel_name = 'mk_seq_postln_d2_jaxref_r8_9ad444'

def setup_inputs(seed: int=0):
    np.random.seed(seed)
    _w = jnp.asarray

    def _L0_attn_setup():
        import jax, jax.numpy as jnp
        import numpy as np
        D_MODEL = 512
        D_XB = 128
        D_INNER = 512
        HEADDIM = 128
        DSTATE = 128
        NHEADS = D_INNER // HEADDIM
        DCONV = 4
        INTER = 1792
        EPS = 1e-05
        CHUNK = 128

        def rmsnorm(x, w):
            return x * jax.lax.rsqrt(jnp.mean(x * x, axis=-1, keepdims=True) + EPS) * w

        def silu(x):
            return x * jax.nn.sigmoid(x)

        def mamba2(x, w_in, conv_w, conv_b, A_log, D, dt_bias, w_out):
            B, L, _ = x.shape
            H, P, N = (NHEADS, HEADDIM, DSTATE)
            G = D_XB // P
            rep = H // G
            zxbcdt = x @ w_in.T
            z, xs, Bs, Cs, dt = jnp.split(zxbcdt, [D_INNER, D_INNER + D_XB, D_INNER + 2 * D_XB, 2 * D_INNER + 2 * D_XB], axis=-1)
            xBC = jnp.concatenate([xs, Bs, Cs], axis=-1)
            conv = jax.lax.conv_general_dilated(xBC.transpose(0, 2, 1), conv_w[:, None, :], (1,), [(DCONV - 1, 0)], feature_group_count=conv_w.shape[0])
            xBC = silu(conv.transpose(0, 2, 1) + conv_b)
            xs, Bs, Cs = jnp.split(xBC, [D_XB, 2 * D_XB], axis=-1)
            dt = jax.nn.softplus(dt + dt_bias)
            A = -jnp.exp(A_log)
            xh = jnp.repeat(xs.reshape(B, L, G, P), rep, axis=2)
            Bh = jnp.repeat(Bs.reshape(B, L, G, N), rep, axis=2)
            Ch = Cs.reshape(B, L, H, N)
            c, Q = (L // CHUNK, CHUNK)
            a = (dt * A).reshape(B, c, Q, H).transpose(0, 1, 3, 2)
            dtc = dt.reshape(B, c, Q, H).transpose(0, 1, 3, 2)
            Xc = xh.reshape(B, c, Q, H, P).transpose(0, 1, 3, 2, 4)
            Bc = Bh.reshape(B, c, Q, H, N).transpose(0, 1, 3, 2, 4)
            Cc = Ch.reshape(B, c, Q, H, N).transpose(0, 1, 3, 2, 4)
            cs = jnp.cumsum(a, axis=-1)
            tri = jnp.tril(jnp.ones((Q, Q), bool))
            Ldec = jnp.where(tri, jnp.exp(cs[..., :, None] - cs[..., None, :]), 0.0)
            Xdt = Xc * dtc[..., None]
            att = jnp.einsum('bchqn,bchkn->bchqk', Cc, Bc) * Ldec
            Yd = jnp.einsum('bchqk,bchkp->bchqp', att, Xdt)
            dec_end = jnp.exp(cs[..., -1:] - cs)
            states = jnp.einsum('bchq,bchqn,bchqp->bchpn', dec_end, Bc, Xdt)
            g = jnp.exp(cs[..., -1])

            def step(S, inp):
                gk, st = inp
                return (gk[:, :, None, None] * S + st, S)
            S0 = jnp.zeros((B, H, P, N), x.dtype)
            _, prev = jax.lax.scan(step, S0, (g.transpose(1, 0, 2), states.transpose(1, 0, 2, 3, 4)))
            prev = prev.transpose(1, 0, 2, 3, 4)
            Yo = jnp.einsum('bchqn,bchpn,bchq->bchqp', Cc, prev, jnp.exp(cs))
            Y = (Yd + Yo).transpose(0, 1, 3, 2, 4).reshape(B, L, H, P)
            Y = Y + D[:, None] * xh
            y = Y.reshape(B, L, D_INNER) * silu(z)
            return y @ w_out.T
        key = jax.random.key(seed)
        ks = jax.random.split(key, 10)
        B, L = (2, 256)
        proj_out = 2 * D_INNER + 2 * D_XB + NHEADS
        conv_dim = 2 * D_XB + D_INNER
        return {'hidden_states': jax.random.normal(ks[0], (B, L, D_MODEL), jnp.float32), 'w_in': jax.random.normal(ks[1], (proj_out, D_MODEL), jnp.float32) * 0.02, 'conv_w': jax.random.normal(ks[2], (conv_dim, DCONV), jnp.float32) * 0.1, 'conv_b': jnp.zeros((conv_dim,), jnp.float32), 'A_log': jnp.log(jnp.arange(1, NHEADS + 1, dtype=jnp.float32)), 'D': jnp.ones((NHEADS,), jnp.float32), 'dt_bias': jax.random.normal(ks[3], (NHEADS,), jnp.float32) * 0.1, 'w_out': jax.random.normal(ks[4], (D_MODEL, D_INNER), jnp.float32) * 0.02, 'ln1_w': jnp.ones((D_MODEL,), jnp.float32), 'ln2_w': jnp.ones((D_MODEL,), jnp.float32), 'gate_w': jax.random.normal(ks[5], (INTER, D_MODEL), jnp.float32) * 0.02, 'up_w': jax.random.normal(ks[6], (INTER, D_MODEL), jnp.float32) * 0.02, 'down_w': jax.random.normal(ks[7], (D_MODEL, INTER), jnp.float32) * 0.02}
    _L0_attn_in = _L0_attn_setup()

    def _L0_ffn_setup():
        import jax, jax.numpy as jnp
        import numpy as np
        D_MODEL = 512
        D_FF = 1376
        key = jax.random.key(seed)
        k1, k2, k3, k4 = jax.random.split(key, 4)
        x = jax.random.normal(k1, (2, 256, D_MODEL), dtype=jnp.float32)
        W_gate = jax.random.normal(k2, (D_FF, D_MODEL), dtype=jnp.float32) * D_MODEL ** (-0.5)
        W_up = jax.random.normal(k3, (D_FF, D_MODEL), dtype=jnp.float32) * D_MODEL ** (-0.5)
        W_down = jax.random.normal(k4, (D_MODEL, D_FF), dtype=jnp.float32) * D_FF ** (-0.5)
        return {'x': x, 'W_gate': W_gate, 'W_up': W_up, 'W_down': W_down}
    _L0_ffn_in = _L0_ffn_setup()

    def _L1_attn_setup():
        import jax, jax.numpy as jnp
        import numpy as np
        SEQ, BATCH, HIDDEN = (256, 1, 512)
        NUM_HEADS, NUM_KV_HEADS, HEAD_DIM = (32, 8, 128)
        Q_PER_GROUP = NUM_HEADS // NUM_KV_HEADS
        TOTAL_PROJ = NUM_KV_HEADS * (Q_PER_GROUP + 2) * HEAD_DIM
        key = jax.random.key(seed)
        k1, k2, k3 = jax.random.split(key, 3)
        tokens = jax.random.normal(k1, (SEQ, BATCH, HIDDEN), dtype=jnp.float32)
        weight_qkv = jax.random.normal(k2, (TOTAL_PROJ, HIDDEN), dtype=jnp.float32) * (2.0 / (TOTAL_PROJ + HIDDEN)) ** 0.5
        weight_proj = jax.random.normal(k3, (HIDDEN, NUM_HEADS * HEAD_DIM), dtype=jnp.float32) * (2.0 / (HIDDEN + NUM_HEADS * HEAD_DIM)) ** 0.5
        return {'tokens': tokens, 'weight_qkv': weight_qkv, 'weight_proj': weight_proj}
    _L1_attn_in = _L1_attn_setup()

    def _L1_ffn_setup():
        import jax, jax.numpy as jnp
        import numpy as np
        HID, INT, LAT, NE, K = (512, 1024, 256, 8, 2)
        LN_EPS = 1e-05

        def _layernorm(x, gamma, beta):
            mu = jnp.mean(x, axis=-1, keepdims=True)
            var = jnp.var(x, axis=-1, keepdims=True)
            return (x - mu) * jax.lax.rsqrt(var + LN_EPS) * gamma + beta
        key = jax.random.key(seed)
        ks = jax.random.split(key, 8)
        s = lambda d: 1.0 / np.sqrt(d)
        return {'hidden_states': jax.random.normal(ks[0], (4, 256, HID), jnp.float32), 'gate_w': jax.random.normal(ks[1], (HID, NE), jnp.float32) * s(HID), 'up_w': jax.random.normal(ks[2], (HID, INT), jnp.float32) * s(HID), 'down_w': jax.random.normal(ks[3], (INT, HID), jnp.float32) * s(INT), 'fc1_w': jax.random.normal(ks[4], (HID, LAT), jnp.float32) * s(HID), 'fc2_w': jax.random.normal(ks[5], (LAT, HID), jnp.float32) * s(LAT), 'expert_w': jax.random.normal(ks[6], (LAT, LAT), jnp.float32), 'ln_gamma': jnp.ones((HID,), jnp.float32), 'ln_beta': jnp.zeros((HID,), jnp.float32)}
    _L1_ffn_in = _L1_ffn_setup()
    _d = {'L0_attn_hidden_states': _L0_attn_in['hidden_states'], 'L0_attn_w_in': _L0_attn_in['w_in'], 'L0_attn_conv_w': _L0_attn_in['conv_w'], 'L0_attn_conv_b': _L0_attn_in['conv_b'], 'L0_attn_A_log': _L0_attn_in['A_log'], 'L0_attn_D': _L0_attn_in['D'], 'L0_attn_dt_bias': _L0_attn_in['dt_bias'], 'L0_attn_w_out': _L0_attn_in['w_out'], 'L0_attn_ln1_w': _L0_attn_in['ln1_w'], 'L0_attn_ln2_w': _L0_attn_in['ln2_w'], 'L0_attn_gate_w': _L0_attn_in['gate_w'], 'L0_attn_up_w': _L0_attn_in['up_w'], 'L0_attn_down_w': _L0_attn_in['down_w'], 'L0_ffn_W_gate': _L0_ffn_in['W_gate'], 'L0_ffn_W_up': _L0_ffn_in['W_up'], 'L0_ffn_W_down': _L0_ffn_in['W_down'], 'L1_attn_weight_qkv': _L1_attn_in['weight_qkv'], 'L1_attn_weight_proj': _L1_attn_in['weight_proj'], 'L1_ffn_gate_w': _L1_ffn_in['gate_w'], 'L1_ffn_up_w': _L1_ffn_in['up_w'], 'L1_ffn_down_w': _L1_ffn_in['down_w'], 'L1_ffn_fc1_w': _L1_ffn_in['fc1_w'], 'L1_ffn_fc2_w': _L1_ffn_in['fc2_w'], 'L1_ffn_expert_w': _L1_ffn_in['expert_w'], 'L1_ffn_ln_gamma': _L1_ffn_in['ln_gamma'], 'L1_ffn_ln_beta': _L1_ffn_in['ln_beta']}
    _x0 = _d['L0_attn_hidden_states']
    _d['L0_attn_hidden_states'] = jax.random.normal(jax.random.fold_in(jax.random.key(seed), 1), (1, 1024, 512), dtype=_x0.dtype)
    del _x0
    return _d

def reference(L0_attn_hidden_states, L0_attn_w_in, L0_attn_conv_w, L0_attn_conv_b, L0_attn_A_log, L0_attn_D, L0_attn_dt_bias, L0_attn_w_out, L0_attn_ln1_w, L0_attn_ln2_w, L0_attn_gate_w, L0_attn_up_w, L0_attn_down_w, L0_ffn_W_gate, L0_ffn_W_up, L0_ffn_W_down, L1_attn_weight_qkv, L1_attn_weight_proj, L1_ffn_gate_w, L1_ffn_up_w, L1_ffn_down_w, L1_ffn_fc1_w, L1_ffn_fc2_w, L1_ffn_expert_w, L1_ffn_ln_gamma, L1_ffn_ln_beta):

    def _L0_attn_ref(hidden_states, w_in, conv_w, conv_b, A_log, D, dt_bias, w_out, ln1_w, ln2_w, gate_w, up_w, down_w):
        import jax, jax.numpy as jnp
        import numpy as np
        D_MODEL = 512
        D_XB = 128
        D_INNER = 512
        HEADDIM = 128
        DSTATE = 128
        NHEADS = D_INNER // HEADDIM
        DCONV = 4
        INTER = 1792
        EPS = 1e-05
        CHUNK = 128

        def rmsnorm(x, w):
            return x * jax.lax.rsqrt(jnp.mean(x * x, axis=-1, keepdims=True) + EPS) * w

        def silu(x):
            return x * jax.nn.sigmoid(x)

        def mamba2(x, w_in, conv_w, conv_b, A_log, D, dt_bias, w_out):
            B, L, _ = x.shape
            H, P, N = (NHEADS, HEADDIM, DSTATE)
            G = D_XB // P
            rep = H // G
            zxbcdt = x @ w_in.T
            z, xs, Bs, Cs, dt = jnp.split(zxbcdt, [D_INNER, D_INNER + D_XB, D_INNER + 2 * D_XB, 2 * D_INNER + 2 * D_XB], axis=-1)
            xBC = jnp.concatenate([xs, Bs, Cs], axis=-1)
            conv = jax.lax.conv_general_dilated(xBC.transpose(0, 2, 1), conv_w[:, None, :], (1,), [(DCONV - 1, 0)], feature_group_count=conv_w.shape[0])
            xBC = silu(conv.transpose(0, 2, 1) + conv_b)
            xs, Bs, Cs = jnp.split(xBC, [D_XB, 2 * D_XB], axis=-1)
            dt = jax.nn.softplus(dt + dt_bias)
            A = -jnp.exp(A_log)
            xh = jnp.repeat(xs.reshape(B, L, G, P), rep, axis=2)
            Bh = jnp.repeat(Bs.reshape(B, L, G, N), rep, axis=2)
            Ch = Cs.reshape(B, L, H, N)
            c, Q = (L // CHUNK, CHUNK)
            a = (dt * A).reshape(B, c, Q, H).transpose(0, 1, 3, 2)
            dtc = dt.reshape(B, c, Q, H).transpose(0, 1, 3, 2)
            Xc = xh.reshape(B, c, Q, H, P).transpose(0, 1, 3, 2, 4)
            Bc = Bh.reshape(B, c, Q, H, N).transpose(0, 1, 3, 2, 4)
            Cc = Ch.reshape(B, c, Q, H, N).transpose(0, 1, 3, 2, 4)
            cs = jnp.cumsum(a, axis=-1)
            tri = jnp.tril(jnp.ones((Q, Q), bool))
            Ldec = jnp.where(tri, jnp.exp(cs[..., :, None] - cs[..., None, :]), 0.0)
            Xdt = Xc * dtc[..., None]
            att = jnp.einsum('bchqn,bchkn->bchqk', Cc, Bc) * Ldec
            Yd = jnp.einsum('bchqk,bchkp->bchqp', att, Xdt)
            dec_end = jnp.exp(cs[..., -1:] - cs)
            states = jnp.einsum('bchq,bchqn,bchqp->bchpn', dec_end, Bc, Xdt)
            g = jnp.exp(cs[..., -1])

            def step(S, inp):
                gk, st = inp
                return (gk[:, :, None, None] * S + st, S)
            S0 = jnp.zeros((B, H, P, N), x.dtype)
            _, prev = jax.lax.scan(step, S0, (g.transpose(1, 0, 2), states.transpose(1, 0, 2, 3, 4)))
            prev = prev.transpose(1, 0, 2, 3, 4)
            Yo = jnp.einsum('bchqn,bchpn,bchq->bchqp', Cc, prev, jnp.exp(cs))
            Y = (Yd + Yo).transpose(0, 1, 3, 2, 4).reshape(B, L, H, P)
            Y = Y + D[:, None] * xh
            y = Y.reshape(B, L, D_INNER) * silu(z)
            return y @ w_out.T
        res = hidden_states
        h = rmsnorm(hidden_states, ln1_w)
        h = res + mamba2(h, w_in, conv_w, conv_b, A_log, D, dt_bias, w_out)
        res = h
        h2 = rmsnorm(h, ln2_w)
        mlp = silu(h2 @ gate_w.T) * (h2 @ up_w.T) @ down_w.T
        return res + mlp

    def _L0_ffn_ref(x, W_gate, W_up, W_down):
        import jax, jax.numpy as jnp
        import numpy as np
        D_MODEL = 512
        D_FF = 1376
        out_shape = x.shape[:-1] + (W_down.shape[0],)
        xf = x.reshape(-1, x.shape[-1])
        up = jnp.einsum('td,fd->tf', xf, W_up)
        gate = jax.nn.silu(jnp.einsum('td,fd->tf', xf, W_gate))
        h = gate * up
        y = jnp.einsum('tf,df->td', h, W_down)
        return y.reshape(out_shape)

    def _L1_attn_ref(tokens, weight_qkv, weight_proj):
        import jax, jax.numpy as jnp
        import numpy as np
        SEQ, BATCH, HIDDEN = (256, 1, 512)
        NUM_HEADS, NUM_KV_HEADS, HEAD_DIM = (32, 8, 128)
        Q_PER_GROUP = NUM_HEADS // NUM_KV_HEADS
        TOTAL_PROJ = NUM_KV_HEADS * (Q_PER_GROUP + 2) * HEAD_DIM
        S, B, H = tokens.shape
        scale = 1.0 / HEAD_DIM ** 0.5
        qkv = jnp.einsum('sbh,ph->sbp', tokens, weight_qkv)
        qkv = qkv.reshape(S, B, NUM_KV_HEADS, Q_PER_GROUP + 2, HEAD_DIM)
        q = qkv[:, :, :, :Q_PER_GROUP, :].reshape(S, B, NUM_HEADS, HEAD_DIM)
        k = qkv[:, :, :, Q_PER_GROUP, :]
        v = qkv[:, :, :, Q_PER_GROUP + 1, :]
        k = jnp.repeat(k, Q_PER_GROUP, axis=2)
        v = jnp.repeat(v, Q_PER_GROUP, axis=2)
        q = q.transpose(1, 2, 0, 3)
        k = k.transpose(1, 2, 0, 3)
        v = v.transpose(1, 2, 0, 3)
        scores = jnp.einsum('bhsd,bhtd->bhst', q, k) * scale
        causal = jnp.tril(jnp.ones((S, S), dtype=bool))
        scores = jnp.where(causal, scores, jnp.finfo(scores.dtype).min)
        attn = jax.nn.softmax(scores, axis=-1)
        out = jnp.einsum('bhst,bhtd->bhsd', attn, v)
        out = out.transpose(2, 0, 1, 3).reshape(S, B, NUM_HEADS * HEAD_DIM)
        return jnp.einsum('sbe,he->sbh', out, weight_proj)

    def _L1_ffn_ref(hidden_states, gate_w, up_w, down_w, fc1_w, fc2_w, expert_w, ln_gamma, ln_beta):
        import jax, jax.numpy as jnp
        import numpy as np
        HID, INT, LAT, NE, K = (512, 1024, 256, 8, 2)
        LN_EPS = 1e-05

        def _layernorm(x, gamma, beta):
            mu = jnp.mean(x, axis=-1, keepdims=True)
            var = jnp.var(x, axis=-1, keepdims=True)
            return (x - mu) * jax.lax.rsqrt(var + LN_EPS) * gamma + beta
        logits = jnp.einsum('bsh,he->bse', hidden_states, gate_w)
        routing_weights, selected_experts = jax.lax.top_k(logits, K)
        h = jax.nn.relu(jnp.einsum('bsh,hi->bsi', hidden_states, up_w)) ** 2
        shared_out = jnp.einsum('bsi,ih->bsh', h, down_w)
        x_latent = jnp.einsum('bsh,hl->bsl', hidden_states, fc1_w)
        expert_out = jnp.einsum('bsl,lm->bsm', x_latent, expert_w)
        moe_out = expert_out * jnp.sum(routing_weights, axis=-1, keepdims=True)
        routed_out = jnp.einsum('bsl,lh->bsh', moe_out, fc2_w)
        return _layernorm(shared_out + routed_out, ln_gamma, ln_beta)
    x = L0_attn_hidden_states
    x = _layernorm(x + _L0_attn_ref(x, L0_attn_w_in, L0_attn_conv_w, L0_attn_conv_b, L0_attn_A_log, L0_attn_D, L0_attn_dt_bias, L0_attn_w_out, L0_attn_ln1_w, L0_attn_ln2_w, L0_attn_gate_w, L0_attn_up_w, L0_attn_down_w), axis=-1)
    x = _layernorm(x + _L0_ffn_ref(x, L0_ffn_W_gate, L0_ffn_W_up, L0_ffn_W_down), axis=-1)
    x = _layernorm(x + _L1_attn_ref(x, L1_attn_weight_qkv, L1_attn_weight_proj), axis=-1)
    x = _layernorm(x + _L1_ffn_ref(x, L1_ffn_gate_w, L1_ffn_up_w, L1_ffn_down_w, L1_ffn_fc1_w, L1_ffn_fc2_w, L1_ffn_expert_w, L1_ffn_ln_gamma, L1_ffn_ln_beta), axis=-1)
    return x

_drawn_inputs = setup_inputs


def setup_inputs(seed=0):
    import zlib

    import numpy as np

    out = dict(_drawn_inputs(seed))
    spreads = {'L0_attn_conv_b': (0.0, 0.8),
     'L0_attn_D': (1.0, 0.6),
     'L0_attn_ln1_w': (1.0, 0.6),
     'L0_attn_ln2_w': (1.0, 0.6),
     'L1_ffn_ln_gamma': (1.0, 0.2),
     'L1_ffn_ln_beta': (0.0, 0.1)}
    factors = {'L0_attn_w_in': 7.293,
     'L0_attn_conv_w': 8.0,
     'L0_attn_A_log': 8.0,
     'L0_attn_dt_bias': 8.0,
     'L0_attn_w_out': 5.162,
     'L0_attn_gate_w': 64.0,
     'L0_attn_up_w': 64.0,
     'L0_attn_down_w': 64.0}
    for name, (base, spread) in spreads.items():
        noise = np.random.default_rng([zlib.crc32(name.encode()), seed]).standard_normal(out[name].shape)
        drawn = base * np.exp(spread * noise) if base else spread * noise
        out[name] = jnp.asarray(drawn.astype(out[name].dtype))
    for name, factor in factors.items():
        out[name] = (out[name] * factor).astype(out[name].dtype)
    return out
```

```python
import concourse.bass as bass
from concourse import mybir

P = 128
T = 1024
D = 512
NT = T // P
KD = D // P
HALF = 512
NH = 4
NCONV = 6
TAPS = 4
NKV = 8
EPS = 1e-5

F32 = mybir.dt.float32
F32R = mybir.dt.float32r
I32 = mybir.dt.int32
ALU = mybir.AluOpType
ACT = mybir.ActivationFunctionType

RSQRT_GUESS = float(0x5F3759DF - (1 << 22) - (1 << 31))
NEWTON = 3


class Block:

    def __init__(self, layer, first, tiles, final, attention=False):
        self.layer, self.first, self.tiles, self.final = layer, first, tiles, final
        self.attention = attention
        self.pairs = [min(2, tiles - 2 * p) for p in range((tiles + 1) // 2)]
        self.mats = 1 if layer == "E" else 2


def plan():
    blocks = [Block("M", 0, 6, False), Block("M", 6, 4, False), Block("M", 10, 4, True),
              Block("F", 0, 6, False), Block("F", 6, 5, True),
              Block("A", 0, 0, True, attention=True),
              Block("E", 0, 4, False), Block("E", 4, 4, True)]
    groups, downs, norms = 0, 0, 2 * NT
    uses = [3, 2, 2]
    for b in blocks:
        b.group0, b.down0, b.use0, b.norm0 = groups, downs, list(uses), norms
        groups += 2 * b.tiles
        downs += NT
        if not b.attention:
            uses[0] += len(b.pairs)
            uses[1] += sum(n == 2 for n in b.pairs)
            uses[2] += len(b.pairs)
        if b.final:
            norms += NT
    for i, b in enumerate(blocks):
        b.group1 = b.group0 + 2 * b.tiles
        b.next_up = next((n for n in blocks[i + 1:] if not n.attention), None)
        b.fresh = i == 0 or blocks[i - 1].final
    return blocks


def build_program(nc, t):
    blocks = plan()
    here = [16512]

    def place(name, shape, dtype=F32, at=None):
        size = 4
        for n in shape:
            size *= n
        if at is None:
            at = here[0]
            here[0] = at + (size + 31) // 32 * 32
        return nc.alloc_sbuf_tensor_at(name, [P, *shape], dtype, offset=at), at + (size + 31) // 32 * 32

    xres, _ = place("xres", [NT, D])
    xT_hi, _ = place("xT_hi", [KD, T], F32R)
    xT_lo, _ = place("xT_lo", [KD, T], F32R)
    mix, _ = place("mix", [KD, D])
    lat, _ = place("lat", [KD, D])
    shared, _ = place("shared", [NT, D], at=here[0] - 2 * KD * D * 4)
    up_hi = [place(f"up_hi{s}", [2, KD, P], F32R)[0] for s in range(2)]
    up_lo = [place(f"up_lo{s}", [2, KD, P], F32R)[0] for s in range(2)]
    raw = [place(f"raw{s}", [2 * KD * P])[0] for s in range(3)]
    xn = [place(f"xn{u}", [D])[0] for u in range(2)]
    rb = [place(f"rb{u}", [D])[0] for u in range(2)]
    ln1, _ = place("ln1", [D])
    ln2, _ = place("ln2", [D])
    gamma, _ = place("gamma", [D])
    beta, _ = place("beta", [D])
    ident, _ = place("ident", [P])
    tri, _ = place("tri", [P])
    after, _ = place("after", [P])
    ones, _ = place("ones", [P])
    conv_w, _ = place("conv_w", [NCONV, TAPS])
    conv_b, _ = place("conv_b", [NCONV])
    heads_in, _ = place("heads_in", [3, NH])
    dtw, _ = place("dtw", [KD, NH])
    dtw_hi, _ = place("dtw_hi", [KD, NH], F32R)
    dtw_lo, _ = place("dtw_lo", [KD, NH], F32R)
    gw, _ = place("gw", [KD, 8])
    gw_hi, _ = place("gw_hi", [KD, 8], F32R)
    gw_lo, _ = place("gw_lo", [KD, 8], F32R)
    neg_A, _ = place("neg_A", [NH])
    dts = [place(f"dts{i}", [NT, NH])[0] for i in range(6)]
    dt_sp, _ = place("dt_sp", [NT, NH])
    decay, _ = place("decay", [NT, NH])
    to_end, _ = place("to_end", [NT, NH])
    stat = [place(f"stat{i}", [6])[0] for i in range(1)][0]
    mv, _ = place("mv", [2])
    ve, _ = place("ve", [1])
    ry, _ = place("ry", [1])
    rt, _ = place("rt", [1])
    top8, _ = place("top8", [8])
    spare, _ = place("spare", [1])
    route = [place(f"route{u}", [1])[0] for u in range(2)]
    region = here[0]

    xBC, e = place("xBC", [NCONV, T + TAPS - 1], at=region)
    z, e_z = place("z", [NH, T], at=e)
    lat_exp, e2 = place("lat_exp", [2, 2 * P], at=e)
    lat_fc2, e2 = place("lat_fc2", [2, D], at=e2)
    lat_fc1, e2 = place("lat_fc1", [2, D], at=e2)
    lat_e2, e2 = place("lat_e2", [2, D], at=e2)
    assert e2 <= e_z
    acc = [None, None]
    acc[0], e = place("acc0", [T], at=e_z)
    acc[1], e = place("acc1", [T], at=e)
    wv, e = place("wv", [NKV, D], at=e)
    wps, e = place("wps", [NKV, D], at=e)
    wpraw = [None, None]
    wpraw[0], e = place("wpraw0", [2, D], at=e)
    wpraw[1], e_mix = place("wpraw1", [2, D], at=e)
    atri, e = place("atri", [NH, P], at=e_z)
    dtri, e = place("dtri", [NH, P], at=e)
    Xs, e = place("Xs", [NH, P], at=e)
    stXB, e = place("stXB", [2, P], at=e)
    XBt, e = place("XBt", [2, P], at=e)
    wo_hi, e = place("wo_hi", [KD, D], F32R, at=e)
    wo_lo, e = place("wo_lo", [KD, D], F32R, at=e)
    ssd = {}
    for name in ("eD", "eE", "att", "Cs", "xsD", "state", "y"):
        ssd[name], e = place(name, [NH, P], at=e)
    y_hi, e = place("y_hi", [NH, P], F32R, at=e)
    y_lo, e = place("y_lo", [NH, P], F32R, at=e)
    end = max(e, e_mix)
    eD, eE, att, Cs, xsD, state, y = (ssd[n] for n in ("eD", "eE", "att", "Cs", "xsD", "state", "y"))

    MAXT = max(b.tiles for b in blocks)
    hT, e = place("hT", [MAXT, T], at=region)
    wd_hi, e = place("wd_hi", [MAXT, D], F32R, at=e)
    wd_lo, e = place("wd_lo", [MAXT, D], F32R, at=e)
    st_hi, st_lo = [None, None], [None, None]
    for u in range(2):
        st_hi[u], e = place(f"st_hi{u}", [2 * KD, P], F32R, at=e)
        st_lo[u], e = place(f"st_lo{u}", [2 * KD, P], F32R, at=e)
    mix_hi, e = place("mix_hi", [KD, D], F32R, at=e)
    mix_lo, e = place("mix_lo", [KD, D], F32R, at=e)
    sg = [None, None]
    sg[0], e = place("sg0", [HALF], at=e)
    sg[1], e = place("sg1", [HALF], at=e)
    end = max(end, e)
    assert end <= nc.sbuf_usable_end, end

    bank = [nc.alloc_psum_tensor(f"bank{i}", [P, 512], F32) for i in range(8)]

    names = """small_in x_in0 x_in1 x_in2 x_in3 lat_in wv_in gains_in
        raw_in0 raw_in1 raw_in2 w_hi0 w_hi1 w_hi2 w_lo0 w_lo1 w_lo2 wp_in0 wp_in1 wp_summed
        consts pads small_split dve_step pool_step act_step
        xn_done tr_mm xT_hi_done xT_lo_done xres_done
        e2_mm e2_done lat_mm lat_done p1_mm p1_done conv_done conv_silu dt_mm dt_v dt_exp
        a_done end_mm end_exp to_end_done mix_mm mix_done
        st_xb atri_done dtri_done xbt_mm xbt_done g_mm d_mm e_mm expd_done expe_done
        edm_done cs_done xsd_done xs_done att_done y_mm s_mm y1_done y_done yhi_done ylo_done
        state_done o_mm ht_done
        gate_mm up_mm act_done h_done st_hi_done st_lo_done down_mm r_done
        mixhl_hi mixhl_lo route_mm route_done routed_done both_done out_done out_sent0 out_sent1""".split()
    S = {n: nc.alloc_semaphore(n) for n in names}

    def wait(e, name, value):
        if isinstance(value, int) and value <= 0:
            return
        e.wait_ge(S[name], value)

    def tok(i):
        return bass.ds(i * P, P)

    def heads(ap):
        return ap.unsqueeze(1).to_broadcast([P, NH, P])

    def per_head(ap):
        return ap.unsqueeze(2).to_broadcast([P, NH, P])

    block = nc.Block()
    with block:

        @block.sync
        def _(sp):
            def raw_load(slot, use, dst, src):
                wait(sp, f"w_lo{slot}", use)
                sp.dma_start(dst, src).then_inc(S[f"raw_in{slot}"], 16)

            def load_win(piece):
                raw_load(piece % 2, piece // 2, raw[piece % 2][:, :], t["w_in"][piece])

            def load_x(i):
                sp.dma_start(xres[:, 2 * i:2 * i + 2, :],
                             t["x"][2 * i * P:2 * (i + 1) * P, :].rearrange("(t p) d -> p t d", p=P)
                             ).then_inc(S[f"x_in{i}"], 16)

            def load_gain(i, gain):
                sp.dma_start(gain[:, :], t["gains"][i:i + 1, :].to_broadcast([P, D])).then_inc(S["gains_in"], 16)

            load_x(0)
            load_gain(0, ln1)
            load_x(1)
            load_win(0)
            load_x(2)
            load_x(3)
            sp.dma_start(heads_in[:, :, :], t["heads"].unsqueeze(0).to_broadcast([P, 3, NH])
                         ).then_inc(S["small_in"], 16)
            for dst, name in ((conv_w, "conv_w"), (conv_b, "conv_b"), (dtw, "dtw"), (gw, "gw")):
                sp.dma_start(dst[:], t[name]).then_inc(S["small_in"], 16)
            load_win(1)
            sp.dma_start(lat_exp[:, :, :], t["expert"]).then_inc(S["lat_in"], 16)
            sp.dma_start(lat_fc2[:, :, :], t["fc2"]).then_inc(S["lat_in"], 16)
            sp.dma_start(lat_fc1[:, :, :], t["fc1"]).then_inc(S["lat_in"], 16)
            load_win(2)
            load_win(3)
            for i, gain in enumerate((ln2, gamma, beta)):
                wait(sp, "xn_done", 1)
                load_gain(i + 1, gain)
            sp.dma_start(wv[:, :, :], t["wv"]).then_inc(S["wv_in"], 16)

            def load_wp(i):
                wait(sp, "wp_summed", i - 1)
                sp.dma_start(wpraw[i % 2][:, :, :], t["wp"][i]).then_inc(S[f"wp_in{i % 2}"], 16)

            for i in range(2 * NKV):
                load_wp(i)
                if i == 12:
                    load_win(4)
            def load_up(b, p, s):
                w = b.mats * KD * P
                use = b.use0[s] + p
                raw_load(s, use, raw[s][:, 0:w],
                         t["up_" + b.layer][bass.ds(b.first + 2 * p + s, 1)].rearrange("o p n -> p (o n)"))

            def load_down(b, p, n):
                raw_load(2, b.use0[2] + p, raw[2][:, 0:n * D].rearrange("p (k n) -> p k n", k=n),
                         t["down_" + b.layer][bass.ds(b.first + 2 * p, n)].rearrange("k p n -> p k n"))

            def pair(b, p, n, following):
                load_down(b, p, n)
                if following is not None:
                    nb, np_, nn = following
                    for s in range(nn):
                        load_up(nb, np_, s)

            def load_wout(i):
                raw_load(2, i, raw[2][:, :].rearrange("p (k n) -> p k n", k=2),
                         t["w_out"][2 * i:2 * i + 2].rearrange("k p n -> p k n"))

            load_wout(0)
            for s in range(2):
                load_up(blocks[0], 0, s)
            load_wout(1)
            for b in blocks:
                if b.attention:
                    continue
                full = sum(n == 2 for n in b.pairs[1:])
                if full:
                    with sp.Fori(0, full) as p:
                        pair(b, p, 2, (b, p + 1, 2))
                for p in range(full, len(b.pairs)):
                    if p + 1 < len(b.pairs):
                        pair(b, p, b.pairs[p], (b, p + 1, b.pairs[p + 1]))
                    elif b.next_up is not None:
                        pair(b, p, b.pairs[p], (b.next_up, 0, 2))
                    else:
                        pair(b, p, b.pairs[p], None)

            def store(p, u):
                wait(sp, "out_done", 2 * p + u + 1)
                sp.dma_start(t["out"][bass.ds((2 * p + u) * P, P), :], xn[u][:, :]
                             ).then_inc(S[f"out_sent{u}"], 16)

            with sp.Fori(0, NT // 2) as p:
                for u in range(2):
                    store(p, u)
            for u in range(2):
                sp.wait_ge(S[f"out_sent{u}"], 16 * NT // 2)

        @block.gpsimd
        def _(pool):
            def select(out, op, base, cm, step):
                pool.wait_ge(S["pool_step"], 1)
                pool.affine_select(out=out[:, :], in_=ones[:, :], compare_op=op, fill=0.0, base=base,
                                   pattern=[[step, P]], channel_multiplier=cm).then_inc(S["consts"], 1)

            pool.memset(ones[:, :], 1.0).then_inc(S["pool_step"], 1)
            select(ident, ALU.is_equal, 0, 1, -1)
            select(tri, ALU.is_ge, 0, -1, 1)
            select(after, ALU.is_gt, 0, 1, -1)
            pool.memset(xBC[:, :, 0:TAPS - 1], 0.0).then_inc(S["pads"], 1)

            def lo(slot, use, src, hi, dst):
                wait(pool, f"w_hi{slot}", use + 1)
                pool.tensor_tensor(dst, src, hi.bitcast(F32), ALU.subtract).then_inc(S[f"w_lo{slot}"], 1)

            def lo_win(piece):
                s = piece % 2
                lo(s, piece // 2, raw[s][:, :].rearrange("p (a k n) -> p a k n", a=2, k=KD),
                   up_hi[s][:, :, :, :], up_lo[s][:, :, :, :])

            def lo_up(b, p, s):
                w = b.mats * KD * P
                lo(s, b.use0[s] + p, raw[s][:, 0:w].rearrange("p (a k n) -> p a k n", a=b.mats, k=KD),
                   up_hi[s][:, 0:b.mats, :, :], up_lo[s][:, 0:b.mats, :, :])

            def lo_down(b, p, n):
                at = bass.ds(2 * p, n)
                lo(2, b.use0[2] + p, raw[2][:, 0:n * D].rearrange("p (k n) -> p k n", k=n),
                   wd_hi[:, at, :], wd_lo[:, at, :])

            lo_win(0)
            lo_win(1)

            adds = [0]

            def sum_wp(i):
                g, half = i // 2, i % 2
                pool.wait_ge(S[f"wp_in{i % 2}"], 16 * (i // 2 + 1))
                for r in range(2):
                    if half == 0 and r == 0:
                        continue
                    if half == 0:
                        ins = pool.tensor_tensor(wps[:, g, :], wpraw[0][:, 0, :], wpraw[0][:, 1, :], ALU.add)
                    else:
                        pool.wait_ge(S["wp_summed"], adds[0])
                        if r == 1:
                            pool.wait_ge(S["pool_step"], 2 + g)
                        ins = pool.tensor_tensor(wps[:, g, :], wps[:, g, :], wpraw[1][:, r, :], ALU.add)
                    if half == 1 and r == 0:
                        ins.then_inc(S["pool_step"], 1)
                    else:
                        adds[0] += 1
                        ins.then_inc(S["wp_summed"], 1)

            for i in range(2 * NKV):
                sum_wp(i)
                if i == 9:
                    lo_win(2)
                if i == 12:
                    lo_win(3)
            lo_win(4)
            for s in range(2):
                lo_up(blocks[0], 0, s)

            def prepare(c):
                wait(pool, "g_mm", c)
                pool.tensor_copy(stXB[:, :, :], xBC[:, 0:2, bass.ds(c * P + TAPS - 1, P)]
                                 ).then_inc(S["st_xb"], 1)
                wait(pool, "e_mm", c)
                a = decay[:, bass.ds(c, 1), :].rearrange("p o h -> p (o h)")
                pool.tensor_tensor(atri[:, :, :], heads(tri[:, :]), per_head(a), ALU.mult
                                   ).then_inc(S["atri_done"], 1)
                wait(pool, "edm_done", c)
                dt = dt_sp[:, bass.ds(c, 1), :].rearrange("p o h -> p (o h)")
                pool.tensor_tensor(dtri[:, :, :], heads(tri[:, :]), per_head(dt), ALU.mult
                                   ).then_inc(S["dtri_done"], 1)

            def scale(c):
                at = bass.ds(c * P + TAPS - 1, P)
                wait(pool, "expd_done", c + 1)
                wait(pool, "dtri_done", c + 1)
                pool.tensor_tensor(eD[:, :, :], eD[:, :, :], dtri[:, :, :], ALU.mult).then_inc(S["edm_done"], 1)
                wait(pool, "expe_done", c + 1)
                wait(pool, "y_mm", c)
                pool.tensor_tensor(Cs[:, :, :], xBC[:, 2:6, at], eE[:, :, :], ALU.mult).then_inc(S["cs_done"], 1)
                wait(pool, "y1_done", c)
                xs = xBC[:, 0:1, at].rearrange("p o n -> p (o n)")
                pool.tensor_tensor(xsD[:, :, :], heads(xs), per_head(heads_in[:, 1, :]), ALU.mult
                                   ).then_inc(S["xsd_done"], 1)

            def add_x(c):
                wait(pool, "ht_done", c + 1)
                at = bass.ds(c, 1)
                pool.tensor_tensor(xres[:, at, :], xres[:, at, :], rb[0][:, :].unsqueeze(1), ALU.add
                                   ).then_inc(S["xres_done"], 1)

            pool.wait_ge(S["a_done"], 1)
            pool.wait_ge(S["conv_silu"], NCONV)
            prepare(0)
            scale(0)
            prepare(1)
            with pool.Fori(1, NT - 1) as s:
                scale(s)
                prepare(s + 1)
                add_x(s - 1)
            scale(NT - 1)
            add_x(NT - 2)
            add_x(NT - 1)

            def stage_lo(b, tile, u):
                wait(pool, "st_hi_done", b.down0 + tile + 1)
                k = 0
                ins = None
                if b.attention or (b.layer == "E" and b.final):
                    ins = pool.tensor_copy(st_lo[u][:, 0:KD, :], xT_lo[:, :, tok(tile)].bitcast(F32))
                    k = KD
                if not b.attention:
                    ins = pool.tensor_tensor(st_lo[u][:, k:k + b.tiles, :], hT[:, 0:b.tiles, tok(tile)],
                                             st_hi[u][:, k:k + b.tiles, :].bitcast(F32), ALU.subtract)
                ins.then_inc(S["st_lo_done"], 1)

            def add_shared(b, tile, u):
                wait(pool, "routed_done", tile + 1)
                wait(pool, "r_done", b.down0)
                pool.tensor_tensor(rb[u][:, :].unsqueeze(1), rb[u][:, :].unsqueeze(1),
                                   shared[:, bass.ds(tile, 1), :], ALU.add).then_inc(S["both_done"], 1)

            def split_mix(src):
                wait(pool, "mixhl_hi", 1 if src is mix else 2)
                pool.tensor_tensor(mix_lo[:, :, :], src[:, :, :], mix_hi[:, :, :].bitcast(F32),
                                   ALU.subtract).then_inc(S["mixhl_lo"], 1)

            def pair(b, p, n, following, last_pair=False):
                lo_down(b, p, n)
                if last_pair:
                    for u in range(2):
                        stage_lo(b, u, u)
                if following is not None:
                    nb, np_, nn = following
                    for s in range(nn):
                        lo_up(nb, np_, s)

            for i, b in enumerate(blocks):
                if not b.attention:
                    full = sum(n == 2 for n in b.pairs[1:])
                    if full:
                        with pool.Fori(0, full) as p:
                            pair(b, p, 2, (b, p + 1, 2))
                    for p in range(full, len(b.pairs)):
                        if p + 1 < len(b.pairs):
                            pair(b, p, b.pairs[p], (b, p + 1, b.pairs[p + 1]))
                        elif b.next_up is not None:
                            pair(b, p, b.pairs[p], (b.next_up, 0, 2), last_pair=True)
                        else:
                            pair(b, p, b.pairs[p], None, last_pair=True)
                    if b.layer == "F" and b.final:
                        split_mix(mix)
                    if b.layer == "E" and not b.final:
                        split_mix(lat)
                if b.attention:
                    for u in range(2):
                        stage_lo(b, u, u)
                with pool.Fori(0, NT // 2 - 1) as p:
                    for u in range(2):
                        stage_lo(b, 2 * p + u + 2, u)
                        if b.layer == "E" and b.final:
                            add_shared(b, 2 * p + u, u)
                for u in range(2):
                    if b.layer == "E" and b.final:
                        add_shared(b, NT - 2 + u, u)

        @block.scalar
        def _(act):
            def copy(dst, src, name):
                return act.activation(dst, src, ACT.Copy).then_inc(S[name], 1)

            def hi(slot, use, src, dst):
                wait(act, f"raw_in{slot}", 16 * (use + 1))
                copy(dst, src, f"w_hi{slot}")

            def hi_win(piece):
                s = piece % 2
                hi(s, piece // 2, raw[s][:, :].rearrange("p (a k n) -> p a k n", a=2, k=KD),
                   up_hi[s][:, :, :, :])

            def hi_up(b, p, s):
                w = b.mats * KD * P
                hi(s, b.use0[s] + p, raw[s][:, 0:w].rearrange("p (a k n) -> p a k n", a=b.mats, k=KD),
                   up_hi[s][:, 0:b.mats, :, :])

            def hi_down(b, p, n):
                hi(2, b.use0[2] + p, raw[2][:, 0:n * D].rearrange("p (k n) -> p k n", k=n),
                   wd_hi[:, bass.ds(2 * p, n), :])

            def evac_hi(j, tile, bk):
                wait(act, "tr_mm", j + 1)
                copy(xT_hi[:, :, tok(tile)], bank[bk][:, :].rearrange("p (k n) -> p k n", k=KD), "xT_hi_done")

            act.preload_act_table(ACT.Silu)
            hi_win(0)
            hi_win(1)

            def evac_p1(g):
                piece, half, f = g // 4, g // 2 % 2, g % 2
                i = 2 * piece + f
                wait(act, "p1_mm", g + 1)
                if i < NCONV:
                    copy(xBC[:, i, TAPS - 1 + half * HALF:TAPS - 1 + (half + 1) * HALF], bank[g % 4][:, :], "p1_done")
                else:
                    act.activation(z[:, i - NCONV, half * HALF:(half + 1) * HALF], bank[g % 4][:, :],
                                   ACT.Silu).then_inc(S["p1_done"], 1)

            def evac_lat(n):
                wait(act, "lat_mm", n + 1)
                copy(lat[:, n, :], bank[4 + n % 2][:, :], "lat_done")

            evac_hi(0, 0, 6)
            evac_hi(1, 1, 7)
            for n in range(2):
                wait(act, "e2_mm", n + 1)
                copy(lat_e2[:, n, :], bank[4 + n][:, :], "e2_done")
            evac_hi(2, 2, 6)
            evac_hi(3, 3, 7)
            evac_p1(0)
            evac_hi(4, 4, 6)
            evac_p1(1)
            evac_hi(5, 5, 7)
            evac_lat(0)
            evac_lat(1)
            evac_hi(6, 6, 6)
            evac_lat(2)
            evac_lat(3)
            evac_hi(7, 7, 7)
            evac_p1(2)
            evac_p1(3)
            act.wait_ge(S["pads"], 1)

            def conv_silu(i):
                wait(act, "conv_done", i + 1)
                act.activation(xBC[:, i, TAPS - 1:], acc[i % 2][:, :], ACT.Silu, bias=conv_b[:, i:i + 1]
                               ).then_inc(S["conv_silu"], 1)

            act.wait_ge(S["small_in"], 16 * 5)
            for piece in range(5):
                if piece:
                    for g in range(4 * piece, 4 * piece + 4):
                        evac_p1(g)
                if piece + 2 < 5:
                    hi_win(piece + 2)
                if 1 <= piece <= 3:
                    conv_silu(2 * piece - 2)
                    conv_silu(2 * piece - 1)
            act.preload_act_table(ACT.Exp)
            act.activation(neg_A[:, :], heads_in[:, 0, :], ACT.Exp).then_inc(S["dt_exp"], 1)
            act.wait_ge(S["dt_v"], 1)
            act.activation(dts[2][:, :, :], dts[1][:, :, :], ACT.Exp, scale=-1.0).then_inc(S["dt_exp"], 1)
            for s in range(2):
                hi_up(blocks[0], 0, s)
            act.wait_ge(S["end_mm"], 1)
            act.activation(dts[3][:, :, :], bank[4][:, 32:64].rearrange("p (c h) -> p c h", c=NT), ACT.Exp
                           ).then_inc(S["end_exp"], 1)
            for n in range(KD):
                wait(act, "mix_mm", n + 1)
                copy(mix[:, n, :], bank[n][:, :], "mix_done")
            for i in range(2):
                hi(2, i, raw[2][:, :].rearrange("p (k n) -> p k n", k=2), wo_hi[:, 2 * i:2 * i + 2, :])

            def ssd_step(c, transposed):
                wait(act, "xbt_mm", c + 1)
                wait(act, "s_mm", c)
                copy(XBt[:, :, :], bank[6][:, 0:2 * P].rearrange("p (a n) -> p a n", a=2), "xbt_done")
                wait(act, "d_mm", c + 1)
                wait(act, "att_done", c)
                act.activation(eD[:, :, :], bank[1][:, :].rearrange("p (h n) -> p h n", h=NH), ACT.Exp
                               ).then_inc(S["expd_done"], 1)
                wait(act, "e_mm", c + 1)
                wait(act, "cs_done", c)
                wait(act, "state_done", c)
                act.activation(eE[:, :, :], bank[2][:, :].rearrange("p (h n) -> p h n", h=NH), ACT.Exp
                               ).then_inc(S["expe_done"], 1)
                if transposed:
                    evac_hi(NT + c - 2, c - 2, 7)
                wait(act, "y_done", c + 1)
                wait(act, "o_mm", c)
                copy(y_hi[:, :, :], y[:, :, :], "yhi_done")

            ssd_step(0, False)
            ssd_step(1, False)
            with act.Fori(2, NT) as s:
                ssd_step(s, True)
            evac_hi(2 * NT - 2, NT - 2, 7)

            def activate(b, g, par):
                wait(act, "gate_mm" if b.mats == 2 else "up_mm", g + 1)
                wait(act, "h_done", g - 1)
                act.activation(sg[par][:, :], bank[2 * par][:, :], ACT.Relu if b.layer == "E" else ACT.Silu
                               ).then_inc(S["act_done"], 1)

            def stage_hi(b, tile, u):
                wait(act, "down_mm", b.down0 + tile - 1)
                k = 0
                ins = None
                if b.attention or (b.layer == "E" and b.final):
                    if b.attention:
                        wait(act, "xT_lo_done", b.norm0 - NT + tile + 1)
                    ins = act.activation(st_hi[u][:, 0:KD, :], xT_hi[:, :, tok(tile)].bitcast(F32), ACT.Copy)
                    k = KD
                if not b.attention:
                    ins = act.activation(st_hi[u][:, k:k + b.tiles, :], hT[:, 0:b.tiles, tok(tile)], ACT.Copy)
                ins.then_inc(S["st_hi_done"], 1)

            def pair(b, p, n, following, pending=None, last_pair=False):
                g = b.group0 + 4 * p
                activate(b, g, 0)
                if pending is not None:
                    evac_hi(*pending)
                if n == 2:
                    activate(b, g + 1, 1)
                hi_down(b, p, n)
                last = g + n
                activate(b, last, n % 2)
                if last_pair:
                    wait(act, "h_done", b.group1 - n)
                    for u in range(2):
                        stage_hi(b, u, u)
                if following is not None:
                    nb, np_, nn = following
                    wait(act, "up_mm", last + 1)
                    hi_up(nb, np_, 0)
                if n == 2:
                    activate(b, last + 1, 1)
                if following is not None and following[2] == 2:
                    if n == 2:
                        wait(act, "up_mm", last + 2)
                    hi_up(nb, np_, 1)

            def keep_xn(b, tile, u):
                wait(act, "xn_done", b.norm0 + tile + 1)
                copy(xres[:, bass.ds(tile, 1), :], xn[u][:, :].unsqueeze(1), "xres_done")

            act.preload_act_table(ACT.Silu)
            for i, b in enumerate(blocks):
                pending = None
                if b.fresh:
                    pending = (b.norm0 - 1, NT - 1, 7)
                if not b.attention:
                    full = sum(n == 2 for n in b.pairs[1:])
                    first = 1 if b.fresh else 0
                    for p in range(first):
                        pair(b, p, b.pairs[p], (b, p + 1, b.pairs[p + 1]), pending)
                    if full > first:
                        with act.Fori(first, full) as p:
                            pair(b, p, 2, (b, p + 1, 2))
                    for p in range(max(first, full), len(b.pairs)):
                        if p + 1 < len(b.pairs):
                            pair(b, p, b.pairs[p], (b, p + 1, b.pairs[p + 1]))
                        elif b.next_up is not None:
                            pair(b, p, b.pairs[p], (b.next_up, 0, 2), last_pair=True)
                        else:
                            pair(b, p, b.pairs[p], None, last_pair=True)
                    pending = None
                    if b.layer == "F" and b.final:
                        copy(mix_hi[:, :, :], mix[:, :, :], "mixhl_hi")
                    if b.layer == "E" and not b.final:
                        copy(mix_hi[:, :, :], lat[:, :, :], "mixhl_hi")
                keep = b.final and b.layer != "E"
                if b.attention:
                    for u in range(2):
                        stage_hi(b, u, u)

                def step(tile, u, stage, evac):
                    if stage:
                        stage_hi(b, tile + 2, u)
                    if evac:
                        evac_hi(b.norm0 + tile - 1, tile - 1, 6 + (u + 1) % 2)
                        keep_xn(b, tile - 1, (u + 1) % 2)
                    if b.layer == "E" and b.final:
                        wait(act, "route_done", tile + 1)
                        wait(act, "route_mm", tile + 1)
                        wait(act, "out_done", tile - 1)
                        act.activation(rb[u][:, :], bank[6 + u][:, :], ACT.Copy, scale=route[u][:, 0:1]
                                       ).then_inc(S["routed_done"], 1)

                step(0, 0, True, False)
                if pending is not None:
                    evac_hi(*pending)
                step(1, 1, True, keep)
                if not b.attention:
                    wait(act, "h_done", b.group1)
                with act.Fori(1, NT // 2 - 1) as p:
                    for u in range(2):
                        step(2 * p + u, u, True, keep)
                for u in range(2):
                    step(NT - 2 + u, u, False, keep)
                if keep:
                    keep_xn(b, NT - 1, 1)

        @block.vector
        def _(dve):
            base = [0]
            n = [0]

            def link(ins):
                n[0] += 1
                ins.then_inc(S["dve_step"], 1)
                dve.wait_ge(S["dve_step"], base[0] + n[0])

            def loop(start, stop, per, body):
                b0 = base[0] + n[0]
                with dve.Fori(start, stop) as i:
                    base[0], n[0] = b0 + (i - start) * per, 0
                    body(i)
                    assert n[0] == per, (n[0], per)
                base[0], n[0] = b0 + (stop - start) * per, 0

            LN_STEPS = 4 + 2 * NEWTON
            RMS_STEPS = 5 + 2 * NEWTON

            def alone():
                dve.memset(spare[:, :], 0.0)

            def rstd(src, rms, meanwhile=alone):
                link(dve.bn_stats(stat[:, :], src))
                meanwhile()
                link(dve.bn_aggr(mv[:, :], stat[:, :]))
                if rms:
                    link(dve.scalar_tensor_tensor(out=rt[:, :], in0=mv[:, 0:1], scalar=mv[:, 0:1],
                                                  in1=mv[:, 1:2], op0=ALU.mult, op1=ALU.add))
                link(dve.tensor_scalar(ve[:, :], rt[:, :] if rms else mv[:, 1:2], EPS, 0.5, ALU.add, ALU.mult))
                link(dve.tensor_scalar(ry[:, :].bitcast(I32), ve[:, :].bitcast(I32), -0.5, RSQRT_GUESS,
                                       ALU.mult, ALU.add))
                for _ in range(NEWTON):
                    link(dve.scalar_tensor_tensor(out=rt[:, :], in0=ry[:, :], scalar=ve[:, :], in1=ry[:, :],
                                                  op0=ALU.mult, op1=ALU.mult))
                    link(dve.scalar_tensor_tensor(out=ry[:, :], in0=rt[:, :], scalar=1.5, in1=ry[:, :],
                                                  op0=ALU.subtract, op1=ALU.mult))

            def evac_lo(j, tile, bk):
                wait(dve, "xT_hi_done", j + 1)
                dve.tensor_tensor(xT_lo[:, :, tok(tile)], bank[bk][:, :].rearrange("p (k n) -> p k n", k=KD),
                                  xT_hi[:, :, tok(tile)].bitcast(F32), ALU.subtract
                                  ).then_inc(S["xT_lo_done"], 1)

            dve.wait_ge(S["gains_in"], 16)
            for j in range(NT):
                if j % 2 == 0:
                    dve.wait_ge(S[f"x_in{j // 2}"], 16)
                rstd(xres[:, j, :], True)
                wait(dve, "tr_mm", j - 1)
                dve.scalar_tensor_tensor(out=xn[j % 2][:, :], in0=xres[:, j, :], scalar=ry[:, 0:1],
                                         in1=ln1[:, :], op0=ALU.mult, op1=ALU.mult).then_inc(S["xn_done"], 1)
                if j:
                    evac_lo(j - 1, j - 1, 6 + (j - 1) % 2)
            evac_lo(NT - 1, NT - 1, 7)

            dve.wait_ge(S["small_in"], 16 * 5)
            for w, w_hi, w_lo in ((dtw, dtw_hi, dtw_lo), (gw, gw_hi, gw_lo)):
                link(dve.tensor_copy(w_hi[:, :, :], w[:, :, :]))
                dve.tensor_tensor(w_lo[:, :, :], w[:, :, :], w_hi[:, :, :].bitcast(F32), ALU.subtract
                                  ).then_inc(S["small_split"], 1)

            for i in range(NCONV):
                if i % 2 == 0:
                    dve.wait_ge(S["p1_done"], 2 * i + 4)
                if i == 0:
                    dve.wait_ge(S["pads"], 1)
                wait(dve, "conv_silu", i - 1)
                a = acc[i % 2]
                link(dve.tensor_scalar(a[:, :], xBC[:, i, TAPS - 1:], conv_w[:, i, TAPS - 1:TAPS], None, ALU.mult))
                for k in range(TAPS - 2, -1, -1):
                    ins = dve.scalar_tensor_tensor(out=a[:, :], in0=xBC[:, i, k:k + T], scalar=conv_w[:, i, k:k + 1],
                                                   in1=a[:, :], op0=ALU.mult, op1=ALU.add)
                    if k:
                        link(ins)
                    else:
                        ins.then_inc(S["conv_done"], 1)

            v, av, e_, s_, s2, pw = dts
            tail = dts[3]
            dve.wait_ge(S["dt_mm"], 1)
            link(dve.tensor_tensor(v[:, :, :], bank[4][:, 0:32].rearrange("p (c h) -> p c h", c=NT),
                                   heads_in[:, 2, :].unsqueeze(1).to_broadcast([P, NT, NH]), ALU.add))
            dve.scalar_tensor_tensor(out=av[:, :, :], in0=v[:, :, :], scalar=-1.0, in1=v[:, :, :],
                                     op0=ALU.mult, op1=ALU.max).then_inc(S["dt_v"], 1)
            dve.wait_ge(S["dt_exp"], 2)
            link(dve.tensor_scalar(s_[:, :, :], e_[:, :, :], 2.0, None, ALU.add))
            link(dve.reciprocal(s2[:, :, :], s_[:, :, :]))
            link(dve.tensor_tensor(s_[:, :, :], e_[:, :, :], s2[:, :, :], ALU.mult))
            link(dve.tensor_tensor(s2[:, :, :], s_[:, :, :], s_[:, :, :], ALU.mult))
            link(dve.tensor_scalar(pw[:, :, :], s2[:, :, :], 1.0 / 15, None, ALU.mult))
            for m in (13, 11, 9, 7, 5, 3):
                link(dve.scalar_tensor_tensor(out=pw[:, :, :], in0=pw[:, :, :], scalar=1.0 / m, in1=s2[:, :, :],
                                              op0=ALU.add, op1=ALU.mult))
            link(dve.scalar_tensor_tensor(out=pw[:, :, :], in0=pw[:, :, :], scalar=1.0, in1=s_[:, :, :],
                                          op0=ALU.add, op1=ALU.mult))
            link(dve.tensor_scalar(v[:, :, :], v[:, :, :], 0.0, None, ALU.max))
            link(dve.scalar_tensor_tensor(out=dt_sp[:, :, :], in0=pw[:, :, :], scalar=2.0, in1=v[:, :, :],
                                          op0=ALU.mult, op1=ALU.add))
            dve.scalar_tensor_tensor(out=decay[:, :, :], in0=dt_sp[:, :, :], scalar=-1.0,
                                     in1=neg_A[:, :].unsqueeze(1).to_broadcast([P, NT, NH]),
                                     op0=ALU.mult, op1=ALU.mult).then_inc(S["a_done"], 1)
            for i in range(2):
                wait(dve, "w_hi2", i + 1)
                dve.tensor_tensor(wo_lo[:, 2 * i:2 * i + 2, :], raw[2][:, :].rearrange("p (k n) -> p k n", k=2),
                                  wo_hi[:, 2 * i:2 * i + 2, :].bitcast(F32), ALU.subtract).then_inc(S["w_lo2"], 1)
            dve.wait_ge(S["end_exp"], 1)
            link(dve.tensor_tensor(to_end[:, :, :], tail[:, :, :], dt_sp[:, :, :], ALU.mult))

            def norm_h(c, j):
                wait(dve, "o_mm", c + 1)
                wait(dve, "xres_done", c)
                dve_in = xres[:, bass.ds(c, 1), :].rearrange("p o n -> p (o n)")
                dve.tensor_tensor(rb[0][:, :], bank[5][:, :], dve_in, ALU.add).then_inc(S["ht_done"], 1)
                wait(dve, "ht_done", c + 1)
                rstd(rb[0][:, :], True)
                wait(dve, "tr_mm", j)
                dve.scalar_tensor_tensor(out=xn[0][:, :], in0=rb[0][:, :], scalar=ry[:, 0:1],
                                         in1=ln2[:, :], op0=ALU.mult, op1=ALU.mult).then_inc(S["xn_done"], 1)

            def ssd_step(c, first, normed, transposed):
                wait(dve, "xbt_done", c + 1)
                wait(dve, "s_mm", c)
                w = to_end[:, bass.ds(c, 1), :].rearrange("p o h -> p (o h)")
                dve.tensor_tensor(Xs[:, :, :], heads(XBt[:, 0, :]), per_head(w), ALU.mult).then_inc(S["xs_done"], 1)
                wait(dve, "g_mm", c + 1)
                wait(dve, "edm_done", c + 1)
                wait(dve, "y_mm", c)
                dve.tensor_tensor(att[:, :, :], bank[0][:, :].rearrange("p (h n) -> p h n", h=NH), eD[:, :, :],
                                  ALU.mult).then_inc(S["att_done"], 1)
                if transposed:
                    evac_lo(NT + c - 2, c - 2, 7)
                if normed:
                    norm_h(c - 1, NT + c - 1)
                wait(dve, "y_mm", c + 1)
                wait(dve, "xsd_done", c + 1)
                dve.tensor_tensor(y[:, :, :], bank[3][:, :].rearrange("p (h n) -> p h n", h=NH), xsD[:, :, :],
                                  ALU.add).then_inc(S["y1_done"], 1)
                wait(dve, "y1_done", c + 1)
                dve.tensor_tensor(y[:, :, :], y[:, :, :], z[:, :, tok(c)], ALU.mult).then_inc(S["y_done"], 1)
                wait(dve, "s_mm", c + 1)
                if first:
                    dve.tensor_copy(state[:, :, :], bank[4][:, :].rearrange("p (h n) -> p h n", h=NH)
                                    ).then_inc(S["state_done"], 1)
                else:
                    wait(dve, "expe_done", c + 1)
                    for h in range(NH):
                        ins = dve.scalar_tensor_tensor(out=state[:, h, :], in0=state[:, h, :],
                                                       scalar=eE[:, h, P - 1:P], in1=bank[4][:, h * P:(h + 1) * P],
                                                       op0=ALU.mult, op1=ALU.add)
                    ins.then_inc(S["state_done"], 1)
                wait(dve, "yhi_done", c + 1)
                dve.tensor_tensor(y_lo[:, :, :], y[:, :, :], y_hi[:, :, :].bitcast(F32), ALU.subtract
                                  ).then_inc(S["ylo_done"], 1)

            dve.wait_ge(S["conv_silu"], NCONV)
            dve.wait_ge(S["gains_in"], 64)
            ssd_step(0, True, False, False)
            ssd_step(1, False, True, False)
            loop(2, NT, RMS_STEPS, lambda s: ssd_step(s, False, True, True))
            evac_lo(2 * NT - 2, NT - 2, 7)
            norm_h(NT - 1, 2 * NT - 1)

            def product(b, g, par, tile, half):
                wait(dve, "act_done", g + 1)
                wait(dve, "up_mm", g + 1)
                src = bank[2 * par] if b.layer == "E" else bank[2 * par + 1]
                dve.tensor_tensor(hT[:, bass.ds(tile, 1), half * HALF:(half + 1) * HALF], sg[par][:, :].unsqueeze(1),
                                  src[:, :].unsqueeze(1), ALU.mult).then_inc(S["h_done"], 1)

            def pair(b, p, n, pending=None):
                g = b.group0 + 4 * p
                product(b, g, 0, 2 * p, 0)
                if pending is not None:
                    evac_lo(*pending)
                if n == 2:
                    product(b, g + 1, 1, 2 * p + 1, 0)
                product(b, g + n, n % 2, 2 * p, 1)
                if n == 2:
                    product(b, g + n + 1, 1, 2 * p + 1, 1)

            def down_mid(b, tile, u):
                wait(dve, "down_mm", b.down0 + tile + 1)
                at = bass.ds(tile, 1)
                if b.layer == "E":
                    dve.tensor_copy(shared[:, at, :], bank[4 + u][:, :].unsqueeze(1)).then_inc(S["r_done"], 1)
                else:
                    dve.tensor_tensor(xres[:, at, :], xres[:, at, :], bank[4 + u][:, :].unsqueeze(1), ALU.add
                                      ).then_inc(S["r_done"], 1)

            def down_norm(b, tile, u, meanwhile=alone):
                wait(dve, "down_mm", b.down0 + tile + 1)
                xr = xres[:, bass.ds(tile, 1), :].rearrange("p o n -> p (o n)")
                dve.tensor_tensor(rb[u][:, :], bank[4 + u][:, :], xr, ALU.add).then_inc(S["r_done"], 1)
                wait(dve, "r_done", b.down0 + tile + 1)
                rstd(rb[u][:, :], False, meanwhile)
                wait(dve, "tr_mm", b.norm0 + tile - 1)
                wait(dve, "xres_done", b.norm0 - NT + tile - 1)
                dve.tensor_scalar(xn[u][:, :], rb[u][:, :], mv[:, 0:1], ry[:, 0:1], ALU.subtract, ALU.mult
                                  ).then_inc(S["xn_done"], 1)

            def down_out(b, tile, u):
                wait(dve, "route_mm", tile + 1)
                alone()
                link(dve.max(top8[:, :], bank[1 + 2 * u][:, 0:8]))
                wait(dve, "routed_done", tile - 1)
                dve.tensor_tensor(route[u][:, :], top8[:, 0:1], top8[:, 1:2], ALU.add).then_inc(S["route_done"], 1)
                wait(dve, "down_mm", b.down0 + tile + 1)
                wait(dve, "both_done", tile + 1)
                dve.tensor_tensor(rb[u][:, :], bank[4 + u][:, :], rb[u][:, :], ALU.add).then_inc(S["r_done"], 1)
                wait(dve, "r_done", b.down0 + tile + 1)
                rstd(rb[u][:, :], False)
                link(dve.tensor_scalar(rb[u][:, :], rb[u][:, :], mv[:, 0:1], ry[:, 0:1], ALU.subtract, ALU.mult))
                link(dve.tensor_tensor(rb[u][:, :], rb[u][:, :], gamma[:, :], ALU.mult))
                link(dve.tensor_tensor(rb[u][:, :], rb[u][:, :], beta[:, :], ALU.add))
                xr = xres[:, bass.ds(tile, 1), :].rearrange("p o n -> p (o n)")
                link(dve.tensor_tensor(rb[u][:, :], rb[u][:, :], xr, ALU.add))
                rstd(rb[u][:, :], False)
                dve.tensor_scalar(xn[u][:, :], rb[u][:, :], mv[:, 0:1], ry[:, 0:1], ALU.subtract, ALU.mult
                                  ).then_inc(S["out_done"], 1)

            for i, b in enumerate(blocks):
                pending = (b.norm0 - 1, NT - 1, 7) if b.fresh else None
                if not b.attention:
                    full = sum(k == 2 for k in b.pairs)
                    first = 1 if b.fresh else 0
                    if first:
                        pair(b, 0, b.pairs[0], pending)
                    if full > first:
                        loop(first, full, 0, lambda p: pair(b, p, 2))
                    if b.pairs[-1] == 1:
                        pair(b, len(b.pairs) - 1, 1)
                    pending = None
                if b.fresh:
                    wait(dve, "xres_done", b.norm0 - NT)
                if not b.final:
                    loop(0, NT // 2, 0, lambda p: [down_mid(b, 2 * p + u, u) for u in range(2)])
                elif b.layer == "E":
                    MOE = 1 + LN_STEPS + 4 + LN_STEPS
                    down_out(b, 0, 0)
                    down_out(b, 1, 1)

                    def out_pair(p):
                        for u in range(2):
                            wait(dve, f"out_sent{u}", 16 * p)
                            down_out(b, 2 * p + u, u)
                    loop(1, NT // 2, 2 * MOE, out_pair)
                else:
                    if pending is not None:
                        down_norm(b, 0, 0, lambda: evac_lo(*pending[:3]))
                    else:
                        down_norm(b, 0, 0)
                    down_norm(b, 1, 1, lambda: evac_lo(b.norm0, 0, 6))

                    def norm_pair(p):
                        for u in range(2):
                            down_norm(b, 2 * p + u, u,
                                      lambda: evac_lo(b.norm0 + 2 * p + u - 1, 2 * p + u - 1, 6 + (u + 1) % 2))
                    loop(1, NT // 2, 2 * LN_STEPS, norm_pair)

        @block.tensor
        def _(pe):
            def mm3(out, s_hi, s_lo, m_hi, m_lo, first, last):
                pe.matmul(out, s_hi, m_hi, start=first, stop=False)
                pe.matmul(out, s_hi, m_lo, start=False, stop=False)
                return pe.matmul(out, s_lo, m_hi, start=False, stop=last)

            def turn(j, src, bk, evacuated=None):
                wait(pe, "xn_done", j + 1)
                wait(pe, "xT_lo_done", j - 1 if evacuated is None else evacuated)
                for k in range(KD):
                    ins = pe.transpose(bank[bk][:, k * P:(k + 1) * P], src[:, k * P:(k + 1) * P], ident[:, :])
                ins.then_inc(S["tr_mm"], 1)

            def turn0(j):
                turn(j, xn[j % 2], 6 + j % 2)

            def p1_group(g):
                piece, half, f = g // 4, g // 2 % 2, g % 2
                s = piece % 2
                wait(pe, f"w_lo{s}", piece // 2 + 1)
                if g < 4:
                    wait(pe, "xT_lo_done", NT // 2 if half == 0 else NT)
                wait(pe, "p1_done", g - 3)
                for k in range(KD):
                    at = slice(half * HALF, (half + 1) * HALF)
                    ins = mm3(bank[g % 4][:, :], up_hi[s][:, f, k, :], up_lo[s][:, f, k, :],
                              xT_hi[:, k, at], xT_lo[:, k, at], k == 0, k == KD - 1)
                ins.then_inc(S["p1_mm"], 1)

            def lat_group(n):
                wait(pe, "lat_done", n - 1)
                for k in range(2):
                    ins = pe.matmul(bank[4 + n % 2][:, :], lat_fc1[:, k, n * P:(n + 1) * P], lat_e2[:, k, :],
                                    start=(k == 0), stop=(k == 1))
                ins.then_inc(S["lat_mm"], 1)

            pe.wait_ge(S["consts"], 3)
            turn0(0)
            turn0(1)
            pe.wait_ge(S["lat_in"], 48)
            for n in range(2):
                for k in range(2):
                    ins = pe.matmul(bank[4 + n][:, :], lat_exp[:, k, n * P:(n + 1) * P], lat_fc2[:, k, :],
                                    start=(k == 0), stop=(k == 1))
                ins.then_inc(S["e2_mm"], 1)
            turn0(2)
            turn0(3)
            p1_group(0)
            turn0(4)
            p1_group(1)
            turn0(5)
            pe.wait_ge(S["e2_done"], 2)
            lat_group(0)
            lat_group(1)
            turn0(6)
            lat_group(2)
            lat_group(3)
            turn0(7)
            for g in range(2, 12):
                p1_group(g)
            pe.wait_ge(S["small_split"], 2)
            pe.wait_ge(S["lat_done"], KD)
            for c in range(NT):
                for k in range(KD):
                    ins = mm3(bank[4][:, c * NH:(c + 1) * NH], xT_hi[:, k, c * P:(c + 1) * P],
                              xT_lo[:, k, c * P:(c + 1) * P], dtw_hi[:, k, :], dtw_lo[:, k, :], k == 0, k == KD - 1)
            ins.then_inc(S["dt_mm"], 1)
            for g in range(12, 20):
                p1_group(g)
            pe.wait_ge(S["p1_done"], 20)
            pe.wait_ge(S["wv_in"], 16)
            for g in range(NKV):
                if g == NKV // 2:
                    pe.wait_ge(S["a_done"], 1)
                    pe.matmul(bank[4][:, 32:64], after[:, :], decay[:, :, :].rearrange("p c h -> p (c h)"),
                              start=True, stop=True).then_inc(S["end_mm"], 1)
                pe.wait_ge(S["wp_summed"], 2 * (g + 1))
                for n in range(KD):
                    ins = pe.matmul(bank[n][:, :], wv[:, g, n * P:(n + 1) * P], wps[:, g, :],
                                    start=(g == 0), stop=(g == NKV - 1))
                    if g == NKV - 1:
                        ins.then_inc(S["mix_mm"], 1)
            pe.wait_ge(S["mix_done"], KD)
            pe.wait_ge(S["end_exp"], 1)

            def scores(c):
                wait(pe, "st_xb", c + 1)
                wait(pe, "xbt_done", c)
                for i in range(2):
                    ins = pe.transpose(bank[6][:, i * P:(i + 1) * P], stXB[:, i, :], ident[:, :])
                ins.then_inc(S["xbt_mm"], 1)
                wait(pe, "att_done", c)
                pe.matmul(bank[0][:, :].rearrange("p (h n) -> p h n", h=NH), stXB[:, 1, :],
                          xBC[:, 2:6, bass.ds(c * P + TAPS - 1, P)], start=True, stop=True
                          ).then_inc(S["g_mm"], 1)
                wait(pe, "atri_done", c + 1)
                wait(pe, "expd_done", c)
                flat = atri[:, :, :].rearrange("p h n -> p (h n)")
                pe.matmul(bank[1][:, :], after[:, :], flat, start=True, stop=True).then_inc(S["d_mm"], 1)
                wait(pe, "expe_done", c)
                pe.matmul(bank[2][:, :], ones[:, :], flat, start=True, stop=True).then_inc(S["e_mm"], 1)

            def mixed(c, first):
                wait(pe, "att_done", c + 1)
                wait(pe, "y1_done", c)
                pe_ins = pe.matmul(bank[3][:, :], XBt[:, 0, :], att[:, :, :].rearrange("p h n -> p (h n)"),
                                   start=True, stop=first)
                if not first:
                    wait(pe, "cs_done", c + 1)
                    wait(pe, "state_done", c)
                    for h in range(NH):
                        pe_ins = pe.matmul(bank[3][:, h * P:(h + 1) * P], state[:, h, :], Cs[:, h, :],
                                           start=False, stop=(h == NH - 1))
                pe_ins.then_inc(S["y_mm"], 1)
                wait(pe, "xs_done", c + 1)
                wait(pe, "state_done", c)
                pe.matmul(bank[4][:, :], XBt[:, 1, :], Xs[:, :, :].rearrange("p h n -> p (h n)"),
                          start=True, stop=True).then_inc(S["s_mm"], 1)

            def project(c):
                wait(pe, "ylo_done", c + 1)
                wait(pe, "ht_done", c)
                for k in range(KD):
                    ins = mm3(bank[5][:, :], y_hi[:, k, :], y_lo[:, k, :], wo_hi[:, k, :], wo_lo[:, k, :],
                              k == 0, k == KD - 1)
                ins.then_inc(S["o_mm"], 1)

            def turn_h(c):
                wait(pe, "xn_done", NT + c + 1)
                wait(pe, "xT_lo_done", NT + c)
                for k in range(KD):
                    ins = pe.transpose(bank[7][:, k * P:(k + 1) * P], xn[0][:, k * P:(k + 1) * P], ident[:, :])
                ins.then_inc(S["tr_mm"], 1)

            scores(0)
            mixed(0, True)
            scores(1)
            pe.wait_ge(S["w_lo2"], 2)
            project(0)
            mixed(1, False)
            with pe.Fori(2, NT) as s:
                scores(s)
                turn_h(s - 2)
                project(s - 1)
                mixed(s, False)
            turn_h(NT - 2)
            project(NT - 1)

            def group(b, g, par, s, half):
                wait(pe, "h_done", g - 1)
                at = slice(half * HALF, (half + 1) * HALF)
                for m in range(b.mats):
                    for k in range(KD):
                        ins = mm3(bank[2 * par + m][:, :], up_hi[s][:, m, k, :], up_lo[s][:, m, k, :],
                                  xT_hi[:, k, at], xT_lo[:, k, at], k == 0, k == KD - 1)
                    if m == 0 and b.mats == 2:
                        ins.then_inc(S["gate_mm"], 1)
                ins.then_inc(S["up_mm"], 1)

            def pair(b, p, n, pending=None):
                g = b.group0 + 4 * p
                if pending is not None:
                    wait(pe, "xT_lo_done", b.norm0 - NT // 2)
                wait(pe, "w_lo0", b.use0[0] + p + 1)
                group(b, g, 0, 0, 0)
                if pending is not None:
                    turn(*pending)
                if n == 2:
                    wait(pe, "w_lo1", b.use0[1] + p + 1)
                    group(b, g + 1, 1, 1, 0)
                if pending is not None:
                    wait(pe, "xT_lo_done", b.norm0)
                group(b, g + n, n % 2, 0, 1)
                if n == 2:
                    group(b, g + n + 1, 1, 1, 1)

            def down(b, tile, u):
                wait(pe, "st_lo_done", b.down0 + tile + 1)
                moe = b.layer == "E" and b.final
                k0 = KD if moe else 0
                if moe:
                    wait(pe, "routed_done", tile - 1)
                    for k in range(KD):
                        mm3(bank[1 + 2 * u][:, 0:8], st_hi[u][:, k, :], st_lo[u][:, k, :], gw_hi[:, k, :], gw_lo[:, k, :],
                            k == 0, k == KD - 1)
                    for k in range(KD):
                        ins = mm3(bank[6 + u][:, :], st_hi[u][:, k, :], st_lo[u][:, k, :],
                                  mix_hi[:, k, :], mix_lo[:, k, :], k == 0, k == KD - 1)
                    ins.then_inc(S["route_mm"], 1)
                wait(pe, "r_done", b.down0 + tile - 1)
                n = KD if b.attention else b.tiles
                w_hi, w_lo = (mix_hi, mix_lo) if b.attention else (wd_hi, wd_lo)
                for k in range(n):
                    ins = mm3(bank[4 + u][:, :], st_hi[u][:, k0 + k, :], st_lo[u][:, k0 + k, :],
                              w_hi[:, k, :], w_lo[:, k, :], k == 0, k == n - 1)
                ins.then_inc(S["down_mm"], 1)

            for i, b in enumerate(blocks):
                pending = None
                if b.fresh:
                    pending = (b.norm0 - 1, xn[0] if i == 0 else xn[1], 7, b.norm0 - 1 if i == 0 else None)
                if not b.attention:
                    full = sum(k == 2 for k in b.pairs)
                    first = 1 if b.fresh else 0
                    if first:
                        pair(b, 0, b.pairs[0], pending)
                    if full > first:
                        with pe.Fori(first, full) as p:
                            pair(b, p, 2)
                    if b.pairs[-1] == 1:
                        pair(b, len(b.pairs) - 1, 1)
                    pending = None
                    wait(pe, "w_lo2", b.use0[2] + len(b.pairs))
                else:
                    wait(pe, "mixhl_lo", 1)
                if b.layer == "E" and b.final:
                    wait(pe, "mixhl_lo", 2)
                keep = b.final and b.layer != "E"
                down(b, 0, 0)
                if pending is not None:
                    turn(*pending)
                down(b, 1, 1)
                if keep:
                    turn(b.norm0, xn[0], 6)
                with pe.Fori(1, NT // 2) as p:
                    for u in range(2):
                        down(b, 2 * p + u, u)
                        if keep:
                            turn(b.norm0 + 2 * p + u - 1, xn[(u + 1) % 2], 6 + (u + 1) % 2)


def lay_out(a):
    import numpy as np
    f = {k: np.asarray(v) for k, v in a.items()}
    cont = np.ascontiguousarray

    def up(*mats):
        o, i = mats[0].shape
        m = np.stack([w.reshape(o // P, P, i // P, P).transpose(0, 3, 2, 1) for w in mats], axis=2)
        return cont(m.reshape(o // P, P, -1))

    def rows(w):
        return w.reshape(w.shape[0] // P, P, -1)

    def by_partition(w):
        return cont(rows(w).transpose(1, 0, 2))

    def pad_rows(w):
        return np.concatenate([w, np.zeros((-w.shape[0] % P, w.shape[1]), w.dtype)])

    w_in = f["L0_attn_w_in"]
    d_inner, d_xb = D, P
    x_b_c = w_in[d_inner:2 * d_inner + 2 * d_xb]
    feat = np.concatenate([x_b_c, w_in[:d_inner]])
    tiles = feat.reshape(10, P, KD, P).transpose(0, 3, 2, 1)
    out = {
        "x": f["L0_attn_hidden_states"][0],
        "w_in": cont(tiles.reshape(5, 2, P, KD * P).transpose(0, 2, 1, 3).reshape(5, P, 2 * KD * P)),
        "dtw": by_partition(w_in[2 * d_inner + 2 * d_xb:].T),
        "conv_w": cont(f["L0_attn_conv_w"].reshape(NCONV, P, TAPS).transpose(1, 0, 2)),
        "conv_b": cont(f["L0_attn_conv_b"].reshape(NCONV, P).T),
        "heads": np.stack([f["L0_attn_A_log"], f["L0_attn_D"], f["L0_attn_dt_bias"]]),
        "w_out": cont(rows(f["L0_attn_w_out"].T)),
        "gains": np.stack([f["L0_attn_ln1_w"], f["L0_attn_ln2_w"], f["L1_ffn_ln_gamma"], f["L1_ffn_ln_beta"]]),
        "up_M": up(f["L0_attn_gate_w"], f["L0_attn_up_w"]),
        "down_M": cont(rows(f["L0_attn_down_w"].T)),
        "up_F": up(pad_rows(f["L0_ffn_W_gate"]), pad_rows(f["L0_ffn_W_up"])),
        "down_F": cont(rows(pad_rows(f["L0_ffn_W_down"].T))),
        "up_E": up(f["L1_ffn_up_w"].T),
        "down_E": rows(f["L1_ffn_down_w"]),
        "gw": by_partition(f["L1_ffn_gate_w"]),
        "expert": by_partition(f["L1_ffn_expert_w"].T),
        "fc2": by_partition(f["L1_ffn_fc2_w"]),
        "fc1": by_partition(f["L1_ffn_fc1_w"].T),
    }
    qkv = f["L1_attn_weight_qkv"].reshape(NKV, 6, P, D)
    out["wv"] = cont(qkv[:, 5].transpose(1, 0, 2))
    proj = f["L1_attn_weight_proj"].reshape(D, NKV, 2, 2, P)
    out["wp"] = cont(proj.transpose(1, 2, 4, 3, 0).reshape(2 * NKV, P, 2, D))
    return {k: cont(v) for k, v in out.items()}


def kernel(**inputs):
    import concourse.bacc as bacc
    from concourse.bass_utils import run_bass_kernel_spmd

    arrays = lay_out(inputs)
    nc = bacc.Bacc("TRN2", target_bir_lowering=False, num_devices=1)
    t = {k: nc.dram_tensor("in_" + k, v.shape, mybir.dt.from_np(v.dtype), kind="ExternalInput").ap()
         for k, v in arrays.items()}
    t["out"] = nc.dram_tensor("out", (T, D), F32, kind="ExternalOutput").ap()
    build_program(nc, t)
    r = run_bass_kernel_spmd(nc, [{"in_" + k: v for k, v in arrays.items()}], core_ids=[0])
    return r.results[0]["out"].reshape(1, T, D)
```

```python
import concourse.bass as bass
from concourse import mybir

P = 128
T = 1024
D = 512
NT = T // P
KD = D // P
HALF = 512
NH = 4
NCONV = 6
TAPS = 4
NKV = 8
EPS = 1e-5

F32 = mybir.dt.float32
F32R = mybir.dt.float32r
I32 = mybir.dt.int32
ALU = mybir.AluOpType
ACT = mybir.ActivationFunctionType

RSQRT_GUESS = float(0x5F3759DF - (1 << 22) - (1 << 31))
NEWTON = 3
BATCH = 4


class Block:

    def __init__(self, layer, first, tiles, final, attention=False):
        self.layer, self.first, self.tiles, self.final = layer, first, tiles, final
        self.attention = attention
        self.pairs = [min(2, tiles - 2 * p) for p in range((tiles + 1) // 2)]
        self.mats = 1 if layer == "E" else 2
        self.moe = layer == "E" and final


def plan():
    blocks = [Block("M", 0, 6, False), Block("M", 6, 4, False), Block("M", 10, 4, True),
              Block("F", 0, 6, False), Block("F", 6, 5, True),
              Block("A", 0, 0, True, attention=True),
              Block("E", 0, 4, False), Block("E", 4, 4, True)]
    groups, downs, norms, scales, kept = 0, 0, 2 * NT, 0, 0
    uses = [3, 2, 2]
    for b in blocks:
        b.group0, b.down0, b.use0, b.norm0, b.rstd0, b.kept0 = groups, downs, list(uses), norms, scales, kept
        groups += 2 * b.tiles
        downs += NT
        if not b.attention:
            uses[0] += len(b.pairs)
            uses[1] += sum(n == 2 for n in b.pairs)
            uses[2] += len(b.pairs)
        if b.final:
            norms += NT
            scales += NT // 2
            kept += NT
    ssd = Block("SSD", 0, 0, True)
    ssd.norm0 = NT
    for i, b in enumerate(blocks):
        b.group1 = b.group0 + 2 * b.tiles
        b.next_up = next((n for n in blocks[i + 1:] if not n.attention), None)
        before = blocks[i - 1] if i else ssd
        b.pending = before if before.final else None
        b.fresh = b.pending is not None
    return blocks


def build_program(nc, t):
    blocks = plan()
    here = [16512]

    def place(name, shape, dtype=F32, at=None):
        size = 4
        for n in shape:
            size *= n
        if at is None:
            at = here[0]
            here[0] = at + (size + 31) // 32 * 32
        return nc.alloc_sbuf_tensor_at(name, [P, *shape], dtype, offset=at), at + (size + 31) // 32 * 32

    xres, _ = place("xres", [NT, D])
    xT_hi, _ = place("xT_hi", [KD, T], F32R)
    xT_lo, _ = place("xT_lo", [KD, T], F32R)
    mix, _ = place("mix", [KD, D])
    lat, _ = place("lat", [KD, D])
    shared, _ = place("shared", [NT, D], at=here[0] - 2 * KD * D * 4)
    up_hi = [place(f"up_hi{s}", [2, KD, P], F32R)[0] for s in range(2)]
    up_lo = [place(f"up_lo{s}", [2, KD, P], F32R)[0] for s in range(2)]
    raw = [place(f"raw{s}", [2 * KD * P])[0] for s in range(3)]
    xn = [place(f"xn{u}", [D])[0] for u in range(2)]
    rb = [place(f"rb{u}", [D])[0] for u in range(2)]
    ln1, _ = place("ln1", [D])
    ln2, _ = place("ln2", [D])
    gamma, _ = place("gamma", [D])
    beta, _ = place("beta", [D])
    ident, _ = place("ident", [P])
    tri, _ = place("tri", [P])
    after, _ = place("after", [P])
    ones, _ = place("ones", [P])
    conv_w, _ = place("conv_w", [NCONV, TAPS])
    conv_b, _ = place("conv_b", [NCONV])
    heads_in, _ = place("heads_in", [3, NH])
    dtw, _ = place("dtw", [KD, NH])
    dtw_hi, _ = place("dtw_hi", [KD, NH], F32R)
    dtw_lo, _ = place("dtw_lo", [KD, NH], F32R)
    gw, _ = place("gw", [KD, 8])
    gw_hi, _ = place("gw_hi", [KD, 8], F32R)
    gw_lo, _ = place("gw_lo", [KD, 8], F32R)
    neg_A, _ = place("neg_A", [NH])
    dts = [place(f"dts{i}", [NT, NH])[0] for i in range(6)]
    dt_sp, _ = place("dt_sp", [NT, NH])
    decay, _ = place("decay", [NT, NH])
    to_end, _ = place("to_end", [NT, NH])
    stat, _ = place("stat", [BATCH, 6])
    mv, _ = place("mv", [BATCH, 2])
    ve, _ = place("ve", [BATCH])
    ry, _ = place("ry", [BATCH])
    rt, _ = place("rt", [BATCH])
    shift, _ = place("shift", [BATCH])
    top8, _ = place("top8", [NT, 8])
    route, _ = place("route", [NT])
    spare, _ = place("spare", [3])
    act_spare, _ = place("act_spare", [1])
    region = here[0]

    xBC, e = place("xBC", [NCONV, T + TAPS - 1], at=region)
    z, e_z = place("z", [NH, T], at=e)
    lat_exp, e2 = place("lat_exp", [2, 2 * P], at=e)
    lat_fc2, e2 = place("lat_fc2", [2, D], at=e2)
    lat_fc1, e2 = place("lat_fc1", [2, D], at=e2)
    lat_e2, e2 = place("lat_e2", [2, D], at=e2)
    assert e2 <= e_z
    acc = [None, None]
    acc[0], e = place("acc0", [T], at=e_z)
    acc[1], e = place("acc1", [T], at=e)
    wv, e = place("wv", [NKV, D], at=e)
    wps, e = place("wps", [NKV, D], at=e)
    wpraw = [None, None]
    wpraw[0], e = place("wpraw0", [2, D], at=e)
    wpraw[1], e_mix = place("wpraw1", [2, D], at=e)
    atri, e = place("atri", [NH, P], at=e_z)
    dtri, e = place("dtri", [NH, P], at=e)
    Xs, e = place("Xs", [NH, P], at=e)
    stXB, e = place("stXB", [2, P], at=e)
    XBt, e = place("XBt", [2, P], at=e)
    wo_hi, e = place("wo_hi", [KD, D], F32R, at=e)
    wo_lo, e = place("wo_lo", [KD, D], F32R, at=e)
    ssd = {}
    for name in ("eD", "eE", "att", "Cs", "xsD", "state", "y"):
        ssd[name], e = place(name, [NH, P], at=e)
    y_hi, e = place("y_hi", [NH, P], F32R, at=e)
    y_lo, e = place("y_lo", [NH, P], F32R, at=e)
    end = max(e, e_mix)
    eD, eE, att, Cs, xsD, state, y = (ssd[n] for n in ("eD", "eE", "att", "Cs", "xsD", "state", "y"))

    MAXT = max(b.tiles for b in blocks)
    hT, e = place("hT", [MAXT, T], at=region)
    wd_hi, e = place("wd_hi", [MAXT, D], F32R, at=e)
    wd_lo, e = place("wd_lo", [MAXT, D], F32R, at=e)
    st_hi, st_lo = [None, None], [None, None]
    for u in range(2):
        st_hi[u], e = place(f"st_hi{u}", [2 * KD, P], F32R, at=e)
        st_lo[u], e = place(f"st_lo{u}", [2 * KD, P], F32R, at=e)
    mix_hi, e = place("mix_hi", [KD, D], F32R, at=e)
    mix_lo, e = place("mix_lo", [KD, D], F32R, at=e)
    sg = [None, None]
    sg[0], e = place("sg0", [HALF], at=e)
    sg[1], e = place("sg1", [HALF], at=e)
    end = max(end, e)
    assert end <= nc.sbuf_usable_end, end

    bank = [nc.alloc_psum_tensor(f"bank{i}", [P, 512], F32) for i in range(8)]

    names = """small_in x_in0 x_in1 x_in2 x_in3 lat_in wv_in gains_in
        raw_in0 raw_in1 raw_in2 w_hi0 w_hi1 w_hi2 w_lo0 w_lo1 w_lo2 wp_in0 wp_in1 wp_summed
        consts pads small_split dve_step pool_step
        xn_done tr_mm xT_hi_done xT_lo_done xres_done
        e2_mm e2_done lat_mm lat_done p1_mm p1_done conv_done conv_silu dtT_mm dtT_done dt_mm dt_v dt_exp
        a_done end_mm end_exp to_end_done mix_mm mix_done
        st_xb atri_done dtri_done xbt_mm xbt_done g_mm d_mm e_mm expd_done expe_done
        edm_done cs_done xsd_done xs_done att_done y_mm s_mm y1_done y_done yhi_done ylo_done
        state_done o_mm
        gate_mm up_mm act_done h_done st_hi_done st_lo_done down_mm r_done
        mixhl_hi mixhl_lo gateT_mm gateT_done logits_mm route_done route_mm routed_done rstd_done both_done r2_done ht_done x_added out_done out_sent0 out_sent1""".split()
    S = {n: nc.alloc_semaphore(n) for n in names}

    def wait(e, name, value):
        if isinstance(value, int) and value <= 0:
            return
        e.wait_ge(S[name], value)

    def tok(i):
        return bass.ds(i * P, P)

    def heads(ap):
        return ap.unsqueeze(1).to_broadcast([P, NH, P])

    def per_head(ap):
        return ap.unsqueeze(2).to_broadcast([P, NH, P])

    block = nc.Block()
    with block:

        @block.sync
        def _(sp):
            def raw_load(slot, use, dst, src):
                wait(sp, f"w_lo{slot}", use)
                sp.dma_start(dst, src).then_inc(S[f"raw_in{slot}"], 16)

            def load_win(piece):
                raw_load(piece % 2, piece // 2, raw[piece % 2][:, :], t["w_in"][piece])

            def load_x(i):
                sp.dma_start(xres[:, 2 * i:2 * i + 2, :],
                             t["x"][2 * i * P:2 * (i + 1) * P, :].rearrange("(t p) d -> p t d", p=P)
                             ).then_inc(S[f"x_in{i}"], 16)

            def load_gain(i, gain):
                sp.dma_start(gain[:, :], t["gains"][i:i + 1, :].to_broadcast([P, D])).then_inc(S["gains_in"], 16)

            load_x(0)
            load_gain(0, ln1)
            load_x(1)
            load_win(0)
            load_x(2)
            load_x(3)
            for dst, name in ((dtw, "dtw"), (gw, "gw"), (conv_w, "conv_w"), (conv_b, "conv_b")):
                sp.dma_start(dst[:], t[name]).then_inc(S["small_in"], 16)
            sp.dma_start(heads_in[:, :, :], t["heads"].unsqueeze(0).to_broadcast([P, 3, NH])
                         ).then_inc(S["small_in"], 16)
            sp.dma_start(lat_exp[:, :, :], t["expert"]).then_inc(S["lat_in"], 16)
            sp.dma_start(lat_fc2[:, :, :], t["fc2"]).then_inc(S["lat_in"], 16)
            sp.dma_start(lat_fc1[:, :, :], t["fc1"]).then_inc(S["lat_in"], 16)
            load_win(1)
            load_win(2)
            load_win(3)
            for i, gain in enumerate((ln2, gamma, beta)):
                wait(sp, "xn_done", 1)
                load_gain(i + 1, gain)
            sp.dma_start(wv[:, :, :], t["wv"]).then_inc(S["wv_in"], 16)

            def load_wp(i):
                wait(sp, "wp_summed", i - 1)
                sp.dma_start(wpraw[i % 2][:, :, :], t["wp"][i]).then_inc(S[f"wp_in{i % 2}"], 16)

            for i in range(2 * NKV):
                load_wp(i)
                if i == 12:
                    load_win(4)
            def load_up(b, p, s):
                w = b.mats * KD * P
                use = b.use0[s] + p
                raw_load(s, use, raw[s][:, 0:w],
                         t["up_" + b.layer][bass.ds(b.first + 2 * p + s, 1)].rearrange("o p n -> p (o n)"))

            def load_down(b, p, n):
                raw_load(2, b.use0[2] + p, raw[2][:, 0:n * D].rearrange("p (k n) -> p k n", k=n),
                         t["down_" + b.layer][bass.ds(b.first + 2 * p, n)].rearrange("k p n -> p k n"))

            def pair(b, p, n, following):
                load_down(b, p, n)
                if following is not None:
                    nb, np_, nn = following
                    for s in range(nn):
                        load_up(nb, np_, s)

            def load_wout(i):
                raw_load(2, i, raw[2][:, :].rearrange("p (k n) -> p k n", k=2),
                         t["w_out"][2 * i:2 * i + 2].rearrange("k p n -> p k n"))

            load_wout(0)
            for s in range(2):
                load_up(blocks[0], 0, s)
            load_wout(1)
            for b in blocks:
                if b.attention:
                    continue
                full = sum(n == 2 for n in b.pairs[1:])
                if full:
                    with sp.Fori(0, full) as p:
                        pair(b, p, 2, (b, p + 1, 2))
                for p in range(full, len(b.pairs)):
                    if p + 1 < len(b.pairs):
                        pair(b, p, b.pairs[p], (b, p + 1, b.pairs[p + 1]))
                    elif b.next_up is not None:
                        pair(b, p, b.pairs[p], (b.next_up, 0, 2))
                    else:
                        pair(b, p, b.pairs[p], None)

            def store(p, u):
                wait(sp, "out_done", 2 * p + u + 1)
                sp.dma_start(t["out"][bass.ds((2 * p + u) * P, P), :], xn[u][:, :]
                             ).then_inc(S[f"out_sent{u}"], 16)

            with sp.Fori(0, NT // 2) as p:
                for u in range(2):
                    store(p, u)
            for u in range(2):
                sp.wait_ge(S[f"out_sent{u}"], 16 * NT // 2)

        @block.gpsimd
        def _(pool):
            def select(out, op, base, cm, step):
                pool.wait_ge(S["pool_step"], 1)
                pool.affine_select(out=out[:, :], in_=ones[:, :], compare_op=op, fill=0.0, base=base,
                                   pattern=[[step, P]], channel_multiplier=cm).then_inc(S["consts"], 1)

            pool.memset(ones[:, :], 1.0).then_inc(S["pool_step"], 1)
            select(ident, ALU.is_equal, 0, 1, -1)
            select(tri, ALU.is_ge, 0, -1, 1)
            select(after, ALU.is_gt, 0, 1, -1)
            pool.memset(xBC[:, :, 0:TAPS - 1], 0.0).then_inc(S["pads"], 1)

            def lo(slot, use, src, hi, dst):
                wait(pool, f"w_hi{slot}", use + 1)
                pool.tensor_tensor(dst, src, hi.bitcast(F32), ALU.subtract).then_inc(S[f"w_lo{slot}"], 1)

            def lo_win(piece):
                s = piece % 2
                lo(s, piece // 2, raw[s][:, :].rearrange("p (a k n) -> p a k n", a=2, k=KD),
                   up_hi[s][:, :, :, :], up_lo[s][:, :, :, :])

            def lo_up(b, p, s):
                w = b.mats * KD * P
                lo(s, b.use0[s] + p, raw[s][:, 0:w].rearrange("p (a k n) -> p a k n", a=b.mats, k=KD),
                   up_hi[s][:, 0:b.mats, :, :], up_lo[s][:, 0:b.mats, :, :])

            lo_win(0)
            lo_win(1)

            adds = [0]

            def sum_wp(i):
                g, half = i // 2, i % 2
                pool.wait_ge(S[f"wp_in{i % 2}"], 16 * (i // 2 + 1))
                for r in range(2):
                    if half == 0 and r == 0:
                        continue
                    if half == 0:
                        ins = pool.tensor_tensor(wps[:, g, :], wpraw[0][:, 0, :], wpraw[0][:, 1, :], ALU.add)
                    else:
                        pool.wait_ge(S["wp_summed"], adds[0])
                        if r == 1:
                            pool.wait_ge(S["pool_step"], 2 + g)
                        ins = pool.tensor_tensor(wps[:, g, :], wps[:, g, :], wpraw[1][:, r, :], ALU.add)
                    if half == 1 and r == 0:
                        ins.then_inc(S["pool_step"], 1)
                    else:
                        adds[0] += 1
                        ins.then_inc(S["wp_summed"], 1)

            for i in range(2 * NKV):
                sum_wp(i)
                if i == 9:
                    lo_win(2)
                if i == 12:
                    lo_win(3)
            lo_win(4)
            for s in range(2):
                lo_up(blocks[0], 0, s)

            def prepare(c):
                wait(pool, "g_mm", c)
                pool.tensor_copy(stXB[:, :, :], xBC[:, 0:2, bass.ds(c * P + TAPS - 1, P)]
                                 ).then_inc(S["st_xb"], 1)
                wait(pool, "e_mm", c)
                a = decay[:, bass.ds(c, 1), :].rearrange("p o h -> p (o h)")
                pool.tensor_tensor(atri[:, :, :], heads(tri[:, :]), per_head(a), ALU.mult
                                   ).then_inc(S["atri_done"], 1)
                wait(pool, "edm_done", c)
                dt = dt_sp[:, bass.ds(c, 1), :].rearrange("p o h -> p (o h)")
                pool.tensor_tensor(dtri[:, :, :], heads(tri[:, :]), per_head(dt), ALU.mult
                                   ).then_inc(S["dtri_done"], 1)

            def scale(c):
                at = bass.ds(c * P + TAPS - 1, P)
                wait(pool, "expd_done", c + 1)
                wait(pool, "dtri_done", c + 1)
                pool.tensor_tensor(eD[:, :, :], eD[:, :, :], dtri[:, :, :], ALU.mult).then_inc(S["edm_done"], 1)
                wait(pool, "expe_done", c + 1)
                wait(pool, "y1_done", c)
                pool.tensor_tensor(Cs[:, :, :], xBC[:, 2:6, at], eE[:, :, :], ALU.mult).then_inc(S["cs_done"], 1)
                xs = xBC[:, 0:1, at].rearrange("p o n -> p (o n)")
                pool.tensor_tensor(xsD[:, :, :], heads(xs), per_head(heads_in[:, 1, :]), ALU.mult
                                   ).then_inc(S["xsd_done"], 1)

            def add_x(c, u):
                wait(pool, "ht_done", c + 1)
                at = bass.ds(c, 1)
                pool.tensor_tensor(xres[:, at, :], xres[:, at, :], rb[u][:, :].unsqueeze(1), ALU.add
                                   ).then_inc(S["x_added"], 1)

            pool.wait_ge(S["a_done"], 1)
            pool.wait_ge(S["conv_silu"], NCONV)
            prepare(0)
            scale(0)
            prepare(1)
            scale(1)
            prepare(2)
            add_x(0, 0)
            with pool.Fori(1, NT // 2 - 1) as p:
                for u in range(2):
                    scale(2 * p + u)
                    prepare(2 * p + u + 1)
                    add_x(2 * p + u - 1, 1 - u)
            scale(NT - 2)
            prepare(NT - 1)
            add_x(NT - 3, 1)
            scale(NT - 1)
            add_x(NT - 2, 0)
            add_x(NT - 1, 1)

            def stage_lo(b, tile, u):
                if b.attention:
                    wait(pool, "down_mm", b.down0 + tile - 1)
                    wait(pool, "xT_lo_done", b.norm0 - NT + tile + 1)
                    ins = pool.tensor_copy(st_lo[u][:, 0:KD, :], xT_lo[:, :, tok(tile)].bitcast(F32))
                else:
                    wait(pool, "st_hi_done", b.down0 + tile + 1)
                    k = KD if b.moe else 0
                    ins = pool.tensor_tensor(st_lo[u][:, k:k + b.tiles, :], hT[:, 0:b.tiles, tok(tile)],
                                             st_hi[u][:, k:k + b.tiles, :].bitcast(F32), ALU.subtract)
                ins.then_inc(S["st_lo_done"], 1)

            def add_shared(b, tile, u):
                wait(pool, "routed_done", tile + 1)
                wait(pool, "r_done", b.down0)
                pool.tensor_tensor(rb[u][:, :].unsqueeze(1), rb[u][:, :].unsqueeze(1),
                                   shared[:, bass.ds(tile, 1), :], ALU.add).then_inc(S["both_done"], 1)

            def pair(b, p, n, following, last_pair=False):
                if last_pair:
                    for u in range(2):
                        stage_lo(b, u, u)
                if following is not None:
                    nb, np_, nn = following
                    for s in range(nn):
                        lo_up(nb, np_, s)

            for i, b in enumerate(blocks):
                if not b.attention:
                    full = sum(n == 2 for n in b.pairs[1:])
                    if full:
                        with pool.Fori(0, full) as p:
                            pair(b, p, 2, (b, p + 1, 2))
                    for p in range(full, len(b.pairs)):
                        if p + 1 < len(b.pairs):
                            pair(b, p, b.pairs[p], (b, p + 1, b.pairs[p + 1]))
                        elif b.next_up is not None:
                            pair(b, p, b.pairs[p], (b.next_up, 0, 2), last_pair=True)
                        else:
                            pair(b, p, b.pairs[p], None, last_pair=True)
                if b.attention:
                    for u in range(2):
                        stage_lo(b, u, u)
                with pool.Fori(0, NT // 2 - 1) as p:
                    for u in range(2):
                        stage_lo(b, 2 * p + u + 2, u)
                        if b.moe:
                            add_shared(b, 2 * p + u, u)
                for u in range(2):
                    if b.moe:
                        add_shared(b, NT - 2 + u, u)

        @block.scalar
        def _(act):
            def copy(dst, src, name):
                return act.activation(dst, src, ACT.Copy).then_inc(S[name], 1)

            def hi(slot, use, src, dst):
                wait(act, f"raw_in{slot}", 16 * (use + 1))
                copy(dst, src, f"w_hi{slot}")

            def hi_win(piece):
                s = piece % 2
                hi(s, piece // 2, raw[s][:, :].rearrange("p (a k n) -> p a k n", a=2, k=KD),
                   up_hi[s][:, :, :, :])

            def hi_up(b, p, s):
                w = b.mats * KD * P
                hi(s, b.use0[s] + p, raw[s][:, 0:w].rearrange("p (a k n) -> p a k n", a=b.mats, k=KD),
                   up_hi[s][:, 0:b.mats, :, :])

            def hi_down(b, p, n):
                hi(2, b.use0[2] + p, raw[2][:, 0:n * D].rearrange("p (k n) -> p k n", k=n),
                   wd_hi[:, bass.ds(2 * p, n), :])

            def evac_hi(j, tile, bk):
                wait(act, "tr_mm", j + 1)
                copy(xT_hi[:, :, tok(tile)], bank[bk][:, :].rearrange("p (k n) -> p k n", k=KD), "xT_hi_done")

            act.preload_act_table(ACT.Silu)
            hi_win(0)
            hi_win(1)

            def evac_p1(g):
                piece, half, f = g // 4, g // 2 % 2, g % 2
                i = 2 * piece + f
                wait(act, "p1_mm", g + 1)
                if i < NCONV:
                    copy(xBC[:, i, TAPS - 1 + half * HALF:TAPS - 1 + (half + 1) * HALF], bank[g % 4][:, :], "p1_done")
                else:
                    act.activation(z[:, i - NCONV, half * HALF:(half + 1) * HALF], bank[g % 4][:, :],
                                   ACT.Silu).then_inc(S["p1_done"], 1)

            def evac_lat(n):
                wait(act, "lat_mm", n + 1)
                copy(lat[:, n, :], bank[4 + n % 2][:, :], "lat_done")

            for j in range(4):
                evac_hi(j, j, 6 + j % 2)
            evac_p1(0)
            evac_p1(1)
            for n in range(2):
                wait(act, "e2_mm", n + 1)
                copy(lat_e2[:, n, :], bank[4 + n][:, :], "e2_done")
            for j in range(4, NT):
                evac_hi(j, j, 6 + j % 2)
            for n in range(KD):
                evac_lat(n)
            evac_p1(2)
            evac_p1(3)
            act.wait_ge(S["pads"], 1)

            def conv_silu(i):
                wait(act, "conv_done", i + 1)
                act.activation(xBC[:, i, TAPS - 1:], acc[i % 2][:, :], ACT.Silu, bias=conv_b[:, i:i + 1]
                               ).then_inc(S["conv_silu"], 1)

            act.wait_ge(S["small_in"], 16 * 5)
            for piece in range(5):
                if piece:
                    for g in range(4 * piece, 4 * piece + 4):
                        evac_p1(g)
                if piece == 1:
                    for half in range(2):
                        wait(act, "dtT_mm", half + 1)
                        copy(xn[half][0:NH, :], bank[4 + half][0:NH, :], "dtT_done")
                if piece + 2 < 5:
                    hi_win(piece + 2)
                if 1 <= piece <= 3:
                    conv_silu(2 * piece - 2)
                    conv_silu(2 * piece - 1)
            act.preload_act_table(ACT.Exp)
            act.activation(neg_A[:, :], heads_in[:, 0, :], ACT.Exp).then_inc(S["dt_exp"], 1)
            act.wait_ge(S["dt_v"], 1)
            act.activation(dts[2][:, :, :], dts[1][:, :, :], ACT.Exp, scale=-1.0).then_inc(S["dt_exp"], 1)
            for s in range(2):
                hi_up(blocks[0], 0, s)
            act.wait_ge(S["end_mm"], 1)
            act.activation(dts[3][:, :, :], bank[4][:, 32:64].rearrange("p (c h) -> p c h", c=NT), ACT.Exp
                           ).then_inc(S["end_exp"], 1)
            for n in range(KD):
                wait(act, "mix_mm", n + 1)
                copy(mix[:, n, :], bank[n][:, :], "mix_done")
            for i in range(2):
                hi(2, i, raw[2][:, :].rearrange("p (k n) -> p k n", k=2), wo_hi[:, 2 * i:2 * i + 2, :])

            def ssd_step(c, transposed):
                wait(act, "xbt_mm", c + 1)
                wait(act, "s_mm", c)
                copy(XBt[:, :, :], bank[6][:, 0:2 * P].rearrange("p (a n) -> p a n", a=2), "xbt_done")
                wait(act, "d_mm", c + 1)
                wait(act, "att_done", c)
                act.activation(eD[:, :, :], bank[1][:, :].rearrange("p (h n) -> p h n", h=NH), ACT.Exp
                               ).then_inc(S["expd_done"], 1)
                wait(act, "e_mm", c + 1)
                wait(act, "cs_done", c)
                wait(act, "state_done", c)
                act.activation(eE[:, :, :], bank[2][:, :].rearrange("p (h n) -> p h n", h=NH), ACT.Exp
                               ).then_inc(S["expe_done"], 1)
                if transposed:
                    evac_hi(NT + c - 4, c - 4, 7)
                wait(act, "y_done", c + 1)
                wait(act, "o_mm", c)
                copy(y_hi[:, :, :], y[:, :, :], "yhi_done")

            for c in range(4):
                ssd_step(c, False)
            with act.Fori(2, NT // 2) as p:
                for u in range(2):
                    ssd_step(2 * p + u, True)
            for i in (NT - 4, NT - 3):
                evac_hi(NT + i, i, 6 + i % 2)

            def activate(b, g, par):
                wait(act, "gate_mm" if b.mats == 2 else "up_mm", g + 1)
                wait(act, "h_done", g - 1)
                act.activation(sg[par][:, :], bank[2 * par][:, :], ACT.Relu if b.layer == "E" else ACT.Silu
                               ).then_inc(S["act_done"], 1)

            def stage_hi(b, tile, u):
                wait(act, "down_mm", b.down0 + tile - 1)
                k = 0
                ins = None
                if b.attention or b.moe:
                    if b.attention:
                        wait(act, "xT_lo_done", b.norm0 - NT + tile + 1)
                    ins = act.activation(st_hi[u][:, 0:KD, :], xT_hi[:, :, tok(tile)].bitcast(F32), ACT.Copy)
                    k = KD
                if b.moe:
                    act.activation(st_lo[u][:, 0:KD, :], xT_lo[:, :, tok(tile)].bitcast(F32), ACT.Copy)
                if not b.attention:
                    ins = act.activation(st_hi[u][:, k:k + b.tiles, :], hT[:, 0:b.tiles, tok(tile)], ACT.Copy)
                ins.then_inc(S["st_hi_done"], 1)

            def scales(b, q):
                wait(act, "rstd_done", b.rstd0 + q + 1)
                if not b.moe:
                    wait(act, "xres_done", b.kept0 + 2 * q)
                act.activation(act_spare[:, :], neg_A[:, 0:1], ACT.Copy)

            def normalize(b, q, u):
                tile = 2 * q + u
                src = xres[:, bass.ds(tile, 1), :].rearrange("p o n -> p (o n)")
                if b.moe:
                    wait(act, f"out_sent{u}", 16 * q)
                act.activation(xn[u][:, :], src, ACT.Identity, scale=ry[:, u:u + 1], bias=shift[:, u:u + 1]
                               ).then_inc(S["out_done" if b.moe else "xn_done"], 1)

            def keep_xn(tile, u):
                copy(xres[:, bass.ds(tile, 1), :], xn[u][:, :].unsqueeze(1), "xres_done")

            def pair(b, p, n, following, pending=None, last_pair=False):
                g = b.group0 + 4 * p
                normed = pending is not None and pending.layer != "SSD"
                if normed:
                    scales(pending, NT // 2 - 1)
                    for u in range(2):
                        normalize(pending, NT // 2 - 1, u)
                activate(b, g, 0)
                if n == 2 and b.mats == 1:
                    activate(b, g + 1, 1)
                if pending is not None:
                    for u in range(2):
                        evac_hi(pending.norm0 + NT - 2 + u, NT - 2 + u, 6 + u)
                    if normed:
                        for u in range(2):
                            keep_xn(NT - 2 + u, u)
                if n == 2 and b.mats == 2:
                    activate(b, g + 1, 1)
                hi_down(b, p, n)
                last = g + n
                activate(b, last, n % 2)
                if last_pair:
                    wait(act, "h_done", b.group1 - n)
                    for u in range(2):
                        stage_hi(b, u, u)
                if following is not None:
                    nb, np_, nn = following
                    wait(act, "up_mm", last + 1)
                    hi_up(nb, np_, 0)
                if n == 2:
                    activate(b, last + 1, 1)
                if following is not None and following[2] == 2:
                    if n == 2:
                        wait(act, "up_mm", last + 2)
                    hi_up(nb, np_, 1)

            act.preload_act_table(ACT.Silu)
            for b in blocks:
                pending = b.pending
                if not b.attention:
                    full = sum(n == 2 for n in b.pairs[1:])
                    first = 1 if b.fresh else 0
                    for p in range(first):
                        pair(b, p, b.pairs[p], (b, p + 1, b.pairs[p + 1]), pending)
                    if b.layer == "F" and b.final:
                        copy(mix_hi[:, :, :], mix[:, :, :], "mixhl_hi")
                    if b.layer == "E" and not b.final:
                        for half in range(2):
                            wait(act, "xres_done", pending.kept0 + NT)
                            wait(act, "gateT_mm", half + 1)
                            copy(xn[half][0:8, :], bank[4 + half][0:8, :], "gateT_done")
                        copy(mix_hi[:, :, :], lat[:, :, :], "mixhl_hi")
                    if full > first:
                        with act.Fori(first, full) as p:
                            pair(b, p, 2, (b, p + 1, 2))
                    for p in range(max(first, full), len(b.pairs)):
                        if p + 1 < len(b.pairs):
                            pair(b, p, b.pairs[p], (b, p + 1, b.pairs[p + 1]))
                        elif b.next_up is not None:
                            pair(b, p, b.pairs[p], (b.next_up, 0, 2), last_pair=True)
                        else:
                            pair(b, p, b.pairs[p], None, last_pair=True)
                    pending = None
                if b.attention:
                    for u in range(2):
                        stage_hi(b, u, u)

                def down_pair(p, stage, previous):
                    for u in range(2):
                        tile = 2 * p + u
                        if stage:
                            stage_hi(b, tile + 2, u)
                        if b.moe:
                            if u == 0:
                                wait(act, "route_done", 1)
                            wait(act, "route_mm", tile + 1)
                            wait(act, "r2_done", tile - 1)
                            act.activation(rb[u][:, :], bank[6 + u][:, :], ACT.Copy,
                                           scale=route[:, bass.ds(tile, 1)]).then_inc(S["routed_done"], 1)
                        if previous is not None and u == (1 if b.moe else 0):
                            a, q = previous
                            scales(a, q)
                            for v in range(2):
                                normalize(a, q, v)
                    if previous is not None and not b.moe:
                        for v in range(2):
                            evac_hi(a.norm0 + 2 * q + v, 2 * q + v, 6 + v)
                        for v in range(2):
                            keep_xn(2 * q + v, v)

                down_pair(0, True, (pending, NT // 2 - 1) if pending is not None else None)
                if not b.attention:
                    wait(act, "h_done", b.group1)
                if b.moe:
                    for p in range(1, NT // 2 - 1):
                        down_pair(p, True, (b, p - 1))
                else:
                    with act.Fori(1, NT // 2 - 1) as p:
                        down_pair(p, True, (b, p - 1) if b.final else None)
                down_pair(NT // 2 - 1, False, (b, NT // 2 - 2) if b.final else None)
                if b.moe:
                    wait(act, "rstd_done", b.rstd0 + NT // 2)
                    for u in range(2):
                        normalize(b, NT // 2 - 1, u)

        @block.vector
        def _(dve):
            base = [0]
            n = [0]

            def link(ins, meanwhile=None):
                n[0] += 1
                ins.then_inc(S["dve_step"], 1)
                if meanwhile is not None:
                    meanwhile()
                dve.wait_ge(S["dve_step"], base[0] + n[0])

            def loop(start, stop, per, body):
                b0 = base[0] + n[0]
                with dve.Fori(start, stop) as i:
                    base[0], n[0] = b0 + (i - start) * per, 0
                    body(i)
                    assert n[0] == per, (n[0], per)
                base[0], n[0] = b0 + (stop - start) * per, 0

            def alone(i):
                dve.memset(spare[:, i:i + 1], 0.0)

            BEGIN_STEPS = {"layer": 3, "rms": 5}
            FINISH_STEPS = 1 + 3 * NEWTON

            def begin_norm(kind, srcs, ready=None, meanwhile=()):
                m, fill = len(srcs), iter(meanwhile)
                for i, src in enumerate(srcs):
                    if ready is not None:
                        ready(i)
                    ins = dve.bn_stats(stat[:, i, :], src)
                link(ins, next(fill, None))
                alone(2)
                for i in range(m):
                    ins = dve.bn_aggr(mv[:, i, :], stat[:, i, :])
                link(ins, next(fill, None))
                mean, under = mv[:, 0:m, 0], mv[:, 0:m, 1]
                if kind == "rms":
                    link(dve.tensor_tensor(rt[:, 0:m], mean, mean, ALU.mult), next(fill, None))
                    link(dve.tensor_tensor(rt[:, 0:m], rt[:, 0:m], under, ALU.add), next(fill, None))
                    under = rt[:, 0:m]
                link(dve.tensor_scalar(ve[:, 0:m], under, EPS, 0.5, ALU.add, ALU.mult), next(fill, None))

            def finish_norm(kind, m, meanwhile=()):
                fill = iter(meanwhile)
                y, v, w = ry[:, 0:m], ve[:, 0:m], rt[:, 0:m]
                link(dve.tensor_scalar(y.bitcast(I32), v.bitcast(I32), -0.5, RSQRT_GUESS, ALU.mult, ALU.add),
                     next(fill, None))
                for _ in range(NEWTON):
                    link(dve.tensor_tensor(w, y, y, ALU.mult), next(fill, None))
                    link(dve.tensor_tensor(w, w, v, ALU.mult), next(fill, None))
                    link(dve.scalar_tensor_tensor(out=y, in0=w, scalar=1.5, in1=y, op0=ALU.subtract, op1=ALU.mult),
                         next(fill, None))
                if kind == "layer":
                    dve.scalar_tensor_tensor(out=shift[:, 0:m], in0=mv[:, 0:m, 0], scalar=-1.0, in1=y,
                                             op0=ALU.mult, op1=ALU.mult).then_inc(S["rstd_done"], 1)

            def evac_lo(j, tile, bk):
                wait(dve, "xT_hi_done", j + 1)
                dve.tensor_tensor(xT_lo[:, :, tok(tile)], bank[bk][:, :].rearrange("p (k n) -> p k n", k=KD),
                                  xT_hi[:, :, tok(tile)].bitcast(F32), ALU.subtract
                                  ).then_inc(S["xT_lo_done"], 1)

            dve.wait_ge(S["gains_in"], 16)
            def scaled(src, i, u, gain, tr):
                wait(dve, "tr_mm", tr)
                dve.scalar_tensor_tensor(out=xn[u][:, :], in0=src, scalar=ry[:, i:i + 1], in1=gain[:, :],
                                         op0=ALU.mult, op1=ALU.mult).then_inc(S["xn_done"], 1)

            for first in (0, BATCH):
                def loaded(i):
                    if i % 2 == 0:
                        dve.wait_ge(S[f"x_in{(first + i) // 2}"], 16)
                begin_norm("rms", [xres[:, first + i, :] for i in range(BATCH)], loaded)
                finish_norm("rms", BATCH)
                for i in range(BATCH):
                    j = first + i
                    scaled(xres[:, j, :], i, j % 2, ln1, j - 1)
                    if i >= 2:
                        evac_lo(j - 2, j - 2, 6 + j % 2)
                for j in (first + 2, first + 3):
                    evac_lo(j, j, 6 + j % 2)

            dve.wait_ge(S["small_in"], 16 * 5)
            for w, w_hi, w_lo in ((dtw, dtw_hi, dtw_lo), (gw, gw_hi, gw_lo)):
                link(dve.tensor_copy(w_hi[:, :, :], w[:, :, :]))
                dve.tensor_tensor(w_lo[:, :, :], w[:, :, :], w_hi[:, :, :].bitcast(F32), ALU.subtract
                                  ).then_inc(S["small_split"], 1)

            for i in range(NCONV):
                if i % 2 == 0:
                    dve.wait_ge(S["p1_done"], 2 * i + 4)
                if i == 0:
                    dve.wait_ge(S["pads"], 1)
                wait(dve, "conv_silu", i - 1)
                a = acc[i % 2]
                link(dve.tensor_scalar(a[:, :], xBC[:, i, TAPS - 1:], conv_w[:, i, TAPS - 1:TAPS], None, ALU.mult))
                for k in range(TAPS - 2, -1, -1):
                    ins = dve.scalar_tensor_tensor(out=a[:, :], in0=xBC[:, i, k:k + T], scalar=conv_w[:, i, k:k + 1],
                                                   in1=a[:, :], op0=ALU.mult, op1=ALU.add)
                    if k:
                        link(ins)
                    else:
                        ins.then_inc(S["conv_done"], 1)

            v, av, e_, s_, s2, pw = dts
            tail = dts[3]
            dve.wait_ge(S["dt_mm"], 1)
            link(dve.tensor_tensor(v[:, :, :], bank[6][:, 0:32].rearrange("p (c h) -> p c h", c=NT),
                                   heads_in[:, 2, :].unsqueeze(1).to_broadcast([P, NT, NH]), ALU.add))
            dve.scalar_tensor_tensor(out=av[:, :, :], in0=v[:, :, :], scalar=-1.0, in1=v[:, :, :],
                                     op0=ALU.mult, op1=ALU.max).then_inc(S["dt_v"], 1)
            dve.wait_ge(S["dt_exp"], 2)
            link(dve.tensor_scalar(s_[:, :, :], e_[:, :, :], 2.0, None, ALU.add))
            link(dve.reciprocal(s2[:, :, :], s_[:, :, :]))
            link(dve.tensor_tensor(s_[:, :, :], e_[:, :, :], s2[:, :, :], ALU.mult))
            link(dve.tensor_tensor(s2[:, :, :], s_[:, :, :], s_[:, :, :], ALU.mult))
            link(dve.tensor_scalar(pw[:, :, :], s2[:, :, :], 1.0 / 15, None, ALU.mult))
            for m in (13, 11, 9, 7, 5, 3):
                link(dve.scalar_tensor_tensor(out=pw[:, :, :], in0=pw[:, :, :], scalar=1.0 / m, in1=s2[:, :, :],
                                              op0=ALU.add, op1=ALU.mult))
            link(dve.scalar_tensor_tensor(out=pw[:, :, :], in0=pw[:, :, :], scalar=1.0, in1=s_[:, :, :],
                                          op0=ALU.add, op1=ALU.mult))
            link(dve.tensor_scalar(v[:, :, :], v[:, :, :], 0.0, None, ALU.max))
            link(dve.scalar_tensor_tensor(out=dt_sp[:, :, :], in0=pw[:, :, :], scalar=2.0, in1=v[:, :, :],
                                          op0=ALU.mult, op1=ALU.add))
            dve.scalar_tensor_tensor(out=decay[:, :, :], in0=dt_sp[:, :, :], scalar=-1.0,
                                     in1=neg_A[:, :].unsqueeze(1).to_broadcast([P, NT, NH]),
                                     op0=ALU.mult, op1=ALU.mult).then_inc(S["a_done"], 1)
            for i in range(2):
                wait(dve, "w_hi2", i + 1)
                dve.tensor_tensor(wo_lo[:, 2 * i:2 * i + 2, :], raw[2][:, :].rearrange("p (k n) -> p k n", k=2),
                                  wo_hi[:, 2 * i:2 * i + 2, :].bitcast(F32), ALU.subtract).then_inc(S["w_lo2"], 1)
            dve.wait_ge(S["end_exp"], 1)
            link(dve.tensor_tensor(to_end[:, :, :], tail[:, :, :], dt_sp[:, :, :], ALU.mult))

            def add_h(c, u):
                wait(dve, "o_mm", c + 1)
                wait(dve, "x_added", c - 1)
                wait(dve, "xn_done", NT + c - 1)
                at = bass.ds(c, 1)
                dve.tensor_tensor(rb[u][:, :].unsqueeze(1), bank[5][:, :].unsqueeze(1), xres[:, at, :], ALU.add
                                  ).then_inc(S["ht_done"], 1)

            def begin_pair(c, meanwhile=()):
                wait(dve, "ht_done", c + 2)
                begin_norm("rms", [rb[u][:, :] for u in range(2)], meanwhile=meanwhile)

            def finish_pair(c, meanwhile=()):
                finish_norm("rms", 2, meanwhile)
                for u in range(2):
                    scaled(rb[u][:, :], u, u, ln2, NT + c + u - 1)

            def ssd_step(c, u, first=False, normed=True, transposed=True):
                wait(dve, "xbt_done", c + 1)
                wait(dve, "s_mm", c)
                w = to_end[:, bass.ds(c, 1), :].rearrange("p o h -> p (o h)")
                dve.tensor_tensor(Xs[:, :, :], heads(XBt[:, 0, :]), per_head(w), ALU.mult).then_inc(S["xs_done"], 1)
                wait(dve, "g_mm", c + 1)
                wait(dve, "edm_done", c + 1)
                wait(dve, "y_mm", c)
                dve.tensor_tensor(att[:, :, :], bank[0][:, :].rearrange("p (h n) -> p h n", h=NH), eD[:, :, :],
                                  ALU.mult).then_inc(S["att_done"], 1)
                if transposed:
                    evac_lo(NT + c - 4, c - 4, 7)
                if normed and u == 1:
                    finish_pair(c - 3)
                if not first:
                    add_h(c - 1, 1 - u)
                if normed and u == 0:
                    begin_pair(c - 2)
                wait(dve, "y_mm", c + 1)
                wait(dve, "xsd_done", c + 1)
                dve.tensor_tensor(y[:, :, :], bank[3][:, :].rearrange("p (h n) -> p h n", h=NH), xsD[:, :, :],
                                  ALU.add).then_inc(S["y1_done"], 1)
                wait(dve, "y1_done", c + 1)
                dve.tensor_tensor(y[:, :, :], y[:, :, :], z[:, :, tok(c)], ALU.mult).then_inc(S["y_done"], 1)
                wait(dve, "s_mm", c + 1)
                if first:
                    dve.tensor_copy(state[:, :, :], bank[4][:, :].rearrange("p (h n) -> p h n", h=NH)
                                    ).then_inc(S["state_done"], 1)
                else:
                    wait(dve, "expe_done", c + 1)
                    for h in range(NH):
                        ins = dve.scalar_tensor_tensor(out=state[:, h, :], in0=state[:, h, :],
                                                       scalar=eE[:, h, P - 1:P], in1=bank[4][:, h * P:(h + 1) * P],
                                                       op0=ALU.mult, op1=ALU.add)
                    ins.then_inc(S["state_done"], 1)
                wait(dve, "yhi_done", c + 1)
                dve.tensor_tensor(y_lo[:, :, :], y[:, :, :], y_hi[:, :, :].bitcast(F32), ALU.subtract
                                  ).then_inc(S["ylo_done"], 1)

            dve.wait_ge(S["conv_silu"], NCONV)
            dve.wait_ge(S["gains_in"], 64)
            ssd_step(0, 0, first=True, normed=False, transposed=False)
            ssd_step(1, 1, normed=False, transposed=False)
            for c in (2, 3):
                ssd_step(c, c % 2, transposed=False)
            loop(2, NT // 2, BEGIN_STEPS["rms"] + FINISH_STEPS,
                 lambda p: [ssd_step(2 * p + u, u) for u in range(2)])
            add_h(NT - 1, 1)
            begin_pair(NT - 2)
            finish_pair(NT - 2, [lambda i=i: evac_lo(NT + i, i, 6 + i % 2) for i in (NT - 4, NT - 3)])

            def product(b, g, par, tile, half):
                wait(dve, "act_done", g + 1)
                wait(dve, "up_mm", g + 1)
                src = bank[2 * par] if b.layer == "E" else bank[2 * par + 1]
                dve.tensor_tensor(hT[:, bass.ds(tile, 1), half * HALF:(half + 1) * HALF], sg[par][:, :].unsqueeze(1),
                                  src[:, :].unsqueeze(1), ALU.mult).then_inc(S["h_done"], 1)

            def lo_down(b, p, n):
                wait(dve, "w_hi2", b.use0[2] + p + 1)
                at = bass.ds(2 * p, n)
                dve.tensor_tensor(wd_lo[:, at, :], raw[2][:, 0:n * D].rearrange("p (k n) -> p k n", k=n),
                                  wd_hi[:, at, :].bitcast(F32), ALU.subtract).then_inc(S["w_lo2"], 1)

            def split_mix(src):
                wait(dve, "mixhl_hi", 1 if src is mix else 2)
                dve.tensor_tensor(mix_lo[:, :, :], src[:, :, :], mix_hi[:, :, :].bitcast(F32),
                                  ALU.subtract).then_inc(S["mixhl_lo"], 1)

            def evac_pending(pending):
                for u in range(2):
                    evac_lo(pending.norm0 + NT - 2 + u, NT - 2 + u, 6 + u)

            def pair(b, p, n, pending=None):
                g = b.group0 + 4 * p
                product(b, g, 0, 2 * p, 0)
                if n == 2 and b.mats == 1:
                    product(b, g + 1, 1, 2 * p + 1, 0)
                if pending is not None:
                    evac_pending(pending)
                if n == 2 and b.mats == 2:
                    product(b, g + 1, 1, 2 * p + 1, 0)
                lo_down(b, p, n)
                product(b, g + n, n % 2, 2 * p, 1)
                if n == 2:
                    product(b, g + n + 1, 1, 2 * p + 1, 1)

            def kept(b, tile):
                if b.fresh and b.pending.layer == "SSD":
                    wait(dve, "x_added", tile + 1)
                elif b.fresh:
                    wait(dve, "xres_done", b.pending.kept0 + tile + 1)

            def down_mid(b, tile, u):
                wait(dve, "down_mm", b.down0 + tile + 1)
                kept(b, tile)
                at = bass.ds(tile, 1)
                if b.layer == "E":
                    dve.tensor_tensor(xres[:, at, :], xres[:, at, :], beta[:, :].unsqueeze(1), ALU.add)
                    dve.tensor_copy(shared[:, at, :], bank[4 + u][:, :].unsqueeze(1)).then_inc(S["r_done"], 1)
                else:
                    dve.tensor_tensor(xres[:, at, :], xres[:, at, :], bank[4 + u][:, :].unsqueeze(1), ALU.add
                                      ).then_inc(S["r_done"], 1)

            def tiles(p):
                return [xres[:, bass.ds(2 * p + u, 1), :].rearrange("p o n -> p (o n)") for u in range(2)]

            def down_norm(b, p, meanwhile=()):
                def add(u):
                    tile = 2 * p + u
                    wait(dve, "down_mm", b.down0 + tile + 1)
                    kept(b, tile)
                    at = bass.ds(tile, 1)
                    dve.tensor_tensor(xres[:, at, :], xres[:, at, :], bank[4 + u][:, :].unsqueeze(1), ALU.add
                                      ).then_inc(S["r_done"], 1)
                    wait(dve, "r_done", b.down0 + tile + 1)
                    alone(u)
                begin_norm("layer", tiles(p), add, meanwhile[:1])
                wait(dve, "xn_done", b.norm0 + 2 * p)
                finish_norm("layer", 2, meanwhile[1:])

            def down_out(b, p):
                def add(u):
                    tile = 2 * p + u
                    wait(dve, "down_mm", b.down0 + tile + 1)
                    wait(dve, "both_done", tile + 1)
                    dve.tensor_tensor(rb[u][:, :], bank[4 + u][:, :], rb[u][:, :], ALU.add).then_inc(S["r_done"], 1)
                    wait(dve, "r_done", b.down0 + tile + 1)
                begin_norm("layer", [rb[u][:, :] for u in range(2)], add)
                wait(dve, "out_done", 2 * p)

                def centred(u):
                    dve.scalar_tensor_tensor(out=rb[u][:, :], in0=rb[u][:, :], scalar=mv[:, u, 0:1],
                                             in1=gamma[:, :], op0=ALU.subtract, op1=ALU.mult)
                finish_norm("rms", 2, [lambda: centred(0), lambda: centred(1)])

                def outer(u):
                    dve.scalar_tensor_tensor(out=tiles(p)[u], in0=rb[u][:, :], scalar=ry[:, u:u + 1],
                                             in1=tiles(p)[u], op0=ALU.mult, op1=ALU.add).then_inc(S["r2_done"], 1)
                for u in range(2):
                    outer(u)
                wait(dve, "r2_done", 2 * p + 2)
                alone(0)
                begin_norm("layer", tiles(p))
                finish_norm("layer", 2)

            def up_phase(b):
                full = sum(k == 2 for k in b.pairs)
                first = 1 if b.fresh else 0
                if first:
                    pair(b, 0, b.pairs[0], b.pending)
                if b.layer == "F" and b.final:
                    split_mix(mix)
                if b.layer == "E" and not b.final:
                    split_mix(lat)
                if full > first:
                    loop(first, full, 0, lambda p: pair(b, p, 2))
                if b.pairs[-1] == 1:
                    pair(b, len(b.pairs) - 1, 1)

            def routing():
                wait(dve, "logits_mm", 1)
                for tile in range(NT):
                    ins = dve.max(top8[:, tile, :], bank[6][:, 8 * tile:8 * tile + 8])
                link(ins)
                dve.tensor_tensor(route[:, :], top8[:, :, 0], top8[:, :, 1], ALU.add).then_inc(S["route_done"], 1)

            LAYER = BEGIN_STEPS["layer"] + FINISH_STEPS
            for b in blocks:
                if not b.attention:
                    up_phase(b)
                if b.layer == "E" and not b.final:
                    routing()
                if not b.final:
                    loop(0, NT // 2, 0, lambda p: [down_mid(b, 2 * p + u, u) for u in range(2)])
                elif b.moe:
                    down_out(b, 0)
                    loop(1, NT // 2, BEGIN_STEPS["layer"] + FINISH_STEPS + LAYER, lambda p: down_out(b, p))
                else:
                    def evacs(a, q):
                        return [lambda u=u: evac_lo(a.norm0 + 2 * q + u, 2 * q + u, 6 + u) for u in range(2)]
                    down_norm(b, 0, evacs(b.pending, NT // 2 - 1) if b.fresh else ())
                    loop(1, NT // 2, LAYER, lambda p: down_norm(b, p, evacs(b, p - 1)))

        @block.tensor
        def _(pe):
            def mm3(out, s_hi, s_lo, m_hi, m_lo, first, last):
                pe.matmul(out, s_hi, m_hi, start=first, stop=False)
                pe.matmul(out, s_hi, m_lo, start=False, stop=False)
                return pe.matmul(out, s_lo, m_hi, start=False, stop=last)

            def turn(j, u, bk, evacuated=None):
                wait(pe, "xn_done", j + 1)
                wait(pe, "xT_lo_done", j - 1 if evacuated is None else evacuated)
                for k in range(KD):
                    ins = pe.transpose(bank[bk][:, k * P:(k + 1) * P], xn[u][:, k * P:(k + 1) * P], ident[:, :])
                ins.then_inc(S["tr_mm"], 1)

            def turn_pair(a, q):
                for u in range(2):
                    turn(a.norm0 + 2 * q + u, u, 6 + u)

            def turn0(j):
                turn(j, j % 2, 6 + j % 2)

            def p1_group(g):
                piece, half, f = g // 4, g // 2 % 2, g % 2
                s = piece % 2
                wait(pe, f"w_lo{s}", piece // 2 + 1)
                if g < 4:
                    wait(pe, "xT_lo_done", NT // 2 if half == 0 else NT)
                wait(pe, "p1_done", g - 3)
                for k in range(KD):
                    at = slice(half * HALF, (half + 1) * HALF)
                    ins = mm3(bank[g % 4][:, :], up_hi[s][:, f, k, :], up_lo[s][:, f, k, :],
                              xT_hi[:, k, at], xT_lo[:, k, at], k == 0, k == KD - 1)
                ins.then_inc(S["p1_mm"], 1)

            def lat_group(n):
                wait(pe, "lat_done", n - 1)
                for k in range(2):
                    ins = pe.matmul(bank[4 + n % 2][:, :], lat_fc1[:, k, n * P:(n + 1) * P], lat_e2[:, k, :],
                                    start=(k == 0), stop=(k == 1))
                ins.then_inc(S["lat_mm"], 1)

            pe.wait_ge(S["consts"], 3)
            for j in range(4):
                turn0(j)
            p1_group(0)
            p1_group(1)
            pe.wait_ge(S["lat_in"], 48)
            for n in range(2):
                for k in range(2):
                    ins = pe.matmul(bank[4 + n][:, :], lat_exp[:, k, n * P:(n + 1) * P], lat_fc2[:, k, :],
                                    start=(k == 0), stop=(k == 1))
                ins.then_inc(S["e2_mm"], 1)
            for j in range(4, NT):
                turn0(j)
            pe.wait_ge(S["e2_done"], 2)
            for n in range(KD):
                lat_group(n)
            for g in range(2, 8):
                p1_group(g)

            def thin(w_hi, w_lo, cols, name):
                for half in range(2):
                    at = slice(half * HALF, (half + 1) * HALF)
                    for k in range(KD):
                        ins = mm3(bank[4 + half][0:cols, :], w_hi[:, k, :], w_lo[:, k, :],
                                  xT_hi[:, k, at], xT_lo[:, k, at], k == 0, k == KD - 1)
                    ins.then_inc(S[name], 1)

            def thin_turn(cols, name):
                for tile in range(NT):
                    half, at = tile // 4, tile % 4 * P
                    ins = pe.transpose(bank[6][:, tile * cols:(tile + 1) * cols], xn[half][0:cols, at:at + P],
                                       ident[0:cols, 0:cols])
                ins.then_inc(S[name], 1)

            pe.wait_ge(S["small_split"], 2)
            pe.wait_ge(S["lat_done"], KD)
            thin(dtw_hi, dtw_lo, NH, "dtT_mm")
            for g in range(8, 12):
                p1_group(g)
            pe.wait_ge(S["dtT_done"], 2)
            thin_turn(NH, "dt_mm")
            for g in range(12, 20):
                p1_group(g)
            pe.wait_ge(S["p1_done"], 20)
            pe.wait_ge(S["wv_in"], 16)
            for g in range(NKV):
                if g == NKV // 2:
                    pe.wait_ge(S["a_done"], 1)
                    pe.matmul(bank[4][:, 32:64], after[:, :], decay[:, :, :].rearrange("p c h -> p (c h)"),
                              start=True, stop=True).then_inc(S["end_mm"], 1)
                pe.wait_ge(S["wp_summed"], 2 * (g + 1))
                for n in range(KD):
                    ins = pe.matmul(bank[n][:, :], wv[:, g, n * P:(n + 1) * P], wps[:, g, :],
                                    start=(g == 0), stop=(g == NKV - 1))
                    if g == NKV - 1:
                        ins.then_inc(S["mix_mm"], 1)
            pe.wait_ge(S["mix_done"], KD)
            pe.wait_ge(S["end_exp"], 1)

            def scores(c):
                wait(pe, "st_xb", c + 1)
                wait(pe, "xbt_done", c)
                for i in range(2):
                    ins = pe.transpose(bank[6][:, i * P:(i + 1) * P], stXB[:, i, :], ident[:, :])
                ins.then_inc(S["xbt_mm"], 1)
                wait(pe, "att_done", c)
                pe.matmul(bank[0][:, :].rearrange("p (h n) -> p h n", h=NH), stXB[:, 1, :],
                          xBC[:, 2:6, bass.ds(c * P + TAPS - 1, P)], start=True, stop=True
                          ).then_inc(S["g_mm"], 1)
                wait(pe, "atri_done", c + 1)
                wait(pe, "expd_done", c)
                flat = atri[:, :, :].rearrange("p h n -> p (h n)")
                pe.matmul(bank[1][:, :], after[:, :], flat, start=True, stop=True).then_inc(S["d_mm"], 1)
                wait(pe, "expe_done", c)
                pe.matmul(bank[2][:, :], ones[:, :], flat, start=True, stop=True).then_inc(S["e_mm"], 1)

            def mixed(c, first):
                wait(pe, "att_done", c + 1)
                wait(pe, "y1_done", c)
                pe_ins = pe.matmul(bank[3][:, :], XBt[:, 0, :], att[:, :, :].rearrange("p h n -> p (h n)"),
                                   start=True, stop=first)
                if not first:
                    wait(pe, "cs_done", c + 1)
                    wait(pe, "state_done", c)
                    for h in range(NH):
                        pe_ins = pe.matmul(bank[3][:, h * P:(h + 1) * P], state[:, h, :], Cs[:, h, :],
                                           start=False, stop=(h == NH - 1))
                pe_ins.then_inc(S["y_mm"], 1)
                wait(pe, "xs_done", c + 1)
                wait(pe, "state_done", c)
                pe.matmul(bank[4][:, :], XBt[:, 1, :], Xs[:, :, :].rearrange("p h n -> p (h n)"),
                          start=True, stop=True).then_inc(S["s_mm"], 1)

            def project(c):
                wait(pe, "ylo_done", c + 1)
                wait(pe, "ht_done", c)
                for k in range(KD):
                    ins = mm3(bank[5][:, :], y_hi[:, k, :], y_lo[:, k, :], wo_hi[:, k, :], wo_lo[:, k, :],
                              k == 0, k == KD - 1)
                ins.then_inc(S["o_mm"], 1)

            def ssd_step(c, projected=True, transposed=True):
                scores(c)
                if transposed:
                    turn(NT + c - 4, u_of[0], 7, NT + c - 4)
                if projected:
                    project(c - 1)
                mixed(c, not projected)

            u_of = [0]
            ssd_step(0, projected=False, transposed=False)
            scores(1)
            pe.wait_ge(S["w_lo2"], 2)
            project(0)
            mixed(1, False)
            for c in (2, 3):
                ssd_step(c, transposed=False)
            with pe.Fori(2, NT // 2) as p:
                for u in range(2):
                    u_of[0] = u
                    ssd_step(2 * p + u)
            project(NT - 1)
            turn(2 * NT - 4, 0, 6, 0)
            turn(2 * NT - 3, 1, 7, 2 * NT - 4)

            def group(b, g, par, s, half):
                wait(pe, "h_done", g - 1)
                at = slice(half * HALF, (half + 1) * HALF)
                for m in range(b.mats):
                    for k in range(KD):
                        ins = mm3(bank[2 * par + m][:, :], up_hi[s][:, m, k, :], up_lo[s][:, m, k, :],
                                  xT_hi[:, k, at], xT_lo[:, k, at], k == 0, k == KD - 1)
                    if m == 0 and b.mats == 2:
                        ins.then_inc(S["gate_mm"], 1)
                ins.then_inc(S["up_mm"], 1)

            def pair(b, p, n, pending=None):
                g = b.group0 + 4 * p
                if pending is not None:
                    wait(pe, "xT_lo_done", b.norm0 - NT // 2)
                wait(pe, "w_lo0", b.use0[0] + p + 1)
                group(b, g, 0, 0, 0)
                if pending is not None and b.mats == 2:
                    turn_pair(pending, NT // 2 - 1)
                if n == 2:
                    wait(pe, "w_lo1", b.use0[1] + p + 1)
                    group(b, g + 1, 1, 1, 0)
                if pending is not None and b.mats == 1:
                    turn_pair(pending, NT // 2 - 1)
                if pending is not None:
                    wait(pe, "xT_lo_done", b.norm0)
                group(b, g + n, n % 2, 0, 1)
                if n == 2:
                    group(b, g + n + 1, 1, 1, 1)

            def down(b, tile, u):
                wait(pe, "st_hi_done", b.down0 + tile + 1)
                wait(pe, "st_lo_done", b.down0 + tile + 1)
                k0 = KD if b.moe else 0
                if b.moe:
                    wait(pe, "routed_done", tile - 1)
                    for k in range(KD):
                        ins = mm3(bank[6 + u][:, :], st_hi[u][:, k, :], st_lo[u][:, k, :],
                                  mix_hi[:, k, :], mix_lo[:, k, :], k == 0, k == KD - 1)
                    ins.then_inc(S["route_mm"], 1)
                wait(pe, "r_done", b.down0 + tile - 1)
                n = KD if b.attention else b.tiles
                w_hi, w_lo = (mix_hi, mix_lo) if b.attention else (wd_hi, wd_lo)
                for k in range(n):
                    ins = mm3(bank[4 + u][:, :], st_hi[u][:, k0 + k, :], st_lo[u][:, k0 + k, :],
                              w_hi[:, k, :], w_lo[:, k, :], k == 0, k == n - 1)
                ins.then_inc(S["down_mm"], 1)

            for b in blocks:
                if not b.attention:
                    full = sum(k == 2 for k in b.pairs)
                    first = 1 if b.fresh else 0
                    if first:
                        pair(b, 0, b.pairs[0], b.pending)
                    if b.layer == "E" and not b.final:
                        wait(pe, "r_done", b.down0)
                        thin(gw_hi, gw_lo, 8, "gateT_mm")
                    if full > first:
                        with pe.Fori(first, full) as p:
                            pair(b, p, 2)
                    if b.pairs[-1] == 1:
                        pair(b, len(b.pairs) - 1, 1)
                    if b.layer == "E" and not b.final:
                        wait(pe, "gateT_done", 2)
                        thin_turn(8, "logits_mm")
                    wait(pe, "w_lo2", b.use0[2] + len(b.pairs))
                else:
                    wait(pe, "mixhl_lo", 1)
                if b.moe:
                    wait(pe, "mixhl_lo", 2)
                    wait(pe, "route_done", 1)
                keep = b.final and not b.moe

                def down_pair(p, previous):
                    for u in range(2):
                        down(b, 2 * p + u, u)
                    if previous is not None:
                        turn_pair(*previous)

                down_pair(0, (b.pending, NT // 2 - 1) if b.attention else None)
                with pe.Fori(1, NT // 2) as p:
                    down_pair(p, (b, p - 1) if keep else None)


def lay_out(a):
    import numpy as np
    f = {k: np.asarray(v) for k, v in a.items()}
    cont = np.ascontiguousarray

    def up(*mats):
        o, i = mats[0].shape
        m = np.stack([w.reshape(o // P, P, i // P, P).transpose(0, 3, 2, 1) for w in mats], axis=2)
        return cont(m.reshape(o // P, P, -1))

    def rows(w):
        return w.reshape(w.shape[0] // P, P, -1)

    def by_partition(w):
        return cont(rows(w).transpose(1, 0, 2))

    def pad_rows(w):
        return np.concatenate([w, np.zeros((-w.shape[0] % P, w.shape[1]), w.dtype)])

    w_in = f["L0_attn_w_in"]
    d_inner, d_xb = D, P
    x_b_c = w_in[d_inner:2 * d_inner + 2 * d_xb]
    feat = np.concatenate([x_b_c, w_in[:d_inner]])
    tiles = feat.reshape(10, P, KD, P).transpose(0, 3, 2, 1)
    out = {
        "x": f["L0_attn_hidden_states"][0],
        "w_in": cont(tiles.reshape(5, 2, P, KD * P).transpose(0, 2, 1, 3).reshape(5, P, 2 * KD * P)),
        "dtw": by_partition(w_in[2 * d_inner + 2 * d_xb:].T),
        "conv_w": cont(f["L0_attn_conv_w"].reshape(NCONV, P, TAPS).transpose(1, 0, 2)),
        "conv_b": cont(f["L0_attn_conv_b"].reshape(NCONV, P).T),
        "heads": np.stack([f["L0_attn_A_log"], f["L0_attn_D"], f["L0_attn_dt_bias"]]),
        "w_out": cont(rows(f["L0_attn_w_out"].T)),
        "gains": np.stack([f["L0_attn_ln1_w"], f["L0_attn_ln2_w"], f["L1_ffn_ln_gamma"], f["L1_ffn_ln_beta"]]),
        "up_M": up(f["L0_attn_gate_w"], f["L0_attn_up_w"]),
        "down_M": cont(rows(f["L0_attn_down_w"].T)),
        "up_F": up(pad_rows(f["L0_ffn_W_gate"]), pad_rows(f["L0_ffn_W_up"])),
        "down_F": cont(rows(pad_rows(f["L0_ffn_W_down"].T))),
        "up_E": up(f["L1_ffn_up_w"].T),
        "down_E": rows(f["L1_ffn_down_w"]),
        "gw": by_partition(f["L1_ffn_gate_w"]),
        "expert": by_partition(f["L1_ffn_expert_w"].T),
        "fc2": by_partition(f["L1_ffn_fc2_w"]),
        "fc1": by_partition(f["L1_ffn_fc1_w"].T),
    }
    qkv = f["L1_attn_weight_qkv"].reshape(NKV, 6, P, D)
    out["wv"] = cont(qkv[:, 5].transpose(1, 0, 2))
    proj = f["L1_attn_weight_proj"].reshape(D, NKV, 2, 2, P)
    out["wp"] = cont(proj.transpose(1, 2, 4, 3, 0).reshape(2 * NKV, P, 2, D))
    return {k: cont(v) for k, v in out.items()}


def kernel(**inputs):
    import concourse.bacc as bacc
    from concourse.bass_utils import run_bass_kernel_spmd

    arrays = lay_out(inputs)
    nc = bacc.Bacc("TRN2", target_bir_lowering=False, num_devices=1)
    t = {k: nc.dram_tensor("in_" + k, v.shape, mybir.dt.from_np(v.dtype), kind="ExternalInput").ap()
         for k, v in arrays.items()}
    t["out"] = nc.dram_tensor("out", (T, D), F32, kind="ExternalOutput").ap()
    build_program(nc, t)
    r = run_bass_kernel_spmd(nc, [{"in_" + k: v for k, v in arrays.items()}], core_ids=[0])
    return r.results[0]["out"].reshape(1, T, D)
```

```python
import concourse.bass as bass
from concourse import mybir

P = 128
T = 1024
D = 512
NT = T // P
KD = D // P
HALF = 512
NH = 4
NCONV = 6
TAPS = 4
MIX_BANKS = (3, 4, 5, 7)
NKV = 8
EPS = 1e-5

F32 = mybir.dt.float32
F32R = mybir.dt.float32r
I32 = mybir.dt.int32
ALU = mybir.AluOpType
ACT = mybir.ActivationFunctionType

RSQRT_GUESS = float(0x5F3759DF - (1 << 22) - (1 << 31))
NEWTON = 3
BATCH = 4


class Block:

    def __init__(self, layer, first, tiles, final, attention=False):
        self.layer, self.first, self.tiles, self.final = layer, first, tiles, final
        self.attention = attention
        self.pairs = [min(2, tiles - 2 * p) for p in range((tiles + 1) // 2)]
        self.mats = 1 if layer == "E" else 2
        self.moe = layer == "E" and final


def plan():
    blocks = [Block("M", 0, 6, False), Block("M", 6, 4, False), Block("M", 10, 4, True),
              Block("F", 0, 6, False), Block("F", 6, 5, True),
              Block("A", 0, 0, True, attention=True),
              Block("E", 0, 4, False), Block("E", 4, 4, True)]
    groups, downs, norms, scales = 0, 0, 2 * NT, 0
    kept = 1
    uses = [3, 2, 1]
    for b in blocks:
        b.group0, b.down0, b.use0, b.norm0, b.rstd0, b.kept0 = groups, downs, list(uses), norms, scales, kept
        groups += 2 * b.tiles
        downs += NT
        if not b.attention:
            uses[0] += len(b.pairs)
            uses[1] += sum(n == 2 for n in b.pairs)
            uses[2] += len(b.pairs)
        if b.final:
            norms += NT
            scales += NT // 2
            kept += NT
    ssd = Block("SSD", 0, 0, True)
    ssd.norm0 = NT
    for i, b in enumerate(blocks):
        b.group1 = b.group0 + 2 * b.tiles
        b.next_up = next((n for n in blocks[i + 1:] if not n.attention), None)
        before = blocks[i - 1] if i else ssd
        b.pending = before if before.final else None
        b.following = blocks[i + 1] if i + 1 < len(blocks) else None
        b.fresh = b.pending is not None
    return blocks


def build_program(nc, t):
    blocks = plan()
    here = [16512]

    def place(name, shape, dtype=F32, at=None):
        size = 4
        for n in shape:
            size *= n
        if at is None:
            at = here[0]
            here[0] = at + (size + 31) // 32 * 32
        return nc.alloc_sbuf_tensor_at(name, [P, *shape], dtype, offset=at), at + (size + 31) // 32 * 32

    xres, _ = place("xres", [NT, D])
    xT_hi, _ = place("xT_hi", [KD, T], F32R)
    xT_lo, _ = place("xT_lo", [KD, T], F32R)
    mix, _ = place("mix", [KD, D])
    lat, _ = place("lat", [KD, D])
    shared, _ = place("shared", [NT, D], at=here[0] - 2 * KD * D * 4)
    up_hi = [place(f"up_hi{s}", [2, KD, P], F32R)[0] for s in range(2)]
    up_lo = [place(f"up_lo{s}", [2, KD, P], F32R)[0] for s in range(2)]
    raw = [place(f"raw{s}", [2 * KD * P])[0] for s in range(4)]
    xn = [place(f"xn{u}", [D])[0] for u in range(2)]
    rb = [place(f"rb{u}", [D])[0] for u in range(2)]
    ln1, _ = place("ln1", [D])
    ln2, _ = place("ln2", [D])
    gamma, _ = place("gamma", [D])
    beta, _ = place("beta", [D])
    ident, _ = place("ident", [P])
    tri, _ = place("tri", [P])
    after, _ = place("after", [P])
    ones, _ = place("ones", [P])
    conv_w, _ = place("conv_w", [NCONV, TAPS])
    conv_b, _ = place("conv_b", [NCONV])
    heads_in, _ = place("heads_in", [3, NH])
    dtw, _ = place("dtw", [KD, NH])
    dtw_hi, _ = place("dtw_hi", [KD, NH], F32R)
    dtw_lo, _ = place("dtw_lo", [KD, NH], F32R)
    gw, _ = place("gw", [KD, 8])
    gw_hi, _ = place("gw_hi", [KD, 8], F32R)
    gw_lo, _ = place("gw_lo", [KD, 8], F32R)
    neg_A, _ = place("neg_A", [NH])
    dts = [place(f"dts{i}", [NT, NH])[0] for i in range(6)]
    dt_sp, _ = place("dt_sp", [NT, NH])
    decay, _ = place("decay", [NT, NH])
    to_end, _ = place("to_end", [NT, NH])
    stat, _ = place("stat", [BATCH, 6])
    mv, _ = place("mv", [BATCH, 2])
    ve, _ = place("ve", [BATCH])
    ry, _ = place("ry", [BATCH])
    rt, _ = place("rt", [BATCH])
    shift, _ = place("shift", [BATCH])
    top8, _ = place("top8", [NT, 8])
    route, _ = place("route", [NT])
    spare, _ = place("spare", [3])
    act_spare, _ = place("act_spare", [1])
    region = here[0]

    xBC, e = place("xBC", [NCONV, T + TAPS - 1], at=region)
    z, e_z = place("z", [NH, T], at=e)
    lat_exp, e2 = place("lat_exp", [2, 2 * P], at=e)
    lat_fc2, e2 = place("lat_fc2", [2, D], at=e2)
    lat_fc1, e2 = place("lat_fc1", [2, D], at=e2)
    lat_e2, e2 = place("lat_e2", [2, D], at=e2)
    assert e2 <= e_z
    acc = [None, None]
    acc[0], e = place("acc0", [T], at=e_z)
    acc[1], e = place("acc1", [T], at=e)
    wv, e = place("wv", [NKV, D], at=e)
    wps, e = place("wps", [NKV, D], at=e)
    wpraw = [None, None]
    wpraw[0], e = place("wpraw0", [2, D], at=e)
    wpraw[1], e_mix = place("wpraw1", [2, D], at=e)
    atri, e = place("atri", [NH, P], at=e_z)
    dtri, e = place("dtri", [NH, P], at=e)
    Xs, e = place("Xs", [NH, P], at=e)
    stXB, e = place("stXB", [2, P], at=e)
    XBt, e = place("XBt", [2, P], at=e)
    wo_hi, e = place("wo_hi", [KD, D], F32R, at=e)
    wo_lo, e = place("wo_lo", [KD, D], F32R, at=e)
    ssd = {}
    for name in ("eD", "eE", "att", "Cs", "xsD", "state", "y"):
        ssd[name], e = place(name, [NH, P], at=e)
    y_hi, e = place("y_hi", [NH, P], F32R, at=e)
    y_lo, e = place("y_lo", [NH, P], F32R, at=e)
    end = max(e, e_mix)
    eD, eE, att, Cs, xsD, state, y = (ssd[n] for n in ("eD", "eE", "att", "Cs", "xsD", "state", "y"))

    MAXT = max(b.tiles for b in blocks)
    hT, e = place("hT", [MAXT, T], at=region)
    wd_hi, e = place("wd_hi", [MAXT, D], F32R, at=e)
    wd_lo, e = place("wd_lo", [MAXT, D], F32R, at=e)
    st_hi, st_lo = [None, None], [None, None]
    for u in range(2):
        st_hi[u], e = place(f"st_hi{u}", [2 * KD, P], F32R, at=e)
        st_lo[u], e = place(f"st_lo{u}", [2 * KD, P], F32R, at=e)
    mix_hi, e = place("mix_hi", [KD, D], F32R, at=e)
    mix_lo, e = place("mix_lo", [KD, D], F32R, at=e)
    sg = [None, None]
    sg[1], e = place("sg1", [HALF], at=e)
    sg[0], e = place("sg0", [HALF], at=max(e, end))
    end = max(end, e)
    assert end <= nc.sbuf_usable_end, end

    bank = [nc.alloc_psum_tensor(f"bank{i}", [P, 512], F32) for i in range(8)]

    names = """small_in x_in0 x_in1 x_in2 x_in3 lat_in fc1_in wv_in gains_in
        raw_in0 raw_in1 raw_in2 raw_in3 w_hi0 w_hi1 w_hi2 w_hi3 w_lo0 w_lo1 w_lo2 w_lo3 wp_in0 wp_in1 wp_summed
        consts pads small_split dve_step pool_step
        xn_done tr_mm xT_hi_done xT_lo_done xres_done
        e2_mm e2_done lat_mm lat_done p1_mm p1_done conv_done conv_silu dtT_mm dtT_done dt_mm dt_v dt_exp
        a_done end_mm end_exp mix_mm mix_done
        st_xb atri_done dtri_done xbt_mm xbt_done g_mm d_mm e_mm expd_done expe_done
        edm_done cs_done xsd_done xs_done att_done y_mm s_mm y1_done y_done yhi_done ylo_done
        state_done o_mm
        gate_mm up_mm act_done h_done st_hi_done st_lo_done down_mm r_done
        mixhl_hi mixhl_lo gateT_mm gateT_done logits_mm route_done route_mm routed_done rstd_done both_done r2_done ht_done x_added out_done out_sent0 out_sent1""".split()
    S = {n: nc.alloc_semaphore(n) for n in names}

    def wait(e, name, value):
        if isinstance(value, int) and value <= 0:
            return
        e.wait_ge(S[name], value)

    def tok(i):
        return bass.ds(i * P, P)

    def heads(ap):
        return ap.unsqueeze(1).to_broadcast([P, NH, P])

    def per_head(ap):
        return ap.unsqueeze(2).to_broadcast([P, NH, P])

    block = nc.Block()
    with block:

        @block.sync
        def _(sp):
            def raw_load(slot, use, dst, src):
                wait(sp, f"w_lo{slot}", use)
                sp.dma_start(dst, src).then_inc(S[f"raw_in{slot}"], 16)

            def load_win(piece):
                raw_load(piece % 2, piece // 2, raw[piece % 2][:, :], t["w_in"][piece])

            def load_x(i):
                sp.dma_start(xres[:, 2 * i:2 * i + 2, :],
                             t["x"][2 * i * P:2 * (i + 1) * P, :].rearrange("(t p) d -> p t d", p=P)
                             ).then_inc(S[f"x_in{i}"], 16)

            def load_gain(i, gain):
                sp.dma_start(gain[:, :], t["gains"][i:i + 1, :].to_broadcast([P, D])).then_inc(S["gains_in"], 16)

            load_x(0)
            load_gain(0, ln1)
            load_x(1)
            load_win(0)
            sp.dma_start(lat_exp[:, :, :], t["expert"]).then_inc(S["lat_in"], 16)
            sp.dma_start(lat_fc2[:, :, :], t["fc2"]).then_inc(S["lat_in"], 16)
            load_x(2)
            load_x(3)
            load_win(1)
            for dst, name in ((dtw, "dtw"), (gw, "gw"), (conv_w, "conv_w"), (conv_b, "conv_b")):
                sp.dma_start(dst[:], t[name]).then_inc(S["small_in"], 16)
            sp.dma_start(heads_in[:, :, :], t["heads"].unsqueeze(0).to_broadcast([P, 3, NH])
                         ).then_inc(S["small_in"], 16)
            sp.dma_start(lat_fc1[:, :, :], t["fc1"]).then_inc(S["fc1_in"], 16)
            load_win(2)
            load_win(3)
            for i, gain in enumerate((ln2, gamma, beta)):
                wait(sp, "xn_done", 1)
                load_gain(i + 1, gain)
            sp.dma_start(wv[:, :, :], t["wv"]).then_inc(S["wv_in"], 16)

            def load_wp(i):
                wait(sp, "wp_summed", i - 1)
                sp.dma_start(wpraw[i % 2][:, :, :], t["wp"][i]).then_inc(S[f"wp_in{i % 2}"], 16)

            for i in range(2 * NKV):
                load_wp(i)
                if i == 12:
                    load_win(4)
            def load_up(b, p, s):
                w = b.mats * KD * P
                use = b.use0[s] + p
                raw_load(s, use, raw[s][:, 0:w],
                         t["up_" + b.layer][bass.ds(b.first + 2 * p + s, 1)].rearrange("o p n -> p (o n)"))

            def load_down(b, p, n):
                raw_load(2, b.use0[2] + p, raw[2][:, 0:n * D].rearrange("p (k n) -> p k n", k=n),
                         t["down_" + b.layer][bass.ds(b.first + 2 * p, n)].rearrange("k p n -> p k n"))

            def pair(b, p, n, following):
                load_down(b, p, n)
                if following is not None:
                    nb, np_, nn = following
                    for s in range(nn):
                        load_up(nb, np_, s)

            def load_wout(i):
                raw_load(2 + i, 0, raw[2 + i][:, :].rearrange("p (k n) -> p k n", k=2),
                         t["w_out"][2 * i:2 * i + 2].rearrange("k p n -> p k n"))

            load_wout(0)
            load_wout(1)
            for s in range(2):
                load_up(blocks[0], 0, s)
            for b in blocks:
                if b.attention:
                    continue
                full = sum(n == 2 for n in b.pairs[1:])
                if full:
                    with sp.Fori(0, full) as p:
                        pair(b, p, 2, (b, p + 1, 2))
                for p in range(full, len(b.pairs)):
                    if p + 1 < len(b.pairs):
                        pair(b, p, b.pairs[p], (b, p + 1, b.pairs[p + 1]))
                    elif b.next_up is not None:
                        pair(b, p, b.pairs[p], (b.next_up, 0, 2))
                    else:
                        pair(b, p, b.pairs[p], None)

            def store(p, u):
                wait(sp, "out_done", 2 * p + u + 1)
                sp.dma_start(t["out"][bass.ds((2 * p + u) * P, P), :], xn[u][:, :]
                             ).then_inc(S[f"out_sent{u}"], 16)

            with sp.Fori(0, NT // 2) as p:
                for u in range(2):
                    store(p, u)
            for u in range(2):
                sp.wait_ge(S[f"out_sent{u}"], 16 * NT // 2)

        @block.gpsimd
        def _(pool):
            def select(out, op, base, cm, step):
                pool.wait_ge(S["pool_step"], 1)
                pool.affine_select(out=out[:, :], in_=ones[:, :], compare_op=op, fill=0.0, base=base,
                                   pattern=[[step, P]], channel_multiplier=cm).then_inc(S["consts"], 1)

            pool.memset(ones[:, :], 1.0).then_inc(S["pool_step"], 1)
            select(ident, ALU.is_equal, 0, 1, -1)
            select(tri, ALU.is_ge, 0, -1, 1)
            select(after, ALU.is_gt, 0, 1, -1)
            pool.memset(xBC[:, :, 0:TAPS - 1], 0.0).then_inc(S["pads"], 1)

            def lo(slot, use, src, hi, dst):
                wait(pool, f"w_hi{slot}", use + 1)
                pool.tensor_tensor(dst, src, hi.bitcast(F32), ALU.subtract).then_inc(S[f"w_lo{slot}"], 1)

            def lo_win(piece):
                s = piece % 2
                lo(s, piece // 2, raw[s][:, :].rearrange("p (a k n) -> p a k n", a=2, k=KD),
                   up_hi[s][:, :, :, :], up_lo[s][:, :, :, :])

            def lo_up(b, p, s):
                w = b.mats * KD * P
                lo(s, b.use0[s] + p, raw[s][:, 0:w].rearrange("p (a k n) -> p a k n", a=b.mats, k=KD),
                   up_hi[s][:, 0:b.mats, :, :], up_lo[s][:, 0:b.mats, :, :])

            lo_win(0)
            lo_win(1)

            adds = [0]

            def sum_wp(i):
                g, half = i // 2, i % 2
                pool.wait_ge(S[f"wp_in{i % 2}"], 16 * (i // 2 + 1))
                for r in range(2):
                    if half == 0 and r == 0:
                        continue
                    if half == 0:
                        ins = pool.tensor_tensor(wps[:, g, :], wpraw[0][:, 0, :], wpraw[0][:, 1, :], ALU.add)
                    else:
                        pool.wait_ge(S["wp_summed"], adds[0])
                        if r == 1:
                            pool.wait_ge(S["pool_step"], 2 + g)
                        ins = pool.tensor_tensor(wps[:, g, :], wps[:, g, :], wpraw[1][:, r, :], ALU.add)
                    if half == 1 and r == 0:
                        ins.then_inc(S["pool_step"], 1)
                    else:
                        adds[0] += 1
                        ins.then_inc(S["wp_summed"], 1)

            for i in range(2 * NKV):
                sum_wp(i)
            for s in range(2):
                lo_up(blocks[0], 0, s)

            def prepare(c):
                wait(pool, "g_mm", c)
                pool.tensor_copy(stXB[:, :, :], xBC[:, 0:2, bass.ds(c * P + TAPS - 1, P)]
                                 ).then_inc(S["st_xb"], 1)
                wait(pool, "e_mm", c)
                a = decay[:, bass.ds(c, 1), :].rearrange("p o h -> p (o h)")
                pool.tensor_tensor(atri[:, :, :], heads(tri[:, :]), per_head(a), ALU.mult
                                   ).then_inc(S["atri_done"], 1)
                wait(pool, "edm_done", c)
                dt = dt_sp[:, bass.ds(c, 1), :].rearrange("p o h -> p (o h)")
                pool.tensor_tensor(dtri[:, :, :], heads(tri[:, :]), per_head(dt), ALU.mult
                                   ).then_inc(S["dtri_done"], 1)

            def scale(c):
                at = bass.ds(c * P + TAPS - 1, P)
                wait(pool, "expd_done", c + 1)
                wait(pool, "dtri_done", c + 1)
                pool.tensor_tensor(eD[:, :, :], eD[:, :, :], dtri[:, :, :], ALU.mult).then_inc(S["edm_done"], 1)
                wait(pool, "expe_done", c + 1)
                wait(pool, "y1_done", c)
                pool.tensor_tensor(Cs[:, :, :], xBC[:, 2:6, at], eE[:, :, :], ALU.mult).then_inc(S["cs_done"], 1)
                xs = xBC[:, 0:1, at].rearrange("p o n -> p (o n)")
                pool.tensor_tensor(xsD[:, :, :], heads(xs), per_head(heads_in[:, 1, :]), ALU.mult
                                   ).then_inc(S["xsd_done"], 1)

            def add_x(c, u):
                wait(pool, "ht_done", c + 1)
                at = bass.ds(c, 1)
                pool.tensor_tensor(xres[:, at, :], xres[:, at, :], rb[u][:, :].unsqueeze(1), ALU.add
                                   ).then_inc(S["x_added"], 1)

            pool.wait_ge(S["a_done"], 1)
            pool.wait_ge(S["conv_silu"], NCONV)
            prepare(0)
            scale(0)
            prepare(1)
            scale(1)
            prepare(2)
            add_x(0, 0)
            with pool.Fori(1, NT // 2 - 1) as p:
                for u in range(2):
                    scale(2 * p + u)
                    prepare(2 * p + u + 1)
                    add_x(2 * p + u - 1, 1 - u)
            scale(NT - 2)
            prepare(NT - 1)
            add_x(NT - 3, 1)
            scale(NT - 1)
            add_x(NT - 2, 0)
            add_x(NT - 1, 1)

            def stage_lo(b, tile, u):
                if b.attention:
                    wait(pool, "down_mm", b.down0 + tile - 1)
                    wait(pool, "xT_lo_done", b.norm0 - NT + tile + 1)
                    ins = pool.tensor_copy(st_lo[u][:, 0:KD, :], xT_lo[:, :, tok(tile)].bitcast(F32))
                else:
                    wait(pool, "st_hi_done", b.down0 + tile + 1)
                    k = KD if b.moe else 0
                    ins = pool.tensor_tensor(st_lo[u][:, k:k + b.tiles, :], hT[:, 0:b.tiles, tok(tile)],
                                             st_hi[u][:, k:k + b.tiles, :].bitcast(F32), ALU.subtract)
                ins.then_inc(S["st_lo_done"], 1)

            def add_shared(b, tile, u):
                wait(pool, "routed_done", tile + 1)
                wait(pool, "r_done", b.down0)
                pool.tensor_tensor(rb[u][:, :].unsqueeze(1), rb[u][:, :].unsqueeze(1),
                                   shared[:, bass.ds(tile, 1), :], ALU.add).then_inc(S["both_done"], 1)

            def pair(b, p, n, following, last_pair=False):
                if last_pair:
                    for u in range(2):
                        stage_lo(b, u, u)
                if following is not None:
                    nb, np_, nn = following
                    for s in range(nn):
                        lo_up(nb, np_, s)

            for i, b in enumerate(blocks):
                if not b.attention:
                    full = sum(n == 2 for n in b.pairs[1:])
                    if full:
                        with pool.Fori(0, full) as p:
                            pair(b, p, 2, (b, p + 1, 2))
                    for p in range(full, len(b.pairs)):
                        if p + 1 < len(b.pairs):
                            pair(b, p, b.pairs[p], (b, p + 1, b.pairs[p + 1]))
                        elif b.next_up is not None:
                            pair(b, p, b.pairs[p], (b.next_up, 0, 2), last_pair=True)
                        else:
                            pair(b, p, b.pairs[p], None, last_pair=True)
                if b.attention:
                    for u in range(2):
                        stage_lo(b, u, u)
                with pool.Fori(0, NT // 2 - 1) as p:
                    for u in range(2):
                        stage_lo(b, 2 * p + u + 2, u)
                        if b.moe:
                            add_shared(b, 2 * p + u, u)
                for u in range(2):
                    if b.moe:
                        add_shared(b, NT - 2 + u, u)

        @block.scalar
        def _(act):
            def copy(dst, src, name):
                return act.activation(dst, src, ACT.Copy).then_inc(S[name], 1)

            def hi(slot, use, src, dst):
                wait(act, f"raw_in{slot}", 16 * (use + 1))
                copy(dst, src, f"w_hi{slot}")

            def hi_win(piece):
                s = piece % 2
                hi(s, piece // 2, raw[s][:, :].rearrange("p (a k n) -> p a k n", a=2, k=KD),
                   up_hi[s][:, :, :, :])

            def hi_up(b, p, s):
                w = b.mats * KD * P
                hi(s, b.use0[s] + p, raw[s][:, 0:w].rearrange("p (a k n) -> p a k n", a=b.mats, k=KD),
                   up_hi[s][:, 0:b.mats, :, :])

            def hi_down(b, p, n):
                hi(2, b.use0[2] + p, raw[2][:, 0:n * D].rearrange("p (k n) -> p k n", k=n),
                   wd_hi[:, bass.ds(2 * p, n), :])

            def evac_hi(j, tile, bk):
                wait(act, "tr_mm", j + 1)
                copy(xT_hi[:, :, tok(tile)], bank[bk][:, :].rearrange("p (k n) -> p k n", k=KD), "xT_hi_done")

            act.preload_act_table(ACT.Silu)
            hi_win(0)

            def evac_p1(g):
                piece, half, f = g // 4, g // 2 % 2, g % 2
                i = 2 * piece + f
                wait(act, "p1_mm", g + 1)
                if i < NCONV:
                    copy(xBC[:, i, TAPS - 1 + half * HALF:TAPS - 1 + (half + 1) * HALF], bank[g % 4][:, :], "p1_done")
                else:
                    act.activation(z[:, i - NCONV, half * HALF:(half + 1) * HALF], bank[g % 4][:, :],
                                   ACT.Silu).then_inc(S["p1_done"], 1)

            def evac_lat(n):
                wait(act, "lat_mm", n + 1)
                copy(lat[:, n, :], bank[4 + n % 2][:, :], "lat_done")

            for n in range(2):
                wait(act, "e2_mm", n + 1)
                copy(lat_e2[:, n, :], bank[4 + n][:, :], "e2_done")
            for j in range(4):
                evac_hi(j, j, 6 + j % 2)
            hi_win(1)
            evac_p1(0)
            evac_p1(1)
            for j in range(4, 6):
                evac_hi(j, j, 6 + j % 2)
            for n in range(KD):
                evac_lat(n)
                if n < 2:
                    evac_hi(6 + n, 6 + n, 6 + n)
            evac_p1(2)
            evac_p1(3)
            act.wait_ge(S["pads"], 1)

            def conv_silu(i):
                wait(act, "conv_done", i + 1)
                act.activation(xBC[:, i, TAPS - 1:], acc[i % 2][:, :], ACT.Silu, bias=conv_b[:, i:i + 1]
                               ).then_inc(S["conv_silu"], 1)

            act.wait_ge(S["small_in"], 16 * 5)
            for piece in range(5):
                if piece:
                    for g in range(4 * piece, 4 * piece + 4):
                        evac_p1(g)
                if piece == 1:
                    for half in range(2):
                        wait(act, "dtT_mm", half + 1)
                        copy(xn[half][0:NH, :], bank[4 + half][0:NH, :], "dtT_done")
                if piece + 2 < 5:
                    hi_win(piece + 2)
                if 1 <= piece <= 3:
                    conv_silu(2 * piece - 2)
                    conv_silu(2 * piece - 1)
            act.preload_act_table(ACT.Exp)
            act.activation(neg_A[:, :], heads_in[:, 0, :], ACT.Exp).then_inc(S["dt_exp"], 1)
            act.wait_ge(S["dt_v"], 1)
            act.activation(dts[2][:, :, :], dts[1][:, :, :], ACT.Exp, scale=-1.0).then_inc(S["dt_exp"], 1)
            for s in range(2):
                hi_up(blocks[0], 0, s)
            act.wait_ge(S["end_mm"], 1)
            act.activation(dts[3][:, :, :], bank[6][:, 32:64].rearrange("p (c h) -> p c h", c=NT), ACT.Exp
                           ).then_inc(S["end_exp"], 1)

            def evac_mix():
                for n in range(KD):
                    wait(act, "mix_mm", n + 1)
                    copy(mix[:, n, :], bank[MIX_BANKS[n]][:, :], "mix_done")

            def hi_wout(i):
                hi(2 + i, 0, raw[2 + i][:, :].rearrange("p (k n) -> p k n", k=2), wo_hi[:, 2 * i:2 * i + 2, :])


            def ssd_step(c, transposed):
                wait(act, "xbt_mm", c + 1)
                wait(act, "s_mm", c)
                copy(XBt[:, :, :], bank[6][:, 0:2 * P].rearrange("p (a n) -> p a n", a=2), "xbt_done")
                wait(act, "d_mm", c + 1)
                wait(act, "att_done", c)
                act.activation(eD[:, :, :], bank[1][:, :].rearrange("p (h n) -> p h n", h=NH), ACT.Exp
                               ).then_inc(S["expd_done"], 1)
                wait(act, "e_mm", c + 1)
                wait(act, "cs_done", c)
                wait(act, "state_done", c)
                act.activation(eE[:, :, :], bank[2][:, :].rearrange("p (h n) -> p h n", h=NH), ACT.Exp
                               ).then_inc(S["expe_done"], 1)
                if transposed:
                    evac_hi(NT + c - 4, c - 4, 7)
                if isinstance(c, int) and c == 0:
                    evac_mix()
                    hi_wout(0)
                    hi_wout(1)
                wait(act, "y_done", c + 1)
                wait(act, "o_mm", c)
                copy(y_hi[:, :, :], y[:, :, :], "yhi_done")

            for c in range(4):
                ssd_step(c, False)
            with act.Fori(2, NT // 2) as p:
                for u in range(2):
                    ssd_step(2 * p + u, True)

            def activate(b, g, par):
                wait(act, "gate_mm" if b.mats == 2 else "up_mm", g + 1)
                wait(act, "h_done", g - 1)
                act.activation(sg[par][:, :], bank[2 * par][:, :], ACT.Relu if b.layer == "E" else ACT.Silu
                               ).then_inc(S["act_done"], 1)

            def stage_x(b, tile, u):
                wait(act, "down_mm", b.down0 + tile - 1)
                if b.attention:
                    wait(act, "xT_lo_done", b.norm0 - NT + tile + 1)
                ins = act.activation(st_hi[u][:, 0:KD, :], xT_hi[:, :, tok(tile)].bitcast(F32), ACT.Copy)
                if b.moe:
                    act.activation(st_lo[u][:, 0:KD, :], xT_lo[:, :, tok(tile)].bitcast(F32), ACT.Copy)
                else:
                    ins.then_inc(S["st_hi_done"], 1)

            def stage_h(b, tile, u):
                wait(act, "down_mm", b.down0 + tile - 1)
                k = KD if b.moe else 0
                act.activation(st_hi[u][:, k:k + b.tiles, :], hT[:, 0:b.tiles, tok(tile)], ACT.Copy
                               ).then_inc(S["st_hi_done"], 1)

            def stage_hi(b, tile, u):
                if b.attention or b.moe:
                    stage_x(b, tile, u)
                if not b.attention:
                    stage_h(b, tile, u)

            def scales(b, q):
                wait(act, "rstd_done", b.rstd0 + q + 1)
                if not b.moe:
                    wait(act, "xres_done", b.kept0 + 2 * q)
                act.activation(act_spare[:, :], neg_A[:, 0:1], ACT.Copy)

            def normalize(b, q, u):
                tile = 2 * q + u
                src = xres[:, bass.ds(tile, 1), :].rearrange("p o n -> p (o n)")
                if b.moe:
                    wait(act, f"out_sent{u}", 16 * q)
                act.activation(xn[u][:, :], src, ACT.Identity, scale=ry[:, u:u + 1], bias=shift[:, u:u + 1]
                               ).then_inc(S["out_done" if b.moe else "xn_done"], 1)

            def keep_xn(tile, u):
                copy(xres[:, bass.ds(tile, 1), :], xn[u][:, :].unsqueeze(1), "xres_done")

            def pair(b, p, n, following, pending=None, last_pair=False):
                g = b.group0 + 4 * p
                normed = pending is not None and pending.layer != "SSD"
                if normed:
                    scales(pending, NT // 2 - 1)
                    for u in range(2):
                        normalize(pending, NT // 2 - 1, u)
                activate(b, g, 0)
                if pending is not None and not normed:
                    for i in (NT - 4, NT - 3):
                        evac_hi(NT + i, i, 6 + i % 2)
                if n == 2:
                    activate(b, g + 1, 1)
                if pending is not None:
                    for u in range(2):
                        evac_hi(pending.norm0 + NT - 2 + u, NT - 2 + u, 6 + u)
                    if normed:
                        for u in range(2):
                            keep_xn(NT - 2 + u, u)
                hi_down(b, p, n)
                last = g + n
                if last_pair and b.moe:
                    for u in range(2):
                        stage_x(b, u, u)
                activate(b, last, n % 2)
                if last_pair:
                    wait(act, "h_done", b.group1 - n)
                    for u in range(2):
                        stage_h(b, u, u)
                if following is not None:
                    nb, np_, nn = following
                    wait(act, "up_mm", last + 1)
                    hi_up(nb, np_, 0)
                if n == 2:
                    activate(b, last + 1, 1)
                if following is not None and following[2] == 2:
                    if n == 2:
                        wait(act, "up_mm", last + 2)
                    hi_up(nb, np_, 1)

            act.preload_act_table(ACT.Silu)
            act.activation(act_spare[:, :], neg_A[:, 0:1], ACT.Copy).then_inc(S["xres_done"], 1)
            for b in blocks:
                pending = b.pending
                if not b.attention:
                    full = sum(n == 2 for n in b.pairs[1:])
                    first = 1 if b.fresh else 0
                    for p in range(first):
                        pair(b, p, b.pairs[p], (b, p + 1, b.pairs[p + 1]), pending)
                    if b.layer == "F" and b.final:
                        copy(mix_hi[:, :, :], mix[:, :, :], "mixhl_hi")
                    if b.layer == "E" and not b.final:
                        for half in range(2):
                            wait(act, "xres_done", pending.kept0 + NT)
                            wait(act, "gateT_mm", half + 1)
                            copy(xn[half][0:8, :], bank[4 + half][0:8, :], "gateT_done")
                        copy(mix_hi[:, :, :], lat[:, :, :], "mixhl_hi")
                    if full > first:
                        with act.Fori(first, full) as p:
                            pair(b, p, 2, (b, p + 1, 2))
                    for p in range(max(first, full), len(b.pairs)):
                        if p + 1 < len(b.pairs):
                            pair(b, p, b.pairs[p], (b, p + 1, b.pairs[p + 1]))
                        elif b.next_up is not None:
                            pair(b, p, b.pairs[p], (b.next_up, 0, 2), last_pair=True)
                        else:
                            pair(b, p, b.pairs[p], None, last_pair=True)
                    pending = None
                after_b = b.following if b.following is not None and b.following.attention else None

                def down_pair(p, stage, previous):
                    for u in range(2):
                        tile = 2 * p + u
                        if stage:
                            stage_hi(b, tile + 2, u)
                        elif after_b is not None:
                            stage_hi(after_b, u, u)
                        if b.moe:
                            if u == 0:
                                wait(act, "route_done", 1)
                            wait(act, "route_mm", tile + 1)
                            wait(act, "r2_done", tile - 1)
                            act.activation(rb[u][:, :], bank[6 + u][:, :], ACT.Copy,
                                           scale=route[:, bass.ds(tile, 1)]).then_inc(S["routed_done"], 1)
                        if previous is not None and u == (1 if b.moe else 0):
                            a, q = previous
                            scales(a, q)
                            for v in range(2):
                                normalize(a, q, v)
                    if previous is not None and not b.moe:
                        for v in range(2):
                            evac_hi(a.norm0 + 2 * q + v, 2 * q + v, 6 + v)
                        for v in range(2):
                            keep_xn(2 * q + v, v)

                down_pair(0, True, (pending, NT // 2 - 1) if pending is not None else None)
                if not b.attention:
                    wait(act, "h_done", b.group1)
                if b.moe:
                    for p in range(1, NT // 2):
                        down_pair(p, p < NT // 2 - 1, (b, p - 2) if p >= 2 else None)
                    for q in (NT // 2 - 2, NT // 2 - 1):
                        wait(act, "rstd_done", b.rstd0 + q + 1)
                        for u in range(2):
                            normalize(b, q, u)
                else:
                    with act.Fori(1, NT // 2 - 1) as p:
                        down_pair(p, True, (b, p - 1) if b.final else None)
                    down_pair(NT // 2 - 1, False, (b, NT // 2 - 2) if b.final else None)

        @block.vector
        def _(dve):
            base = [0]
            n = [0]

            def link(ins, between=None):
                n[0] += 1
                ins.then_inc(S["dve_step"], 1)
                if between is not None:
                    between()
                dve.wait_ge(S["dve_step"], base[0] + n[0])

            def loop(start, stop, per, body):
                b0 = base[0] + n[0]
                with dve.Fori(start, stop) as i:
                    base[0], n[0] = b0 + (i - start) * per, 0
                    body(i)
                    assert n[0] == per, (n[0], per)
                base[0], n[0] = b0 + (stop - start) * per, 0

            def alone(i):
                dve.memset(spare[:, i:i + 1], 0.0)

            BEGIN_STEPS = {"layer": 3, "rms": 5}
            FINISH_STEPS = 1 + 3 * NEWTON

            def begin_norm(kind, srcs, ready=None, slot=0):
                at = slice(slot, slot + len(srcs))
                for i, src in enumerate(srcs):
                    if ready is not None:
                        ready(i)
                    ins = dve.bn_stats(stat[:, slot + i, :], src)
                link(ins)
                alone(2)
                for i in range(slot, slot + len(srcs)):
                    ins = dve.bn_aggr(mv[:, i, :], stat[:, i, :])
                link(ins)
                mean, under = mv[:, at, 0], mv[:, at, 1]
                if kind == "rms":
                    link(dve.tensor_tensor(rt[:, at], mean, mean, ALU.mult))
                    link(dve.tensor_tensor(rt[:, at], rt[:, at], under, ALU.add))
                    under = rt[:, at]
                link(dve.tensor_scalar(ve[:, at], under, EPS, 0.5, ALU.add, ALU.mult))

            def finish_norm(m, slot=0, shifted=False, between=lambda k: None):
                at = slice(slot, slot + m)
                y, v, w = ry[:, at], ve[:, at], rt[:, at]
                link(dve.tensor_scalar(y.bitcast(I32), v.bitcast(I32), -0.5, RSQRT_GUESS, ALU.mult, ALU.add),
                     lambda: between(0))
                for i in range(NEWTON):
                    link(dve.tensor_tensor(w, y, y, ALU.mult), lambda: between(3 * i + 1))
                    link(dve.tensor_tensor(w, w, v, ALU.mult), lambda: between(3 * i + 2))
                    link(dve.scalar_tensor_tensor(out=y, in0=w, scalar=1.5, in1=y, op0=ALU.subtract, op1=ALU.mult),
                         lambda: between(3 * i + 3))
                if shifted:
                    dve.scalar_tensor_tensor(out=shift[:, at], in0=mv[:, at, 0], scalar=-1.0, in1=y,
                                             op0=ALU.mult, op1=ALU.mult).then_inc(S["rstd_done"], 1)

            def evac_lo(j, tile, bk):
                wait(dve, "xT_hi_done", j + 1)
                dve.tensor_tensor(xT_lo[:, :, tok(tile)], bank[bk][:, :].rearrange("p (k n) -> p k n", k=KD),
                                  xT_hi[:, :, tok(tile)].bitcast(F32), ALU.subtract
                                  ).then_inc(S["xT_lo_done"], 1)

            dve.wait_ge(S["gains_in"], 16)
            def scaled(src, i, u, gain, tr):
                wait(dve, "tr_mm", tr)
                dve.scalar_tensor_tensor(out=xn[u][:, :], in0=src, scalar=ry[:, i:i + 1], in1=gain[:, :],
                                         op0=ALU.mult, op1=ALU.mult).then_inc(S["xn_done"], 1)

            for first in (0, BATCH):
                def loaded(i):
                    if i % 2 == 0:
                        dve.wait_ge(S[f"x_in{(first + i) // 2}"], 16)
                begin_norm("rms", [xres[:, first + i, :] for i in range(BATCH)], loaded)
                finish_norm(BATCH)
                for i in range(BATCH):
                    j = first + i
                    scaled(xres[:, j, :], i, j % 2, ln1, j - 1)
                    if i >= 2:
                        evac_lo(j - 2, j - 2, 6 + j % 2)
                for j in (first + 2, first + 3):
                    evac_lo(j, j, 6 + j % 2)

            dve.wait_ge(S["small_in"], 16 * 5)
            for w, w_hi, w_lo in ((dtw, dtw_hi, dtw_lo), (gw, gw_hi, gw_lo)):
                link(dve.tensor_copy(w_hi[:, :, :], w[:, :, :]))
                dve.tensor_tensor(w_lo[:, :, :], w[:, :, :], w_hi[:, :, :].bitcast(F32), ALU.subtract
                                  ).then_inc(S["small_split"], 1)

            def lo_win(piece):
                s = piece % 2
                wait(dve, f"w_hi{s}", piece // 2 + 1)
                dve.tensor_tensor(up_lo[s][:, :, :, :], raw[s][:, :].rearrange("p (a k n) -> p a k n", a=2, k=KD),
                                  up_hi[s][:, :, :, :].bitcast(F32), ALU.subtract).then_inc(S[f"w_lo{s}"], 1)

            for i in range(NCONV):
                if i % 2 == 0:
                    dve.wait_ge(S["p1_done"], 2 * i + 4)
                else:
                    lo_win(2 + i // 2)
                if i == 0:
                    dve.wait_ge(S["pads"], 1)
                wait(dve, "conv_silu", i - 1)
                a = acc[i % 2]
                link(dve.tensor_scalar(a[:, :], xBC[:, i, TAPS - 1:], conv_w[:, i, TAPS - 1:TAPS], None, ALU.mult))
                for k in range(TAPS - 2, -1, -1):
                    ins = dve.scalar_tensor_tensor(out=a[:, :], in0=xBC[:, i, k:k + T], scalar=conv_w[:, i, k:k + 1],
                                                   in1=a[:, :], op0=ALU.mult, op1=ALU.add)
                    if k:
                        link(ins)
                    else:
                        ins.then_inc(S["conv_done"], 1)

            v, av, e_, s_, s2, pw = dts
            tail = dts[3]
            dve.wait_ge(S["dt_mm"], 1)
            link(dve.tensor_tensor(v[:, :, :], bank[6][:, 0:32].rearrange("p (c h) -> p c h", c=NT),
                                   heads_in[:, 2, :].unsqueeze(1).to_broadcast([P, NT, NH]), ALU.add))
            dve.scalar_tensor_tensor(out=av[:, :, :], in0=v[:, :, :], scalar=-1.0, in1=v[:, :, :],
                                     op0=ALU.mult, op1=ALU.max).then_inc(S["dt_v"], 1)
            dve.wait_ge(S["dt_exp"], 2)
            link(dve.tensor_scalar(s_[:, :, :], e_[:, :, :], 2.0, None, ALU.add))
            link(dve.reciprocal(s2[:, :, :], s_[:, :, :]))
            link(dve.tensor_tensor(s_[:, :, :], e_[:, :, :], s2[:, :, :], ALU.mult))
            link(dve.tensor_tensor(s2[:, :, :], s_[:, :, :], s_[:, :, :], ALU.mult))
            link(dve.tensor_scalar(pw[:, :, :], s2[:, :, :], 1.0 / 15, None, ALU.mult))
            for m in (13, 11, 9, 7, 5, 3):
                link(dve.scalar_tensor_tensor(out=pw[:, :, :], in0=pw[:, :, :], scalar=1.0 / m, in1=s2[:, :, :],
                                              op0=ALU.add, op1=ALU.mult))
            link(dve.scalar_tensor_tensor(out=pw[:, :, :], in0=pw[:, :, :], scalar=1.0, in1=s_[:, :, :],
                                          op0=ALU.add, op1=ALU.mult))
            link(dve.tensor_scalar(v[:, :, :], v[:, :, :], 0.0, None, ALU.max))
            link(dve.scalar_tensor_tensor(out=dt_sp[:, :, :], in0=pw[:, :, :], scalar=2.0, in1=v[:, :, :],
                                          op0=ALU.mult, op1=ALU.add))
            dve.scalar_tensor_tensor(out=decay[:, :, :], in0=dt_sp[:, :, :], scalar=-1.0,
                                     in1=neg_A[:, :].unsqueeze(1).to_broadcast([P, NT, NH]),
                                     op0=ALU.mult, op1=ALU.mult).then_inc(S["a_done"], 1)

            def lo_wout(i):
                s = 2 + i
                wait(dve, f"w_hi{s}", 1)
                dve.tensor_tensor(wo_lo[:, 2 * i:2 * i + 2, :], raw[s][:, :].rearrange("p (k n) -> p k n", k=2),
                                  wo_hi[:, 2 * i:2 * i + 2, :].bitcast(F32), ALU.subtract).then_inc(S[f"w_lo{s}"], 1)

            dve.wait_ge(S["end_exp"], 1)
            link(dve.tensor_tensor(to_end[:, :, :], tail[:, :, :], dt_sp[:, :, :], ALU.mult))

            def add_h(c, u):
                wait(dve, "o_mm", c + 1)
                wait(dve, "x_added", c - 1)
                wait(dve, "xn_done", NT + c - 1)
                at = bass.ds(c, 1)
                dve.tensor_tensor(rb[u][:, :].unsqueeze(1), bank[5][:, :].unsqueeze(1), xres[:, at, :], ALU.add
                                  ).then_inc(S["ht_done"], 1)

            def begin_pair(c):
                wait(dve, "ht_done", c + 2)
                begin_norm("rms", [rb[u][:, :] for u in range(2)])

            def finish_pair(c, between=lambda k: None):
                finish_norm(2, between=between)
                for u in range(2):
                    scaled(rb[u][:, :], u, u, ln2, NT + c + u - 1)

            def ssd_step(c, u, first=False, normed=True, transposed=True, last=False):
                if not last:
                    wait(dve, "xbt_done", c + 1)
                    wait(dve, "s_mm", c)
                    w = to_end[:, bass.ds(c, 1), :].rearrange("p o h -> p (o h)")
                    dve.tensor_tensor(Xs[:, :, :], heads(XBt[:, 0, :]), per_head(w), ALU.mult).then_inc(S["xs_done"], 1)
                wait(dve, "g_mm", c + 1)
                wait(dve, "edm_done", c + 1)
                wait(dve, "y_mm", c)
                dve.tensor_tensor(att[:, :, :], bank[0][:, :].rearrange("p (h n) -> p h n", h=NH), eD[:, :, :],
                                  ALU.mult).then_inc(S["att_done"], 1)
                if transposed:
                    evac_lo(NT + c - 4, c - 4, 7)
                def y_sum():
                    wait(dve, "y_mm", c + 1)
                    wait(dve, "xsd_done", c + 1)
                    dve.tensor_tensor(y[:, :, :], bank[3][:, :].rearrange("p (h n) -> p h n", h=NH), xsD[:, :, :],
                                      ALU.add).then_inc(S["y1_done"], 1)

                def y_gated():
                    wait(dve, "y1_done", c + 1)
                    dve.tensor_tensor(y[:, :, :], y[:, :, :], z[:, :, tok(c)], ALU.mult).then_inc(S["y_done"], 1)

                def new_state():
                    wait(dve, "s_mm", c + 1)
                    if first:
                        dve.tensor_copy(state[:, :, :], bank[4][:, :].rearrange("p (h n) -> p h n", h=NH)
                                        ).then_inc(S["state_done"], 1)
                        return
                    wait(dve, "expe_done", c + 1)
                    for h in range(NH):
                        ins = dve.scalar_tensor_tensor(out=state[:, h, :], in0=state[:, h, :],
                                                       scalar=eE[:, h, P - 1:P], in1=bank[4][:, h * P:(h + 1) * P],
                                                       op0=ALU.mult, op1=ALU.add)
                    ins.then_inc(S["state_done"], 1)

                def y_rest():
                    wait(dve, "yhi_done", c + 1)
                    dve.tensor_tensor(y_lo[:, :, :], y[:, :, :], y_hi[:, :, :].bitcast(F32), ALU.subtract
                                      ).then_inc(S["ylo_done"], 1)

                if last:
                    def y_between(k):
                        if k == 6:
                            y_sum()
                        if k == 7:
                            y_gated()
                        if k == 8:
                            y_rest()
                    finish_pair(c - 3, y_between)
                    add_h(c - 1, 1 - u)
                    return
                if normed and u == 1:
                    finish_pair(c - 3)
                if not first:
                    add_h(c - 1, 1 - u)
                if normed and u == 0:
                    begin_pair(c - 2)
                y_sum()
                y_gated()
                if first:
                    for i in range(2):
                        lo_wout(i)
                new_state()
                y_rest()

            dve.wait_ge(S["conv_silu"], NCONV)
            dve.wait_ge(S["gains_in"], 64)
            ssd_step(0, 0, first=True, normed=False, transposed=False)
            ssd_step(1, 1, normed=False, transposed=False)
            for c in (2, 3):
                ssd_step(c, c % 2, transposed=False)
            loop(2, NT // 2 - 1, BEGIN_STEPS["rms"] + FINISH_STEPS,
                 lambda p: [ssd_step(2 * p + u, u) for u in range(2)])
            ssd_step(NT - 2, 0)
            ssd_step(NT - 1, 1, last=True)
            add_h(NT - 1, 1)
            begin_pair(NT - 2)

            def evac_between(i):
                if i < 2:
                    evac_lo(2 * NT - 4 + i, NT - 4 + i, 6 + i)
            finish_pair(NT - 2, evac_between)

            def product(b, g, par, tile, half):
                wait(dve, "act_done", g + 1)
                wait(dve, "up_mm", g + 1)
                src = bank[2 * par] if b.layer == "E" else bank[2 * par + 1]
                dve.tensor_tensor(hT[:, bass.ds(tile, 1), half * HALF:(half + 1) * HALF], sg[par][:, :].unsqueeze(1),
                                  src[:, :].unsqueeze(1), ALU.mult).then_inc(S["h_done"], 1)

            def lo_down(b, p, n):
                wait(dve, "w_hi2", b.use0[2] + p + 1)
                at = bass.ds(2 * p, n)
                dve.tensor_tensor(wd_lo[:, at, :], raw[2][:, 0:n * D].rearrange("p (k n) -> p k n", k=n),
                                  wd_hi[:, at, :].bitcast(F32), ALU.subtract).then_inc(S["w_lo2"], 1)

            def split_mix(src):
                wait(dve, "mixhl_hi", 1 if src is mix else 2)
                dve.tensor_tensor(mix_lo[:, :, :], src[:, :, :], mix_hi[:, :, :].bitcast(F32),
                                  ALU.subtract).then_inc(S["mixhl_lo"], 1)

            def evac_pending(pending):
                for u in range(2):
                    evac_lo(pending.norm0 + NT - 2 + u, NT - 2 + u, 6 + u)

            def pair(b, p, n, pending=None):
                g = b.group0 + 4 * p
                late = b.mats == 1 or pending is not None and pending.layer == "SSD"
                product(b, g, 0, 2 * p, 0)
                if n == 2 and late:
                    product(b, g + 1, 1, 2 * p + 1, 0)
                if pending is not None:
                    evac_pending(pending)
                if n == 2 and not late:
                    product(b, g + 1, 1, 2 * p + 1, 0)
                lo_down(b, p, n)
                product(b, g + n, n % 2, 2 * p, 1)
                if n == 2:
                    product(b, g + n + 1, 1, 2 * p + 1, 1)

            def kept(b, tile):
                if b.fresh and b.pending.layer == "SSD":
                    wait(dve, "x_added", tile + 1)
                elif b.fresh:
                    wait(dve, "xres_done", b.pending.kept0 + tile + 1)

            def down_mid(b, tile, u):
                wait(dve, "down_mm", b.down0 + tile + 1)
                kept(b, tile)
                at = bass.ds(tile, 1)
                if b.layer == "E":
                    dve.tensor_tensor(xres[:, at, :], xres[:, at, :], beta[:, :].unsqueeze(1), ALU.add)
                    dve.tensor_copy(shared[:, at, :], bank[4 + u][:, :].unsqueeze(1)).then_inc(S["r_done"], 1)
                else:
                    dve.tensor_tensor(xres[:, at, :], xres[:, at, :], bank[4 + u][:, :].unsqueeze(1), ALU.add
                                      ).then_inc(S["r_done"], 1)

            def tiles(p):
                return [xres[:, bass.ds(2 * p + u, 1), :].rearrange("p o n -> p (o n)") for u in range(2)]

            def down_norm(b, p, before=None):
                def add(u):
                    tile = 2 * p + u
                    wait(dve, "down_mm", b.down0 + tile + 1)
                    kept(b, tile)
                    at = bass.ds(tile, 1)
                    dve.tensor_tensor(xres[:, at, :], xres[:, at, :], bank[4 + u][:, :].unsqueeze(1), ALU.add
                                      ).then_inc(S["r_done"], 1)
                    wait(dve, "r_done", b.down0 + tile + 1)
                    alone(u)
                begin_norm("layer", tiles(p), add)
                wait(dve, "xn_done", b.norm0 + 2 * p)
                finish_norm(2, shifted=True)
                if before is not None:
                    a, q = before
                    for u in range(2):
                        evac_lo(a.norm0 + 2 * q + u, 2 * q + u, 6 + u)

            def down_out(b, p, first=False, used=None):
                def ready(i):
                    if i == 0 and not first:
                        wait(dve, "r2_done", 2 * p)
                        alone(0)
                    if i >= 2 or first:
                        u = i % 2
                        tile = 2 * p + u
                        wait(dve, "down_mm", b.down0 + tile + 1)
                        wait(dve, "both_done", tile + 1)
                        dve.tensor_tensor(rb[u][:, :], bank[4 + u][:, :], rb[u][:, :], ALU.add
                                          ).then_inc(S["r_done"], 1)
                        wait(dve, "r_done", b.down0 + tile + 1)

                def centred(u):
                    if u < 2:
                        dve.scalar_tensor_tensor(out=rb[u][:, :], in0=rb[u][:, :], scalar=mv[:, 2 + u, 0:1],
                                                 in1=gamma[:, :], op0=ALU.subtract, op1=ALU.mult)
                inner = [rb[u][:, :] for u in range(2)]
                slot = 2 if first else 0
                srcs = inner if first else tiles(p - 1) + inner
                begin_norm("layer", srcs, ready, slot=slot)
                if used is not None:
                    wait(dve, "out_done", used)
                finish_norm(len(srcs), slot=slot, shifted=not first, between=centred)
                for u in range(2):
                    dve.scalar_tensor_tensor(out=tiles(p)[u], in0=rb[u][:, :], scalar=ry[:, 2 + u:3 + u],
                                             in1=tiles(p)[u], op0=ALU.mult, op1=ALU.add).then_inc(S["r2_done"], 1)

            def up_phase(b):
                full = sum(k == 2 for k in b.pairs)
                first = 1 if b.fresh else 0
                if first:
                    pair(b, 0, b.pairs[0], b.pending)
                if b.layer == "F" and b.final:
                    split_mix(mix)
                if b.layer == "E" and not b.final:
                    split_mix(lat)
                if full > first:
                    loop(first, full, 0, lambda p: pair(b, p, 2))
                if b.pairs[-1] == 1:
                    pair(b, len(b.pairs) - 1, 1)

            def routing():
                wait(dve, "logits_mm", 1)
                for tile in range(NT):
                    ins = dve.max(top8[:, tile, :], bank[6][:, 8 * tile:8 * tile + 8])
                link(ins)
                dve.tensor_tensor(route[:, :], top8[:, :, 0], top8[:, :, 1], ALU.add).then_inc(S["route_done"], 1)

            LAYER = BEGIN_STEPS["layer"] + FINISH_STEPS
            for b in blocks:
                if not b.attention:
                    up_phase(b)
                if b.layer == "E" and not b.final:
                    routing()
                if not b.final:
                    loop(0, NT // 2, 0, lambda p: [down_mid(b, 2 * p + u, u) for u in range(2)])
                elif b.moe:
                    down_out(b, 0, first=True)
                    down_out(b, 1)
                    loop(2, NT // 2, LAYER, lambda p: down_out(b, p, used=2 * p - 2))
                    wait(dve, "r2_done", NT)
                    begin_norm("layer", tiles(NT // 2 - 1))
                    wait(dve, "out_done", NT - 2)
                    finish_norm(2, shifted=True)
                else:
                    down_norm(b, 0, (b.pending, NT // 2 - 1) if b.fresh else None)
                    loop(1, NT // 2, LAYER, lambda p: down_norm(b, p, (b, p - 1)))

        @block.tensor
        def _(pe):
            def mm3(out, s_hi, s_lo, m_hi, m_lo, first, last):
                pe.matmul(out, s_hi, m_hi, start=first, stop=False)
                pe.matmul(out, s_hi, m_lo, start=False, stop=False)
                return pe.matmul(out, s_lo, m_hi, start=False, stop=last)

            def turn(j, u, bk, evacuated=None):
                wait(pe, "xn_done", j + 1)
                wait(pe, "xT_lo_done", j - 1 if evacuated is None else evacuated)
                for k in range(KD):
                    ins = pe.transpose(bank[bk][:, k * P:(k + 1) * P], xn[u][:, k * P:(k + 1) * P], ident[:, :])
                ins.then_inc(S["tr_mm"], 1)

            def turn_pair(a, q):
                for u in range(2):
                    turn(a.norm0 + 2 * q + u, u, 6 + u)

            def turn0(j):
                turn(j, j % 2, 6 + j % 2)

            def p1_group(g):
                piece, half, f = g // 4, g // 2 % 2, g % 2
                s = piece % 2
                wait(pe, f"w_lo{s}", piece // 2 + 1)
                if g < 4:
                    wait(pe, "xT_lo_done", NT // 2 if half == 0 else NT)
                wait(pe, "p1_done", g - 3)
                for k in range(KD):
                    at = slice(half * HALF, (half + 1) * HALF)
                    ins = mm3(bank[g % 4][:, :], up_hi[s][:, f, k, :], up_lo[s][:, f, k, :],
                              xT_hi[:, k, at], xT_lo[:, k, at], k == 0, k == KD - 1)
                ins.then_inc(S["p1_mm"], 1)

            def lat_group(n):
                wait(pe, "lat_done", n - 1)
                for k in range(2):
                    ins = pe.matmul(bank[4 + n % 2][:, :], lat_fc1[:, k, n * P:(n + 1) * P], lat_e2[:, k, :],
                                    start=(k == 0), stop=(k == 1))
                ins.then_inc(S["lat_mm"], 1)

            pe.wait_ge(S["consts"], 3)
            pe.wait_ge(S["lat_in"], 32)
            for n in range(2):
                for k in range(2):
                    ins = pe.matmul(bank[4 + n][:, :], lat_exp[:, k, n * P:(n + 1) * P], lat_fc2[:, k, :],
                                    start=(k == 0), stop=(k == 1))
                ins.then_inc(S["e2_mm"], 1)
            for j in range(4):
                turn0(j)
            p1_group(0)
            p1_group(1)
            pe.wait_ge(S["fc1_in"], 16)
            for j in range(4, 6):
                turn0(j)
            pe.wait_ge(S["e2_done"], 2)
            for n in range(KD):
                lat_group(n)
                if n < 2:
                    turn0(6 + n)
            for g in range(2, 8):
                p1_group(g)

            def thin(w_hi, w_lo, cols, name, half):
                at = slice(half * HALF, (half + 1) * HALF)
                for k in range(KD):
                    ins = mm3(bank[4 + half][0:cols, :], w_hi[:, k, :], w_lo[:, k, :],
                              xT_hi[:, k, at], xT_lo[:, k, at], k == 0, k == KD - 1)
                ins.then_inc(S[name], 1)

            def thin_turn(cols, name):
                for tile in range(NT):
                    half, at = tile // 4, tile % 4 * P
                    ins = pe.transpose(bank[6][:, tile * cols:(tile + 1) * cols], xn[half][0:cols, at:at + P],
                                       ident[0:cols, 0:cols])
                ins.then_inc(S[name], 1)

            pe.wait_ge(S["small_split"], 2)
            pe.wait_ge(S["lat_done"], KD)
            for half in range(2):
                thin(dtw_hi, dtw_lo, NH, "dtT_mm", half)
            for g in range(8, 12):
                p1_group(g)
            pe.wait_ge(S["dtT_done"], 2)
            thin_turn(NH, "dt_mm")
            for g in range(12, 20):
                p1_group(g)
            pe.wait_ge(S["p1_done"], 20)
            pe.wait_ge(S["wv_in"], 16)
            def mix_group(g):
                pe.wait_ge(S["wp_summed"], 2 * (g + 1))
                for n in range(KD):
                    ins = pe.matmul(bank[MIX_BANKS[n]][:, :], wv[:, g, n * P:(n + 1) * P], wps[:, g, :],
                                    start=(g == 0), stop=(g == NKV - 1))
                    if g == NKV - 1:
                        ins.then_inc(S["mix_mm"], 1)

            for g in range(NKV - 1):
                if g == NKV // 2:
                    pe.wait_ge(S["a_done"], 1)
                    pe.matmul(bank[6][:, 32:64], after[:, :], decay[:, :, :].rearrange("p c h -> p (c h)"),
                              start=True, stop=True).then_inc(S["end_mm"], 1)
                mix_group(g)
            pe.wait_ge(S["end_exp"], 1)

            def scores(c):
                wait(pe, "st_xb", c + 1)
                wait(pe, "xbt_done", c)
                for i in range(2):
                    ins = pe.transpose(bank[6][:, i * P:(i + 1) * P], stXB[:, i, :], ident[:, :])
                ins.then_inc(S["xbt_mm"], 1)
                wait(pe, "att_done", c)
                pe.matmul(bank[0][:, :].rearrange("p (h n) -> p h n", h=NH), stXB[:, 1, :],
                          xBC[:, 2:6, bass.ds(c * P + TAPS - 1, P)], start=True, stop=True
                          ).then_inc(S["g_mm"], 1)
                wait(pe, "atri_done", c + 1)
                wait(pe, "expd_done", c)
                flat = atri[:, :, :].rearrange("p h n -> p (h n)")
                pe.matmul(bank[1][:, :], after[:, :], flat, start=True, stop=True).then_inc(S["d_mm"], 1)
                wait(pe, "expe_done", c)
                pe.matmul(bank[2][:, :], ones[:, :], flat, start=True, stop=True).then_inc(S["e_mm"], 1)

            def mixed(c, first):
                wait(pe, "att_done", c + 1)
                wait(pe, "y1_done", c)
                pe_ins = pe.matmul(bank[3][:, :], XBt[:, 0, :], att[:, :, :].rearrange("p h n -> p (h n)"),
                                   start=True, stop=first)
                if not first:
                    wait(pe, "cs_done", c + 1)
                    wait(pe, "state_done", c)
                    for h in range(NH):
                        pe_ins = pe.matmul(bank[3][:, h * P:(h + 1) * P], state[:, h, :], Cs[:, h, :],
                                           start=False, stop=(h == NH - 1))
                pe_ins.then_inc(S["y_mm"], 1)
                if isinstance(c, int) and c == NT - 1:
                    return
                wait(pe, "xs_done", c + 1)
                wait(pe, "state_done", c)
                pe.matmul(bank[4][:, :], XBt[:, 1, :], Xs[:, :, :].rearrange("p h n -> p (h n)"),
                          start=True, stop=True).then_inc(S["s_mm"], 1)

            def project(c):
                wait(pe, "ylo_done", c + 1)
                wait(pe, "ht_done", c)
                for k in range(KD):
                    ins = mm3(bank[5][:, :], y_hi[:, k, :], y_lo[:, k, :], wo_hi[:, k, :], wo_lo[:, k, :],
                              k == 0, k == KD - 1)
                ins.then_inc(S["o_mm"], 1)

            def ssd_step(c, u, transposed=True):
                scores(c)
                if transposed:
                    turn(NT + c - 4, u, 7, NT + c - 4)
                project(c - 1)
                mixed(c, False)

            scores(0)
            mix_group(NKV - 1)
            pe.wait_ge(S["mix_done"], 2)
            mixed(0, True)
            scores(1)
            pe.wait_ge(S["mix_done"], KD)
            pe.wait_ge(S["w_lo2"], 1)
            pe.wait_ge(S["w_lo3"], 1)
            project(0)
            mixed(1, False)
            for c in (2, 3):
                ssd_step(c, c % 2, transposed=False)
            with pe.Fori(2, NT // 2 - 1) as p:
                for u in range(2):
                    ssd_step(2 * p + u, u)
            for c in (NT - 2, NT - 1):
                ssd_step(c, c % 2)

            def finish_ssd():
                project(NT - 1)
                turn(2 * NT - 4, 0, 6, 0)
                turn(2 * NT - 3, 1, 7, 2 * NT - 4)

            def group(b, g, par, s, half, between=None):
                wait(pe, "h_done", g - 1)
                at = slice(half * HALF, (half + 1) * HALF)
                for m in range(b.mats):
                    for k in range(KD):
                        ins = mm3(bank[2 * par + m][:, :], up_hi[s][:, m, k, :], up_lo[s][:, m, k, :],
                                  xT_hi[:, k, at], xT_lo[:, k, at], k == 0, k == KD - 1)
                    if m == 0 and b.mats == 2:
                        ins.then_inc(S["gate_mm"], 1)
                        if between is not None:
                            between()
                ins.then_inc(S["up_mm"], 1)

            def pair(b, p, n, pending=None):
                g = b.group0 + 4 * p
                if pending is not None:
                    wait(pe, "xT_lo_done", b.norm0 - NT // 2)
                wait(pe, "w_lo0", b.use0[0] + p + 1)
                ssd = pending is not None and pending.layer == "SSD"
                late = ssd or b.mats == 1
                if ssd:
                    wait(pe, "att_done", NT)
                    wait(pe, "expd_done", NT)
                group(b, g, 0, 0, 0)
                if ssd:
                    finish_ssd()
                    wait(pe, "expe_done", NT)
                    wait(pe, "y1_done", NT)
                if n == 2:
                    wait(pe, "w_lo1", b.use0[1] + p + 1)
                    turns = lambda: turn_pair(pending, NT // 2 - 1)
                    group(b, g + 1, 1, 1, 0, turns if pending is not None and not late else None)
                if b.layer == "E" and pending is not None:
                    wait(pe, "r_done", b.down0)
                    thin(gw_hi, gw_lo, 8, "gateT_mm", 0)
                if pending is not None and late:
                    turn_pair(pending, NT // 2 - 1)
                if pending is not None:
                    wait(pe, "xT_lo_done", b.norm0)
                group(b, g + n, n % 2, 0, 1)
                if n == 2:
                    group(b, g + n + 1, 1, 1, 1)

            def down(b, tile, u):
                wait(pe, "st_hi_done", b.down0 + tile + 1)
                wait(pe, "st_lo_done", b.down0 + tile + 1)
                k0 = KD if b.moe else 0
                if b.moe:
                    wait(pe, "routed_done", tile - 1)
                    for k in range(KD):
                        ins = mm3(bank[6 + u][:, :], st_hi[u][:, k, :], st_lo[u][:, k, :],
                                  mix_hi[:, k, :], mix_lo[:, k, :], k == 0, k == KD - 1)
                    ins.then_inc(S["route_mm"], 1)
                wait(pe, "r_done", b.down0 + tile - 1)
                n = KD if b.attention else b.tiles
                w_hi, w_lo = (mix_hi, mix_lo) if b.attention else (wd_hi, wd_lo)
                for k in range(n):
                    ins = mm3(bank[4 + u][:, :], st_hi[u][:, k0 + k, :], st_lo[u][:, k0 + k, :],
                              w_hi[:, k, :], w_lo[:, k, :], k == 0, k == n - 1)
                ins.then_inc(S["down_mm"], 1)

            for b in blocks:
                if not b.attention:
                    full = sum(k == 2 for k in b.pairs)
                    first = 1 if b.fresh else 0
                    if first:
                        pair(b, 0, b.pairs[0], b.pending)
                    if b.layer == "E" and not b.final:
                        thin(gw_hi, gw_lo, 8, "gateT_mm", 1)
                    if full > first:
                        with pe.Fori(first, full) as p:
                            pair(b, p, 2)
                    if b.pairs[-1] == 1:
                        pair(b, len(b.pairs) - 1, 1)
                    if b.layer == "E" and not b.final:
                        wait(pe, "gateT_done", 2)
                        thin_turn(8, "logits_mm")
                    wait(pe, "w_lo2", b.use0[2] + len(b.pairs))
                else:
                    wait(pe, "mixhl_lo", 1)
                if b.moe:
                    wait(pe, "mixhl_lo", 2)
                    wait(pe, "route_done", 1)
                keep = b.final and not b.moe

                def down_pair(p, previous):
                    for u in range(2):
                        down(b, 2 * p + u, u)
                    if previous is not None:
                        turn_pair(*previous)

                down_pair(0, (b.pending, NT // 2 - 1) if b.attention else None)
                with pe.Fori(1, NT // 2) as p:
                    down_pair(p, (b, p - 1) if keep else None)


def lay_out(a):
    import numpy as np
    f = {k: np.asarray(v) for k, v in a.items()}
    cont = np.ascontiguousarray

    def up(*mats):
        o, i = mats[0].shape
        m = np.stack([w.reshape(o // P, P, i // P, P).transpose(0, 3, 2, 1) for w in mats], axis=2)
        return cont(m.reshape(o // P, P, -1))

    def rows(w):
        return w.reshape(w.shape[0] // P, P, -1)

    def by_partition(w):
        return cont(rows(w).transpose(1, 0, 2))

    def pad_rows(w):
        return np.concatenate([w, np.zeros((-w.shape[0] % P, w.shape[1]), w.dtype)])

    w_in = f["L0_attn_w_in"]
    d_inner, d_xb = D, P
    x_b_c = w_in[d_inner:2 * d_inner + 2 * d_xb]
    feat = np.concatenate([x_b_c, w_in[:d_inner]])
    tiles = feat.reshape(10, P, KD, P).transpose(0, 3, 2, 1)
    out = {
        "x": f["L0_attn_hidden_states"][0],
        "w_in": cont(tiles.reshape(5, 2, P, KD * P).transpose(0, 2, 1, 3).reshape(5, P, 2 * KD * P)),
        "dtw": by_partition(w_in[2 * d_inner + 2 * d_xb:].T),
        "conv_w": cont(f["L0_attn_conv_w"].reshape(NCONV, P, TAPS).transpose(1, 0, 2)),
        "conv_b": cont(f["L0_attn_conv_b"].reshape(NCONV, P).T),
        "heads": np.stack([f["L0_attn_A_log"], f["L0_attn_D"], f["L0_attn_dt_bias"]]),
        "w_out": cont(rows(f["L0_attn_w_out"].T)),
        "gains": np.stack([f["L0_attn_ln1_w"], f["L0_attn_ln2_w"], f["L1_ffn_ln_gamma"], f["L1_ffn_ln_beta"]]),
        "up_M": up(f["L0_attn_gate_w"], f["L0_attn_up_w"]),
        "down_M": cont(rows(f["L0_attn_down_w"].T)),
        "up_F": up(pad_rows(f["L0_ffn_W_gate"]), pad_rows(f["L0_ffn_W_up"])),
        "down_F": cont(rows(pad_rows(f["L0_ffn_W_down"].T))),
        "up_E": up(f["L1_ffn_up_w"].T),
        "down_E": rows(f["L1_ffn_down_w"]),
        "gw": by_partition(f["L1_ffn_gate_w"]),
        "expert": by_partition(f["L1_ffn_expert_w"].T),
        "fc2": by_partition(f["L1_ffn_fc2_w"]),
        "fc1": by_partition(f["L1_ffn_fc1_w"].T),
    }
    qkv = f["L1_attn_weight_qkv"].reshape(NKV, 6, P, D)
    out["wv"] = cont(qkv[:, 5].transpose(1, 0, 2))
    proj = f["L1_attn_weight_proj"].reshape(D, NKV, 2, 2, P)
    out["wp"] = cont(proj.transpose(1, 2, 4, 3, 0).reshape(2 * NKV, P, 2, D))
    return {k: cont(v) for k, v in out.items()}


def kernel(**inputs):
    import concourse.bacc as bacc
    from concourse.bass_utils import run_bass_kernel_spmd

    arrays = lay_out(inputs)
    nc = bacc.Bacc("TRN2", target_bir_lowering=False, num_devices=1)
    t = {k: nc.dram_tensor("in_" + k, v.shape, mybir.dt.from_np(v.dtype), kind="ExternalInput").ap()
         for k, v in arrays.items()}
    t["out"] = nc.dram_tensor("out", (T, D), F32, kind="ExternalOutput").ap()
    build_program(nc, t)
    r = run_bass_kernel_spmd(nc, [{"in_" + k: v for k, v in arrays.items()}], core_ids=[0])
    return r.results[0]["out"].reshape(1, T, D)
```
